# Optimizing a Trainium2 kernel written in Bass

```python
import numpy as np
import jax
import jax.numpy as jnp

def _softmax(x, axis=-1):
    return jax.nn.softmax(x, axis=axis)

def _gelu(x):
    return jax.nn.gelu(x, approximate=True)

def _silu(x):
    return jax.nn.silu(x)

def _sigmoid(x):
    return jax.nn.sigmoid(x)

def _layernorm(x, axis=-1, eps=1e-05):
    m = jnp.mean(x, axis=axis, keepdims=True)
    v = jnp.var(x, axis=axis, keepdims=True)
    return (x - m) / jnp.sqrt(v + eps)

def _scatter_add(tgt, idx, src, axis=0):
    return tgt.at[idx].add(src)

def _segment_sum(src, seg, n):
    return jax.ops.segment_sum(src, seg, n)
kernel_name = 'mk_xattn_ffn_d1_seqx_r2_d8ec2c'

def setup_inputs(seed: int=0):
    np.random.seed(seed)
    _w = jnp.asarray

    def _rec_inputs():
        import jax
        import jax.numpy as jnp
        _rk = jax.random.key(seed)
        x = 7.22e-05 + 1 * jax.random.normal(jax.random.fold_in(_rk, 1), (8, 100, 512), jnp.float32)
        _lenS = 100 - jax.random.randint(jax.random.fold_in(_rk, 7), (8,), 0, max(1, 100 // 4) + 1, jnp.int32)
        _lenS2 = 722 - jax.random.randint(jax.random.fold_in(_rk, 8), (8,), 0, max(1, 722 // 4) + 1, jnp.int32)
        _ctx_1024P = jax.random.normal(jax.random.fold_in(_rk, 11), (8, 16, 512), jnp.float32)
        _ctx_1024c = jax.random.dirichlet(jax.random.fold_in(_rk, 511), 0.3 * jnp.ones((16,), jnp.float32), (8, 722))
        _ctx_1024t = jnp.einsum('bsk,bkd->bsd', _ctx_1024c, _ctx_1024P)
        _ctx_1024t = _ctx_1024t * jax.lax.rsqrt(jnp.mean(jnp.square(_ctx_1024t)) + 1e-12) * 0.953939
        ctx_1024 = 4.13588e-05 + 0.999923 * (_ctx_1024t + 0.3 * jax.random.normal(jax.random.fold_in(_rk, 611), (8, 722, 512), jnp.float32))
        return (x, ctx_1024)
    x, ctx_1024 = _rec_inputs()

    def _L0_xattn_setup():
        import jax, jax.numpy as jnp
        import numpy as np
        D = 512
        DKQ = 512
        DV = 512
        FF = 2048
        B, T, M = (4, 1024, 1024)
        EPS = 1e-05

        def _ln(x, g, b):
            mu = jnp.mean(x, axis=-1, keepdims=True)
            var = jnp.var(x, axis=-1, keepdims=True)
            return (x - mu) * jax.lax.rsqrt(var + EPS) * g + b
        key = jax.random.key(seed)
        ks = jax.random.split(key, 20)
        s = lambda fan: 1.0 / np.sqrt(fan)
        return {'tgt': jax.random.normal(ks[0], (B, T, D), jnp.float32), 'memory': jax.random.normal(ks[1], (B, M, D), jnp.float32), 'in_proj_w': jax.random.normal(ks[2], (3 * D, D), jnp.float32) * s(D), 'in_proj_b': jnp.zeros((3 * D,), jnp.float32), 'out_proj_w': jax.random.normal(ks[3], (D, D), jnp.float32) * s(D), 'out_proj_b': jnp.zeros((D,), jnp.float32), 'wq': jax.random.normal(ks[4], (DKQ, D), jnp.float32) * s(D), 'bq': jnp.zeros((DKQ,), jnp.float32), 'wk': jax.random.normal(ks[5], (DKQ, D), jnp.float32) * s(D), 'bk': jnp.zeros((DKQ,), jnp.float32), 'wv': jax.random.normal(ks[6], (DV, D), jnp.float32) * s(D), 'bv': jnp.zeros((DV,), jnp.float32), 'w1': jax.random.normal(ks[7], (FF, D), jnp.float32) * s(D), 'b1': jnp.zeros((FF,), jnp.float32), 'w2': jax.random.normal(ks[8], (D, FF), jnp.float32) * s(FF), 'b2': jnp.zeros((D,), jnp.float32), 'g1': jnp.ones((D,), jnp.float32), 'be1': jnp.zeros((D,), jnp.float32), 'g2': jnp.ones((D,), jnp.float32), 'be2': jnp.zeros((D,), jnp.float32), 'g3': jnp.ones((D,), jnp.float32), 'be3': jnp.zeros((D,), jnp.float32)}
    _L0_xattn_all = _L0_xattn_setup()
    _L0_xattn_in = {k: v for k, v in _L0_xattn_all.items() if k in ('in_proj_w', 'in_proj_b', 'out_proj_w', 'out_proj_b', 'wq', 'bq', 'wk', 'bk', 'wv', 'bv', 'w1', 'b1', 'w2', 'b2', 'g1', 'be1', 'g2', 'be2', 'g3', 'be3')}
    del _L0_xattn_all

    def _L0_ffn_setup():
        import jax, jax.numpy as jnp
        import numpy as np
        B, T, D = (1, 1024, 512)
        E, DFF = (8, 2048)

        def _gating(logits):
            S, num_e = logits.shape
            gates = jax.nn.softmax(logits.astype(jnp.float32), axis=1)
            idx1 = jnp.argmax(gates, axis=1)
            mask1 = jax.nn.one_hot(idx1, num_e, dtype=jnp.int32)
            logits_ex1 = jnp.where(mask1.astype(bool), -jnp.inf, logits)
            idx2 = jnp.argmax(logits_ex1, axis=1)
            mask2 = jax.nn.one_hot(idx2, num_e, dtype=jnp.int32)
            loc1 = jnp.cumsum(mask1, axis=0) - 1
            loc2 = jnp.cumsum(mask2, axis=0) - 1 + jnp.sum(mask1, axis=0, keepdims=True)
            loc1_s = jnp.sum(loc1 * mask1, axis=1)
            loc2_s = jnp.sum(loc2 * mask2, axis=1)
            g1 = jnp.sum(gates * mask1, axis=1)
            g2 = jnp.sum(gates * mask2, axis=1)
            denom = jnp.maximum(g1 + g2, jnp.finfo(jnp.float32).eps)
            g1, g2 = (g1 / denom, g2 / denom)
            cap = S
            loc1_sc = jax.nn.one_hot(loc1_s, cap, dtype=jnp.float32)
            loc2_sc = jax.nn.one_hot(loc2_s, cap, dtype=jnp.float32)
            combine = (g1[:, None] * mask1)[:, :, None] * loc1_sc[:, None, :] + (g2[:, None] * mask2)[:, :, None] * loc2_sc[:, None, :]
            dispatch_mask = combine != 0
            return (combine.astype(logits.dtype), dispatch_mask)
        key = jax.random.key(seed)
        k1, k2, k3, k4 = jax.random.split(key, 4)
        x = jax.random.normal(k1, (B, T, D), dtype=jnp.float32)
        Wg = jax.random.normal(k2, (D, E), dtype=jnp.float32) * (1.0 / np.sqrt(D))
        w1 = jax.random.normal(k3, (D, DFF), dtype=jnp.float32) * (1.0 / np.sqrt(D))
        w2 = jax.random.normal(k4, (DFF, D), dtype=jnp.float32) * (1.0 / np.sqrt(DFF))
        return {'x': x, 'Wg': Wg, 'w1': w1, 'w2': w2}
    _L0_ffn_all = _L0_ffn_setup()
    _L0_ffn_in = {k: v for k, v in _L0_ffn_all.items() if k in ('Wg', 'w1', 'w2')}
    del _L0_ffn_all
    return {'x': x, 'ctx_1024': ctx_1024, 'L0_xattn_in_proj_w': _L0_xattn_in['in_proj_w'], 'L0_xattn_in_proj_b': _L0_xattn_in['in_proj_b'], 'L0_xattn_out_proj_w': _L0_xattn_in['out_proj_w'], 'L0_xattn_out_proj_b': _L0_xattn_in['out_proj_b'], 'L0_xattn_wq': _L0_xattn_in['wq'], 'L0_xattn_bq': _L0_xattn_in['bq'], 'L0_xattn_wk': _L0_xattn_in['wk'], 'L0_xattn_bk': _L0_xattn_in['bk'], 'L0_xattn_wv': _L0_xattn_in['wv'], 'L0_xattn_bv': _L0_xattn_in['bv'], 'L0_xattn_w1': _L0_xattn_in['w1'], 'L0_xattn_b1': _L0_xattn_in['b1'], 'L0_xattn_w2': _L0_xattn_in['w2'], 'L0_xattn_b2': _L0_xattn_in['b2'], 'L0_xattn_g1': _L0_xattn_in['g1'], 'L0_xattn_be1': _L0_xattn_in['be1'], 'L0_xattn_g2': _L0_xattn_in['g2'], 'L0_xattn_be2': _L0_xattn_in['be2'], 'L0_xattn_g3': _L0_xattn_in['g3'], 'L0_xattn_be3': _L0_xattn_in['be3'], 'L0_ffn_Wg': _L0_ffn_in['Wg'], 'L0_ffn_w1': _L0_ffn_in['w1'], 'L0_ffn_w2': _L0_ffn_in['w2']}

def reference(x, ctx_1024, L0_xattn_in_proj_w, L0_xattn_in_proj_b, L0_xattn_out_proj_w, L0_xattn_out_proj_b, L0_xattn_wq, L0_xattn_bq, L0_xattn_wk, L0_xattn_bk, L0_xattn_wv, L0_xattn_bv, L0_xattn_w1, L0_xattn_b1, L0_xattn_w2, L0_xattn_b2, L0_xattn_g1, L0_xattn_be1, L0_xattn_g2, L0_xattn_be2, L0_xattn_g3, L0_xattn_be3, L0_ffn_Wg, L0_ffn_w1, L0_ffn_w2):
    import jax
    import jax.numpy as jnp

    def _L0_xattn_ref(tgt, memory, in_proj_w, in_proj_b, out_proj_w, out_proj_b, wq, bq, wk, bk, wv, bv, w1, b1, w2, b2, g1, be1, g2, be2, g3, be3):
        import jax, jax.numpy as jnp
        import numpy as np
        D = 512
        DKQ = 512
        DV = 512
        FF = 2048
        B, T, M = (4, 1024, 1024)
        EPS = 1e-05

        def _ln(x, g, b):
            mu = jnp.mean(x, axis=-1, keepdims=True)
            var = jnp.var(x, axis=-1, keepdims=True)
            return (x - mu) * jax.lax.rsqrt(var + EPS) * g + b
        q = tgt @ in_proj_w[:D].T + in_proj_b[:D]
        k = tgt @ in_proj_w[D:2 * D].T + in_proj_b[D:2 * D]
        v = tgt @ in_proj_w[2 * D:].T + in_proj_b[2 * D:]
        scores = jnp.einsum('btd,bsd->bts', q, k) / jnp.sqrt(jnp.float32(D))
        attn = jax.nn.softmax(scores, axis=-1)
        sa = jnp.einsum('bts,bsd->btd', attn, v) @ out_proj_w.T + out_proj_b
        x = _ln(tgt + sa, g1, be1)
        q1 = x @ wq.T + bq
        k2 = memory @ wk.T + bk
        v2 = memory @ wv.T + bv
        cscores = jnp.einsum('btd,bmd->btm', q1, k2) / jnp.sqrt(jnp.float32(DKQ))
        ca = jnp.einsum('btm,bmd->btd', jax.nn.softmax(cscores, axis=-1), v2)
        x = _ln(x + ca, g2, be2)
        ff = jax.nn.relu(x @ w1.T + b1) @ w2.T + b2
        return _ln(x + ff, g3, be3)

    def _L0_ffn_ref(x, Wg, w1, w2):
        import jax, jax.numpy as jnp
        import numpy as np
        B, T, D = (1, 1024, 512)
        E, DFF = (8, 2048)

        def _gating(logits):
            S, num_e = logits.shape
            gates = jax.nn.softmax(logits.astype(jnp.float32), axis=1)
            idx1 = jnp.argmax(gates, axis=1)
            mask1 = jax.nn.one_hot(idx1, num_e, dtype=jnp.int32)
            logits_ex1 = jnp.where(mask1.astype(bool), -jnp.inf, logits)
            idx2 = jnp.argmax(logits_ex1, axis=1)
            mask2 = jax.nn.one_hot(idx2, num_e, dtype=jnp.int32)
            loc1 = jnp.cumsum(mask1, axis=0) - 1
            loc2 = jnp.cumsum(mask2, axis=0) - 1 + jnp.sum(mask1, axis=0, keepdims=True)
            loc1_s = jnp.sum(loc1 * mask1, axis=1)
            loc2_s = jnp.sum(loc2 * mask2, axis=1)
            g1 = jnp.sum(gates * mask1, axis=1)
            g2 = jnp.sum(gates * mask2, axis=1)
            denom = jnp.maximum(g1 + g2, jnp.finfo(jnp.float32).eps)
            g1, g2 = (g1 / denom, g2 / denom)
            cap = S
            loc1_sc = jax.nn.one_hot(loc1_s, cap, dtype=jnp.float32)
            loc2_sc = jax.nn.one_hot(loc2_s, cap, dtype=jnp.float32)
            combine = (g1[:, None] * mask1)[:, :, None] * loc1_sc[:, None, :] + (g2[:, None] * mask2)[:, :, None] * loc2_sc[:, None, :]
            dispatch_mask = combine != 0
            return (combine.astype(logits.dtype), dispatch_mask)
        d_model = x.shape[2]
        xs = x.reshape(-1, d_model)
        logits = xs @ Wg
        combine, dispatch_mask = _gating(logits)
        dispatched = jnp.einsum('sec,sm->ecm', dispatch_mask.astype(jnp.float32), xs)
        expert_out = jax.nn.relu(dispatched @ w1) @ w2
        out = jnp.einsum('sec,ecm->sm', combine, expert_out)
        return out.reshape(x.shape)
    x = x + _L0_xattn_ref(_layernorm(x, axis=-1), ctx_1024, L0_xattn_in_proj_w, L0_xattn_in_proj_b, L0_xattn_out_proj_w, L0_xattn_out_proj_b, L0_xattn_wq, L0_xattn_bq, L0_xattn_wk, L0_xattn_bk, L0_xattn_wv, L0_xattn_bv, L0_xattn_w1, L0_xattn_b1, L0_xattn_w2, L0_xattn_b2, L0_xattn_g1, L0_xattn_be1, L0_xattn_g2, L0_xattn_be2, L0_xattn_g3, L0_xattn_be3)
    x = x + _L0_ffn_ref(_layernorm(x, axis=-1), L0_ffn_Wg, L0_ffn_w1, L0_ffn_w2)
    return x

_drawn_inputs = setup_inputs


def setup_inputs(seed=0):
    import zlib

    import numpy as np

    out = dict(_drawn_inputs(seed))
    spreads = {'L0_xattn_in_proj_b': (0.0, 0.1),
     'L0_xattn_out_proj_b': (0.0, 0.1),
     'L0_xattn_bq': (0.0, 0.8),
     'L0_xattn_bk': (0.0, 0.8),
     'L0_xattn_bv': (0.0, 0.1),
     'L0_xattn_b1': (0.0, 0.269),
     'L0_xattn_b2': (0.0, 0.1),
     'L0_xattn_g1': (1.0, 0.2),
     'L0_xattn_be1': (0.0, 0.1),
     'L0_xattn_g2': (1.0, 0.2),
     'L0_xattn_be2': (0.0, 0.1),
     'L0_xattn_g3': (1.0, 0.2),
     'L0_xattn_be3': (0.0, 0.1)}
    factors = {'L0_ffn_Wg': 8.0}
    for name, (base, spread) in spreads.items():
        noise = np.random.default_rng([zlib.crc32(name.encode()), seed]).standard_normal(out[name].shape)
        drawn = base * np.exp(spread * noise) if base else spread * noise
        out[name] = jnp.asarray(drawn.astype(out[name].dtype))
    for name, factor in factors.items():
        out[name] = (out[name] * factor).astype(out[name].dtype)
    return out
```

```python
from contextlib import ExitStack

import concourse.bass as bass
from concourse import mybir

F32 = mybir.dt.float32
F32R = mybir.dt.float32r
ALU = mybir.AluOpType
ACT = mybir.ActivationFunctionType
AX = mybir.AxisListType

P = 128
B, T, D = 8, 100, 512
M = 722
FF = 2048
NE = 8
N = B * T
HALF = N // 2
HB = B // 2
KC = D // P
MC = (M + P - 1) // P
MH = M // 2
MW = MH + 1
ML = M - (MC - 1) * P
NF = FF // D
EPS = 1e-5
F32_EPS = 1.1920928955078125e-07
SCALE = 1.0 / float(D) ** 0.5

U_Q, U_K, U_V, U_O, U_CQ, U_CK, U_CV = range(7)
U_F = 7
U_M = U_F + 2 * NF
NU = U_M + 2 * NF
KINDS = (["fp32", "fp32", "split", "residual", "split", "split_nobias", "residual"]
         + ["relu_bias", "down_residual"] + ["relu_bias", "down_add"] * (NF - 1)
         + ["relu", "down_first"] + ["relu", "down_add"] * (NF - 1))
GROUPS = 2 * KC

C_BQ, C_BK, C_BV, C_BO, C_CBQ, C_CBK, C_CBV, C_B1 = 0, 4, 8, 12, 16, 20, 24, 28
C_B2, C_G1, C_E1, C_G2, C_E2, C_WG = 44, 48, 52, 56, 60, 64
C_ALL = C_WG + KC * NE


def act_writes(n):
    return KINDS[n] in ("fp32", "split", "split_nobias", "relu_bias", "relu")


def dve_writes(n):
    return KINDS[n] != "fp32"


def act_count(n, h, e):
    return GROUPS * sum(act_writes(i) for i in range(n)) + KC * h + e + 1


def dve_count(n, h, e):
    return GROUPS * sum(dve_writes(i) for i in range(n)) + KC * h + e + 1


def frees_on_act(n):
    return KINDS[n] in ("fp32", "relu_bias")


def build(nc, x, ctxt, ctxn, wts, consts, g3, be3, out):
    with ExitStack() as ctx:
        def sem(name):
            return ctx.enter_context(nc.semaphore(name))

        base = 16512
        at = {}
        for name, size in (("X", 2 * KC * N * 4), ("R1", 2 * KC * N * 4), ("R2", 29312), ("R3", B * D * 4),
                           ("R4", 2 * KC * 724 * 4), ("R5", 2 * MC * D * 4), ("R6", KC * M * 4 + MC * D * 4),
                           ("W", 5 * KC * D * 4), ("C", 3360)):
            at[name] = base
            base += (size + 31) // 32 * 32

        def sb(name, region, offset, shape, dt=F32):
            return nc.alloc_sbuf_tensor_at(name, shape, dt, offset=at[region] + offset)

        XB = KC * N * 4
        XH = sb("XH", "X", 0, [P, KC, N], F32R)
        XL = sb("XL", "X", XB, [P, KC, N], F32R)
        qT = sb("qT", "R1", 0, [P, KC, N])
        kT = sb("kT", "R1", XB, [P, KC, N])
        AH = sb("AH", "R1", 0, [P, KC, N], F32R)
        AL = sb("AL", "R1", XB, [P, KC, N], F32R)
        QH = sb("QH", "R2", 0, [P, KC, N], F32R)
        QL = sb("QL", "R2", XB, [P, KC, N], F32R)
        acc = sb("acc", "R2", 0, [P, KC, N])
        tok = sb("tok", "R3", 0, [T, B, D])
        CTS = 2 * KC * 724 * 4
        ctH = [sb("ctH0", "R4", 0, [P, KC, 724], F32R), sb("ctH1", "R2", 0, [P, KC, 724], F32R)]
        ctL = [sb("ctL0", "R4", CTS // 2, [P, KC, 724], F32R), sb("ctL1", "R2", CTS // 2, [P, KC, 724], F32R)]
        prob = sb("prob", "R2", CTS, [T, 2, MC * P])
        cnH = sb("cnH", "R5", 0, [P, MC, D], F32R)
        cnL = sb("cnL", "R5", MC * D * 4, [P, MC, D], F32R)
        ptH = sb("ptH", "R3", 0, [P, MC * T], F32R)
        ptL = sb("ptL", "R3", 2400, [P, MC * T], F32R)
        utok = sb("utok", "R3", 4800, [T, 2, D])
        crow = sb("crow", "R3", 8896, [2, N])
        r1 = sb("r1", "R5", 0, [P, KC, N])
        sprob = sb("sprob", "R5", 12800, [T, HB, T])
        sprobT = sb("sprobT", "R5", 16000, [T, HB, T])
        lnt = sb("lnt", "R5", 19200, [P, 2, HALF])
        tok2 = sb("tok2", "R4", 0, [T, B, D])
        g3b = sb("g3b", "R5", 0, [P, D])
        be3b = sb("be3b", "R5", 2048, [P, D])
        glog = sb("glog", "R5", 4096, [2 * NE, N])
        outb = sb("outb", "R5", 8192, [T, 4, D])
        relt = sb("relt", "R6", 0, [P, 3, HALF])
        ctR = sb("ctR", "R6", 0, [P, KC, M])
        cnR = sb("cnR", "R6", KC * M * 4, [P, MC, D])
        WH = [sb("WH%d" % i, "W", i * 16384, [P, KC, D], F32R) for i in range(2)]
        WL = [sb("WL%d" % i, "W", i * 16384 + 8192, [P, KC, D], F32R) for i in range(2)]
        WR = sb("WR", "W", 32768, [P, KC, D])
        off = [0]

        def small(name, shape, dt=F32):
            size = 4
            for s in shape[1:]:
                size *= s
            t = sb(name, "C", off[0], shape, dt)
            off[0] += (size + 31) // 32 * 32
            return t

        ident = small("ident", [P, P])
        cst = small("cst", [P, C_ALL])
        bkS = small("bkS", [P, KC, 2], F32R)
        wgS = small("wgS", [P, KC, 2 * NE], F32R)
        ones2 = small("ones2", [2, 1])
        fold = small("fold", [2 * NE, NE])
        bnst = small("bnst", [T, B, 6])
        mv = small("mv", [T, B, 2])
        veps = small("veps", [T, HB])
        rstd = small("rstd", [T, B])
        nhalf = small("nhalf", [T, HB])
        smx = small("smx", [T, B])
        snb = small("snb", [T, B])
        ssum = small("ssum", [T, B])
        srec = small("srec", [T, B])
        cshift = small("cshift", [T, B])
        gl = small("gl", [T, B, NE])
        gtop = small("gtop", [T, B, NE])
        gexp = small("gexp", [T, B, NE])
        gsm = small("gsm", [T, 8, B])
        assert off[0] <= 3360, off[0]

        ps = ctx.enter_context(nc.psum_tensor("ps", [P, 8, 512], F32))

        x_loaded = [sem("x_loaded0"), sem("x_loaded1")]
        consts_loaded = sem("consts_loaded")
        weights_loaded = sem("weights_loaded")
        ct_loaded = [sem("ct_loaded0"), sem("ct_loaded1")]
        cn_loaded = [sem("cn_loaded0"), sem("cn_loaded1"), sem("cn_loaded2")]
        xres_loaded = sem("xres_loaded")
        gb_loaded = sem("gb_loaded")
        stored = sem("stored")
        pool_init = sem("pool_init")
        pads_set = sem("pads_set")
        pool_step = sem("pool_step")
        rstd_ready = sem("rstd_ready")
        xres_ready = sem("xres_ready")
        w_high = sem("w_high")
        w_low = sem("w_low")
        ct_high, ct_low = sem("ct_high"), sem("ct_low")
        cn_high, cn_low = sem("cn_high"), sem("cn_low")
        small_high, small_low = sem("small_high"), sem("small_low")
        gemm_done = sem("gemm_done")
        act_evac, dve_evac = sem("act_evac"), sem("dve_evac")
        dve_step = sem("dve_step")
        stats_ready = sem("stats_ready")
        tok_ready = sem("tok_ready")
        to_tok = sem("to_tok")
        to_feat = sem("to_feat")
        x_high, x_ready = sem("x_high"), sem("x_ready")
        s_scores, s_max, s_exp, s_norm = sem("s_scores"), sem("s_max"), sem("s_exp"), sem("s_norm")
        s_probT, s_probT_sb = sem("s_probT"), sem("s_probT_sb")
        s_att, s_att_high, s_att_low = sem("s_att"), sem("s_att_high"), sem("s_att_low")
        c_row, c_row_sb, c_col, c_col_sb = sem("c_row"), sem("c_row_sb"), sem("c_col"), sem("c_col_sb")
        c_scores, c_max, c_exp, c_rec = sem("c_scores"), sem("c_max"), sem("c_exp"), sem("c_rec")
        c_probT, c_probT_high, c_probT_low = sem("c_probT"), sem("c_probT_high"), sem("c_probT_low")
        c_chunk = sem("c_chunk")
        c_att_sb = sem("c_att_sb")
        c_attT, c_attT_high, c_attT_low = sem("c_attT"), sem("c_attT_high"), sem("c_attT_low")
        g_rows, g_rows_sb, g_cols, g_shift = sem("g_rows"), sem("g_rows_sb"), sem("g_cols"), sem("g_shift")
        g_exp, g_weight = sem("g_exp"), sem("g_weight")
        out_ready = sem("out_ready")

        def half(t, h, k):
            return t[:, k, h * HALF:(h + 1) * HALF]

        def raw(ap):
            return ap.bitcast(F32)

        operand = {}
        for n in range(NU):
            operand[n] = (XH, XL)
        operand[U_V] = operand[U_CK] = (QH, QL)
        operand[U_O] = operand[U_CV] = (AH, AL)
        for j in range(NF):
            operand[U_F + 2 * j + 1] = operand[U_M + 2 * j + 1] = (AH, AL)

        def wait_operand(eng, n, h, k):
            if n in (U_Q, U_K):
                eng.wait_ge(x_ready, KC * h + k + 1)
            elif n == U_V:
                eng.wait_ge(s_att_low, KC * h + k + 1)
            elif n in (U_O, U_CK):
                eng.wait_ge(dve_evac, dve_count(n - 1, h, k))
            elif n == U_CQ:
                eng.wait_ge(x_ready, 8 + KC * h + k + 1)
            elif n == U_CV:
                eng.wait_ge(c_attT_low, HB * (h + 1))
            elif n >= U_F and (n - U_F) % 2:
                eng.wait_ge(dve_evac, dve_count(n - 1, h, k))
            elif n < U_M:
                eng.wait_ge(x_ready, 16 + KC * h + k + 1)
            else:
                eng.wait_ge(x_ready, 24 + KC * h + k + 1)

        block = ctx.enter_context(nc.Block())

        @block.sync
        def _(sp):
            sp.dma_start(tok[:, 0:HB, :], x[0:HB].rearrange("b t d -> t b d")).then_inc(x_loaded[0], 16)
            sp.dma_start(cst[:, :], consts).then_inc(consts_loaded, 16)
            sp.dma_start(WR[:, :, :], wts[0]).then_inc(weights_loaded, 16)
            sp.dma_start(tok[:, HB:B, :], x[HB:B].rearrange("b t d -> t b d")).then_inc(x_loaded[1], 16)

            def load_weights(n):
                sp.wait_ge(w_low, KC * n)
                sp.dma_start(WR[:, :, :], wts[n]).then_inc(weights_loaded, 16)

            def load_ct(b):
                for i in range(2):
                    if b >= 1:
                        sp.wait_ge(ct_low, 2 * (b - 1) + i + 1)
                    sp.dma_start(ctR[:, 2 * i:2 * i + 2, :],
                                 ctxt[b, 2 * P * i:2 * P * (i + 1), :].rearrange("(k p) m -> p k m", p=P)
                                 ).then_inc(ct_loaded[i], 16)

            def load_cn(b):
                for i in range(3):
                    if b >= 1:
                        sp.wait_ge(cn_low, 3 * (b - 1) + i + 1)
                    if b == 0 and i == 2:
                        sp.wait_ge(pads_set, 1)
                    full = 2 if i < 2 else 1
                    sp.dma_start(cnR[:, 2 * i:2 * i + full, :],
                                 ctxn[b, 2 * P * i:2 * P * i + full * P, :].rearrange("(c p) d -> p c d", p=P)
                                 ).then_inc(cn_loaded[i], 16)
                    if i == 2:
                        sp.dma_start(cnR[0:ML, MC - 1, :], ctxn[b, (MC - 1) * P:M, :]).then_inc(cn_loaded[i], 16)

            load_weights(1)
            load_ct(0)
            load_cn(0)
            for n in range(2, U_CV + 1):
                load_weights(n)
            load_ct(1)
            load_weights(U_F)
            load_cn(1)
            load_ct(2)
            for b in range(B):
                if b + 3 < B:
                    load_ct(b + 3)
                if b + 2 < B:
                    load_cn(b + 2)
            sp.wait_ge(c_attT, B)
            sp.dma_start(tok[:, :, :], x.rearrange("b t d -> t b d")).then_inc(xres_loaded, 16)
            sp.dma_start(g3b[:, :], g3.partition_broadcast(P)).then_inc(gb_loaded, 16)
            sp.dma_start(be3b[:, :], be3.partition_broadcast(P)).then_inc(gb_loaded, 16)
            for n in range(U_F + 1, NU):
                load_weights(n)
            for b in range(B):
                sp.wait_ge(out_ready, b + 1)
                sp.dma_start(out[b], outb[:, b % 4, :]).then_inc(stored, 16)
            sp.wait_ge(stored, 16 * B)

        @block.gpsimd
        def _(pool):
            pool.memset(ident[:, :], 0.0).then_inc(pool_step, 1)
            pool.wait_ge(pool_step, 1)
            pool.affine_select(out=ident[:, :], in_=ident[:, :], compare_op=ALU.not_equal, fill=1.0, base=0,
                               pattern=[[-1, P]], channel_multiplier=1).then_inc(pool_step, 1)
            pool.memset(nhalf[:, :], -0.5)
            pool.memset(ones2[:, :], 1.0)
            pool.wait_ge(pool_step, 2)
            pool.tensor_tensor(fold[:, :], ident[0:2 * NE, 0:NE], ident[0:2 * NE, NE:2 * NE],
                               ALU.add).then_inc(pool_init, 1)
            pool.memset(cnR[:, MC - 1, :], 0.0).then_inc(pads_set, 1)
            for t in (ctH[0], ctL[0]):
                pool.memset(t[:, :, M:724].bitcast(F32), 0.0).then_inc(pads_set, 1)

            def inverse_deviation(i, h):
                pool.wait_ge(stats_ready, i + 1)
                if i >= 1:
                    pool.wait_ge(rstd_ready, i)
                pool.tensor_scalar(veps[:, :], mv[:, HB * h:HB * (h + 1), 1], EPS, None,
                                   ALU.add).then_inc(pool_step, 1)
                pool.wait_ge(pool_step, i + 3)
                pool.tensor_tensor(rstd[:, HB * h:HB * (h + 1)], veps[:, :], nhalf[:, :],
                                   ALU.pow).then_inc(rstd_ready, 1)

            for i in range(4):
                inverse_deviation(i, i % 2)
            pool.wait_ge(gemm_done, GROUPS * (U_CK + 1))
            for t in (ctH[1], ctL[1]):
                pool.memset(t[:, :, M:724].bitcast(F32), 0.0).then_inc(pads_set, 1)
            pool.memset(prob[:, :, M:MC * P], 0.0).then_inc(pads_set, 1)
            for i in range(4, 6):
                inverse_deviation(i, i % 2)
            pool.wait_ge(xres_loaded, 16)
            pool.wait_ge(gb_loaded, 32)
            for b in range(B):
                pool.tensor_tensor(tok[:, b, :], tok[:, b, :], be3b[0:T, :], ALU.add).then_inc(xres_ready, 1)
            for i in range(6, 10):
                inverse_deviation(i, (i - 6) // 2)

        @block.tensor
        def _(pe):
            def products(dst, n, h, e):
                slot = n % 2
                mh, ml = operand[n]
                for k in range(KC):
                    if e == 0:
                        wait_operand(pe, n, h, k)
                        if h == 0:
                            pe.wait_ge(w_low, KC * n + k + 1)
                    wh = WH[slot][:, k, e * P:(e + 1) * P]
                    wl = WL[slot][:, k, e * P:(e + 1) * P]
                    pe.matmul(dst, wh, half(mh, h, k), start=(k == 0), stop=False)
                    pe.matmul(dst, wh, half(ml, h, k), start=False, stop=False)
                    mm = pe.matmul(dst, wl, half(mh, h, k), start=False, stop=(k == KC - 1))
                return mm

            def unit(n, h, groups=range(KC)):
                for e in groups:
                    pn, ph = (n, 0) if h else (n - 1, 1)
                    if n == U_V:
                        pe.wait_ge(s_att_low, KC * h + e + 1)
                    elif n == U_CV and h == 0:
                        pe.wait_ge(c_attT_low, B if e == 3 else B - 1)
                        pe.wait_ge(c_att_sb, B)
                    elif pn >= 0:
                        if frees_on_act(pn):
                            pe.wait_ge(act_evac, act_count(pn, ph, e))
                        else:
                            pe.wait_ge(dve_evac, dve_count(pn, ph, e))
                    products(ps[:, e, 0:HALF], n, h, e).then_inc(gemm_done, 1)

            def to_features(i, h, src):
                for k in range(KC):
                    if k == 0:
                        pe.wait_ge(tok_ready, 8 * i + HB * (h + 1))
                        if i == 0 and h == 1:
                            pe.wait_ge(x_ready, KC)
                    for j in range(HB):
                        mm = pe.transpose(ps[:, 4 + k, j * T:(j + 1) * T],
                                          src[:, HB * h + j, k * P:(k + 1) * P], ident[0:T, 0:T])
                    mm.then_inc(to_feat, 1)

            def to_tokens(i, h, n, src):
                pe.wait_ge(dve_evac, dve_count(n, h, KC - 1))
                for j in range(HB):
                    if i == 4 and h == 1:
                        pe.wait_ge(out_ready, j + 1)
                    elif h == 1:
                        pe.wait_ge(x_ready, 8 * i + j + 1)
                    else:
                        pe.wait_ge(x_ready, 8 * min(i, 4))
                    t0 = (HB * h + j) * T
                    for k in range(KC):
                        mm = pe.transpose(ps[0:T, 4 + j, k * P:(k + 1) * P], src[:, k, t0:t0 + T], ident[:, :])
                    mm.then_inc(to_tok, 1)

            def self_scores(h):
                pe.wait_ge(act_evac, act_count(U_K, h, KC - 1))
                pe.wait_ge(x_ready, KC * h + KC)
                for j in range(HB):
                    t0 = (HB * h + j) * T
                    for k in range(KC):
                        mm = pe.matmul(ps[0:T, 4 + h, j * T:(j + 1) * T], qT[:, k, t0:t0 + T], kT[:, k, t0:t0 + T],
                                       start=(k == 0), stop=(k == KC - 1))
                mm.then_inc(s_scores, 1)

            def self_prob_transpose(h):
                pe.wait_ge(s_norm, h + 1)
                for j in range(HB):
                    mm = pe.transpose(ps[0:T, 6 + h, j * T:(j + 1) * T], sprob[:, j, :], ident[0:T, 0:T])
                mm.then_inc(s_probT, 1)

            def self_attend(h):
                pe.wait_ge(s_probT_sb, h + 1)
                for k in range(KC):
                    if h == 0:
                        pe.wait_ge(act_evac, act_count(U_K, 1, k))
                    else:
                        pe.wait_ge(dve_evac, dve_count(U_V, 0, k))
                    for j in range(HB):
                        mm = pe.matmul(ps[:, k, j * T:(j + 1) * T], tok[:, HB * h + j, k * P:(k + 1) * P],
                                       sprobT[:, j, :], start=True, stop=True)
                    mm.then_inc(s_att, 1)

            def key_bias_rows(h):
                pe.wait_ge(dve_evac, dve_count(U_CQ, h, KC - 1))
                pe.wait_ge(small_low, 1)
                pe.wait_ge(x_ready, 16)
                for k in range(KC):
                    pe.matmul(ps[0:2, 4 + h, 0:HALF], bkS[:, k, :], half(QH, h, k), start=(k == 0), stop=False)
                    mm = pe.matmul(ps[0:2, 4 + h, 0:HALF], bkS[:, k, :], half(QL, h, k), start=False,
                                   stop=(k == KC - 1))
                mm.then_inc(c_row, 1)

            def key_bias_columns():
                pe.wait_ge(c_row_sb, 2)
                for b in range(B):
                    mm = pe.matmul(ps[0:T, 6, b:b + 1], crow[:, b * T:(b + 1) * T], ones2[:, :],
                                   start=True, stop=True)
                mm.then_inc(c_col, 1)

            def cross_scores(b):
                slot, bank = b % 2, 4 + 2 * (b % 2)
                if b == 1:
                    pe.wait_ge(c_col_sb, 1)
                if b >= 2:
                    pe.wait_ge(c_exp, b - 1)
                pe.wait_ge(pads_set, 3 if b == 0 else 6)
                for k in range(KC):
                    pe.wait_ge(ct_low, 2 * b + k // 2 + 1)
                    qh, ql = AH[:, k, b * T:(b + 1) * T], AL[:, k, b * T:(b + 1) * T]
                    for i in range(2):
                        ch = ctH[slot][:, k, i * MH:i * MH + MW]
                        cl = ctL[slot][:, k, i * MH:i * MH + MW]
                        dst = ps[0:T, bank + i, 0:MW]
                        pe.matmul(dst, qh, ch, start=(k == 0), stop=False)
                        pe.matmul(dst, qh, cl, start=False, stop=False)
                        mm = pe.matmul(dst, ql, ch, start=False, stop=(k == KC - 1))
                mm.then_inc(c_scores, 1)

            def cross_prob_transpose(b):
                pe.wait_ge(c_exp, b + 1)
                if b >= 1:
                    pe.wait_ge(c_probT_low, b)
                for c in range(MC):
                    mm = pe.transpose(ps[:, c // 3, (c % 3) * T:(c % 3 + 1) * T],
                                      prob[:, b % 2, c * P:(c + 1) * P], ident[0:T, 0:T])
                mm.then_inc(c_probT, 1)

            def cross_attend(b):
                pe.wait_ge(c_probT_low, b + 1)
                if b >= 1:
                    pe.wait_ge(c_att_sb, b)
                for c in range(MC):
                    pe.wait_ge(cn_low, 3 * b + c // 2 + 1)
                    ph, pl = ptH[:, c * T:(c + 1) * T], ptL[:, c * T:(c + 1) * T]
                    pe.matmul(ps[0:T, 2, :], ph, cnH[:, c, :], start=(c == 0), stop=False)
                    pe.matmul(ps[0:T, 2, :], ph, cnL[:, c, :], start=False, stop=False)
                    pe.matmul(ps[0:T, 2, :], pl, cnH[:, c, :], start=False,
                              stop=(c == MC - 1)).then_inc(c_chunk, 1)

            def cross_attend_transpose(b):
                pe.wait_ge(c_att_sb, b + 1)
                if b >= 1:
                    pe.wait_ge(c_attT_low, b)
                for k in range(KC):
                    mm = pe.transpose(ps[:, 3, k * T:(k + 1) * T], utok[:, b % 2, k * P:(k + 1) * P],
                                      ident[0:T, 0:T])
                mm.then_inc(c_attT, 1)

            def gate_rows(h):
                pe.wait_ge(x_ready, 32)
                for k in range(KC):
                    pe.matmul(ps[0:2 * NE, 4 + h, 0:HALF], wgS[:, k, :], half(XH, h, k), start=(k == 0), stop=False)
                    mm = pe.matmul(ps[0:2 * NE, 4 + h, 0:HALF], wgS[:, k, :], half(XL, h, k), start=False,
                                   stop=(k == KC - 1))
                mm.then_inc(g_rows, 1)

            def gate_columns():
                pe.wait_ge(g_rows_sb, 2)
                for b in range(B):
                    mm = pe.matmul(ps[0:T, 6, b * NE:(b + 1) * NE], glog[:, b * T:(b + 1) * T], fold[:, :],
                                   start=True, stop=True)
                mm.then_inc(g_cols, 1)

            def norm_between(i, n, src, tiles):
                unit(n, 1, [0])
                to_tokens(i, 0, n, src)
                unit(n, 1, [1, 2])
                to_features(i, 0, tiles)
                unit(n, 1, [3])
                unit(n + 1, 0, [0])
                to_tokens(i, 1, n, src)
                unit(n + 1, 0, [1, 2])
                to_features(i, 1, tiles)
                unit(n + 1, 0, [3])

            pe.wait_ge(pool_init, 1)
            to_features(0, 0, tok)
            unit(U_Q, 0)
            to_features(0, 1, tok)
            unit(U_Q, 1)
            unit(U_K, 0)
            unit(U_K, 1, [0])
            self_scores(0)
            unit(U_K, 1, [1, 2, 3])
            self_scores(1)
            self_prob_transpose(0)
            self_attend(0)
            unit(U_V, 0)
            self_prob_transpose(1)
            self_attend(1)
            unit(U_V, 1)
            unit(U_O, 0)
            norm_between(1, U_O, r1, tok)
            unit(U_CQ, 1)
            key_bias_rows(0)
            unit(U_CK, 0)
            key_bias_rows(1)
            unit(U_CK, 1)
            key_bias_columns()
            pe.wait_ge(dve_evac, dve_count(U_CK, 1, KC - 1))
            cross_scores(0)
            cross_scores(1)
            for b in range(B):
                cross_prob_transpose(b)
                cross_attend(b)
                if b + 2 < B:
                    cross_scores(b + 2)
                cross_attend_transpose(b)
            unit(U_CV, 0)
            norm_between(2, U_CV, acc, tok2)
            unit(U_F, 1)
            for n in range(U_F + 1, U_M - 1):
                unit(n, 0)
                unit(n, 1)
            unit(U_M - 1, 0)
            norm_between(3, U_M - 1, acc, tok2)
            unit(U_M, 1)
            gate_rows(0)
            gate_rows(1)
            for n in range(U_M + 1, NU - 1):
                unit(n, 0)
                if n == U_M + 1:
                    gate_columns()
                unit(n, 1)
            unit(NU - 1, 0)
            unit(NU - 1, 1, [0])
            to_tokens(4, 0, NU - 1, acc)
            unit(NU - 1, 1, [1, 2, 3])
            to_tokens(4, 1, NU - 1, acc)

        @block.scalar
        def _(act):
            def split_weights(n, k):
                if k == 0:
                    act.wait_ge(weights_loaded, 16 * (n + 1))
                    if n >= 2:
                        act.wait_ge(gemm_done, GROUPS * (n - 1))
                act.activation(WH[n % 2][:, k, :], WR[:, k, :], ACT.Copy).then_inc(w_high, 1)

            def split_ct(b, i):
                act.wait_ge(ct_loaded[i], 16 * (b + 1))
                if b == 1:
                    act.wait_ge(gemm_done, GROUPS * (U_CK + 1))
                if b >= 2:
                    act.wait_ge(c_scores, b - 1)
                act.activation(ctH[b % 2][:, 2 * i:2 * i + 2, 0:M], ctR[:, 2 * i:2 * i + 2, :],
                               ACT.Copy).then_inc(ct_high, 1)

            def split_cn(b, i):
                act.wait_ge(cn_loaded[i], (16 if i < 2 else 32) * (b + 1))
                if b == 0:
                    act.wait_ge(x_ready, 16)
                else:
                    act.wait_ge(c_chunk, MC * (b - 1) + 2 * i + 2)
                act.activation(cnH[:, 2 * i:2 * i + 2, :], cnR[:, 2 * i:2 * i + 2, :],
                               ACT.Copy).then_inc(cn_high, 1)

            def unit(n, h, groups=range(KC)):
                for e in groups:
                    src = ps[:, e, 0:HALF]
                    kind = KINDS[n]
                    if act_writes(n):
                        act.wait_ge(gemm_done, GROUPS * n + KC * h + e + 1)
                    if kind == "fp32":
                        dst, col = (qT, C_BQ) if n == U_Q else (kT, C_BK)
                        act.activation(half(dst, h, e), src, ACT.Identity,
                                       bias=cst[:, col + e:col + e + 1]).then_inc(act_evac, 1)
                    elif kind == "split":
                        dst, col = (AH, C_BV) if n == U_V else (QH, C_CBQ)
                        act.activation(half(dst, h, e), src, ACT.Identity,
                                       bias=cst[:, col + e:col + e + 1]).then_inc(act_evac, 1)
                    elif kind == "split_nobias":
                        act.activation(half(AH, h, e), src, ACT.Copy).then_inc(act_evac, 1)
                    elif kind == "relu_bias":
                        j = (n - U_F) // 2
                        i = GROUPS * j + KC * h + e
                        b1 = cst[:, C_B1 + KC * j + e:C_B1 + KC * j + e + 1]
                        if i >= 3:
                            pi = i - 3
                            act.wait_ge(dve_evac, dve_count(U_F + 2 * (pi // GROUPS), pi % GROUPS // KC, pi % KC))
                        act.activation(relt[:, i % 3, :], src, ACT.Relu, bias=b1)
                        act.activation(half(AH, h, e), src, ACT.Relu, bias=b1).then_inc(act_evac, 1)
                    elif kind == "relu":
                        act.activation(half(AH, h, e), src, ACT.Relu).then_inc(act_evac, 1)
                    if 1 <= KC * h + e <= KC and n + 1 < NU:
                        split_weights(n + 1, KC * h + e - 1)

            def norm_features(i, h):
                for k in range(KC):
                    act.wait_ge(to_feat, 8 * i + KC * h + k + 1)
                    src = ps[:, 4 + k, 0:HALF]
                    if i in (0, 3):
                        act.activation(half(XH, h, k), src, ACT.Copy).then_inc(x_high, 1)
                        continue
                    gc, bc = (C_G1, C_E1) if i == 1 else (C_G2, C_E2)
                    c = KC * h + k
                    if c >= 2:
                        act.wait_ge(x_ready, 8 * i + c - 1)
                    gain, shift = cst[:, gc + k:gc + k + 1], cst[:, bc + k:bc + k + 1]
                    act.activation(lnt[:, c % 2, :], src, ACT.Identity, bias=shift, scale=gain)
                    act.activation(half(XH, h, k), src, ACT.Identity, bias=shift,
                                   scale=gain).then_inc(x_high, 1)

            def self_exp(h):
                act.wait_ge(s_max, h + 1)
                if h == 1:
                    act.wait_ge(s_probT, 1)
                for j in range(HB):
                    b = HB * h + j
                    ex = act.activation(sprob[:, j, :], ps[0:T, 4 + h, j * T:(j + 1) * T], ACT.Exp,
                                        bias=snb[:, b:b + 1], scale=SCALE, accum_out=ssum[:, b:b + 1])
                ex.then_inc(s_exp, 1)

            def self_probT(h):
                act.wait_ge(s_probT, h + 1)
                if h == 1:
                    act.wait_ge(s_att, KC)
                act.activation(sprobT[:, :, :].rearrange("p a b -> p (a b)"), ps[0:T, 6 + h, 0:HALF],
                               ACT.Copy).then_inc(s_probT_sb, 1)

            def self_attended(h):
                for k in range(KC):
                    act.wait_ge(s_att, KC * h + k + 1)
                    act.activation(half(QH, h, k), ps[:, k, 0:HALF], ACT.Copy).then_inc(s_att_high, 1)

            def cross_exp(b):
                bank = 4 + 2 * (b % 2)
                act.wait_ge(c_max, b + 1)
                if b == 0:
                    act.wait_ge(pads_set, 6)
                if b >= 2:
                    act.wait_ge(c_probT, b - 1)
                act.activation(prob[:, b % 2, 0:M].rearrange("p (i m) -> p i m", i=2), ps[0:T, bank:bank + 2, 0:MH],
                               ACT.Exp, bias=snb[:, b:b + 1], scale=SCALE,
                               accum_out=ssum[:, b:b + 1]).then_inc(c_exp, 1)

            def cross_probT(b):
                act.wait_ge(c_probT, b + 1)
                if b >= 1:
                    act.wait_ge(c_chunk, MC * b)
                act.activation(ptH[:, :].rearrange("p (i m) -> p i m", i=2), ps[:, 0:2, 0:3 * T],
                               ACT.Copy).then_inc(c_probT_high, 1)

            def cross_attended(b):
                act.wait_ge(c_chunk, MC * (b + 1))
                act.wait_ge(c_rec, b + 1)
                if b >= 2:
                    act.wait_ge(c_attT, b - 1)
                act.activation(utok[:, b % 2, :], ps[0:T, 2, :], ACT.Copy,
                               scale=srec[:, b:b + 1]).then_inc(c_att_sb, 1)

            def cross_attendedT(b):
                act.wait_ge(c_attT, b + 1)
                act.activation(AH[:, :, b * T:(b + 1) * T],
                               ps[:, 3, 0:KC * T].rearrange("p (k t) -> p k t", k=KC),
                               ACT.Copy).then_inc(c_attT_high, 1)

            def norm_between(i, n):
                unit(n, 1, [0, 1, 2])
                norm_features(i, 0)
                unit(n, 1, [3])
                unit(n + 1, 0, [0, 1, 2])
                norm_features(i, 1)
                unit(n + 1, 0, [3])

            act.wait_ge(consts_loaded, 16)
            act.activation(bkS[:, :, 0], cst[:, C_CBK:C_CBK + KC], ACT.Copy)
            act.activation(wgS[:, :, 0:NE], cst[:, C_WG:C_ALL].rearrange("p (k e) -> p k e", k=KC),
                           ACT.Copy).then_inc(small_high, 1)
            for k in range(KC):
                split_weights(0, k)
            norm_features(0, 0)
            unit(U_Q, 0)
            norm_features(0, 1)
            unit(U_Q, 1)
            unit(U_K, 0)
            unit(U_K, 1, [0])
            self_exp(0)
            unit(U_K, 1, [1, 2, 3])
            self_probT(0)
            self_exp(1)
            self_attended(0)
            unit(U_V, 0)
            self_probT(1)
            self_attended(1)
            unit(U_V, 1)
            unit(U_O, 0)
            norm_between(1, U_O)
            split_ct(0, 0)
            split_ct(0, 1)
            unit(U_CQ, 1)
            act.wait_ge(c_row, 1)
            act.activation(crow[:, 0:HALF], ps[0:2, 4, 0:HALF], ACT.Copy).then_inc(c_row_sb, 1)
            unit(U_CK, 0)
            for i in range(3):
                split_cn(0, i)
            act.wait_ge(c_row, 2)
            act.activation(crow[:, HALF:N], ps[0:2, 5, 0:HALF], ACT.Copy).then_inc(c_row_sb, 1)
            unit(U_CK, 1)
            split_ct(1, 0)
            split_ct(1, 1)
            cross_exp(0)
            for b in range(B):
                cross_probT(b)
                if b + 1 < B:
                    cross_exp(b + 1)
                if b + 2 < B:
                    split_ct(b + 2, 0)
                    split_ct(b + 2, 1)
                cross_attended(b)
                if b + 1 < B:
                    for i in range(3):
                        split_cn(b + 1, i)
                cross_attendedT(b)
            unit(U_CV, 0)
            norm_between(2, U_CV)
            unit(U_F, 1)
            for n in range(U_F + 1, U_M - 1):
                unit(n, 0)
                unit(n, 1)
            unit(U_M - 1, 0)
            norm_between(3, U_M - 1)
            unit(U_M, 1)
            for h in range(2):
                act.wait_ge(g_rows, h + 1)
                act.activation(glog[:, h * HALF:(h + 1) * HALF], ps[0:2 * NE, 4 + h, 0:HALF],
                               ACT.Copy).then_inc(g_rows_sb, 1)
            unit(U_M + 1, 0)
            act.wait_ge(g_shift, 2)
            act.activation(gexp[:, :, :], gexp[:, :, :], ACT.Exp)
            act.activation(gsm[:, 0, :], gsm[:, 0, :], ACT.Exp).then_inc(g_exp, 1)
            unit(U_M + 1, 1)
            for n in range(U_M + 2, NU):
                unit(n, 0)
                unit(n, 1)

        @block.vector
        def _(dve):
            steps = [0]

            def settle(ins):
                steps[0] += 1
                ins.then_inc(dve_step, 1)
                dve.wait_ge(dve_step, steps[0])

            def split_weights(n, k):
                dve.wait_ge(w_high, KC * n + k + 1)
                dve.tensor_tensor(WL[n % 2][:, k, :], WR[:, k, :], raw(WH[n % 2][:, k, :]),
                                  ALU.subtract).then_inc(w_low, 1)

            def split_ct(b, i):
                dve.wait_ge(ct_high, 2 * b + i + 1)
                dve.tensor_tensor(ctL[b % 2][:, 2 * i:2 * i + 2, 0:M], ctR[:, 2 * i:2 * i + 2, :],
                                  raw(ctH[b % 2][:, 2 * i:2 * i + 2, 0:M]), ALU.subtract).then_inc(ct_low, 1)

            def split_cn(b, i):
                dve.wait_ge(cn_high, 3 * b + i + 1)
                dve.tensor_tensor(cnL[:, 2 * i:2 * i + 2, :], cnR[:, 2 * i:2 * i + 2, :],
                                  raw(cnH[:, 2 * i:2 * i + 2, :]), ALU.subtract).then_inc(cn_low, 1)

            def unit(n, h, groups=range(KC)):
                for e in groups:
                    src = ps[:, e, 0:HALF]
                    kind = KINDS[n]
                    if act_writes(n) and dve_writes(n):
                        dve.wait_ge(act_evac, act_count(n, h, e))
                    elif dve_writes(n):
                        dve.wait_ge(gemm_done, GROUPS * n + KC * h + e + 1)
                    if kind == "split":
                        dh, dl, col = (AH, AL, C_BV) if n == U_V else (QH, QL, C_CBQ)
                        dve.scalar_tensor_tensor(out=half(dl, h, e), in0=src, scalar=cst[:, col + e:col + e + 1],
                                                 in1=raw(half(dh, h, e)), op0=ALU.add,
                                                 op1=ALU.subtract).then_inc(dve_evac, 1)
                    elif kind == "split_nobias":
                        dve.tensor_tensor(half(AL, h, e), src, raw(half(AH, h, e)),
                                          ALU.subtract).then_inc(dve_evac, 1)
                    elif kind == "relu_bias":
                        i = GROUPS * ((n - U_F) // 2) + KC * h + e
                        dve.tensor_tensor(half(AL, h, e), relt[:, i % 3, :], raw(half(AH, h, e)),
                                          ALU.subtract).then_inc(dve_evac, 1)
                    elif kind == "relu":
                        dve.scalar_tensor_tensor(out=half(AL, h, e), in0=src, scalar=0.0, in1=raw(half(AH, h, e)),
                                                 op0=ALU.max, op1=ALU.subtract).then_inc(dve_evac, 1)
                    elif kind in ("residual", "down_residual"):
                        col = {U_O: C_BO, U_CV: C_CBV}.get(n, C_B2)
                        dst = r1 if n == U_O else acc
                        settle(dve.scalar_tensor_tensor(out=half(dst, h, e), in0=src,
                                                        scalar=cst[:, col + e:col + e + 1],
                                                        in1=raw(half(XH, h, e)), op0=ALU.add, op1=ALU.add))
                        dve.tensor_tensor(half(dst, h, e), half(dst, h, e), raw(half(XL, h, e)),
                                          ALU.add).then_inc(dve_evac, 1)
                    elif kind == "down_first":
                        dve.tensor_copy(half(acc, h, e), src).then_inc(dve_evac, 1)
                    elif kind == "down_add":
                        dve.wait_ge(dve_evac, dve_count(n - 2, h, e))
                        dve.tensor_tensor(half(acc, h, e), src, half(acc, h, e), ALU.add).then_inc(dve_evac, 1)
                    if 1 <= KC * h + e <= KC and n + 1 < NU:
                        split_weights(n + 1, KC * h + e - 1)

            def statistics(h, srcs):
                for j in range(HB):
                    b = HB * h + j
                    if srcs is None:
                        st = dve.bn_stats(bnst[:, b, :], tok[:, b, :])
                    else:
                        dve.wait_ge(to_tok, srcs + j + 1)
                        st = dve.bn_stats(bnst[:, b, :], ps[0:T, 4 + j, :])
                settle(st)
                for j in range(HB):
                    ag = dve.bn_aggr(mv[:, HB * h + j, :], bnst[:, HB * h + j, :])
                ag.then_inc(stats_ready, 1)

            def normalise(i, h, dst):
                dve.wait_ge(rstd_ready, 2 * i + h + 1)
                for j in range(HB):
                    b = HB * h + j
                    src = tok[:, b, :] if i == 0 else ps[0:T, 4 + j, :]
                    dve.tensor_scalar(dst[:, b, :], src, mv[:, b, 0:1], rstd[:, b:b + 1], ALU.subtract,
                                      ALU.mult).then_inc(tok_ready, 1)

            def norm_features(i, h):
                for k in range(KC):
                    dve.wait_ge(x_high, 8 * i + KC * h + k + 1)
                    src = ps[:, 4 + k, 0:HALF] if i in (0, 3) else lnt[:, (KC * h + k) % 2, :]
                    dve.tensor_tensor(half(XL, h, k), src, raw(half(XH, h, k)), ALU.subtract).then_inc(x_ready, 1)

            def self_max(h):
                dve.wait_ge(s_scores, h + 1)
                settle(dve.tensor_reduce(smx[:, HB * h:HB * (h + 1)],
                                         ps[0:T, 4 + h, 0:HALF].rearrange("p (j s) -> p j s", j=HB), AX.X, ALU.max))
                dve.tensor_scalar(snb[:, HB * h:HB * (h + 1)], smx[:, HB * h:HB * (h + 1)], -SCALE, None,
                                  ALU.mult).then_inc(s_max, 1)

            def self_normalise(h):
                dve.wait_ge(s_exp, h + 1)
                settle(dve.reciprocal(srec[:, HB * h:HB * (h + 1)], ssum[:, HB * h:HB * (h + 1)]))
                for j in range(HB):
                    b = HB * h + j
                    nm = dve.tensor_scalar(sprob[:, j, :], sprob[:, j, :], srec[:, b:b + 1], None, ALU.mult)
                nm.then_inc(s_norm, 1)

            def self_attended(h):
                for k in range(KC):
                    dve.wait_ge(s_att_high, KC * h + k + 1)
                    dve.tensor_tensor(half(QL, h, k), ps[:, k, 0:HALF], raw(half(QH, h, k)),
                                      ALU.subtract).then_inc(s_att_low, 1)

            def cross_max(b):
                bank = 4 + 2 * (b % 2)
                dve.wait_ge(c_scores, b + 1)
                settle(dve.tensor_reduce(smx[:, b:b + 1], ps[0:T, bank:bank + 2, 0:MH], AX.XY, ALU.max))
                settle(dve.tensor_tensor(smx[:, b:b + 1], smx[:, b:b + 1], cshift[:, b:b + 1], ALU.add))
                settle(dve.tensor_tensor(snb[:, b:b + 1], cshift[:, b:b + 1], smx[:, b:b + 1], ALU.subtract))
                dve.tensor_scalar(snb[:, b:b + 1], snb[:, b:b + 1], SCALE, None, ALU.mult).then_inc(c_max, 1)

            def cross_probT(b):
                dve.wait_ge(c_probT_high, b + 1)
                dve.tensor_tensor(ptL[:, :].rearrange("p (i m) -> p i m", i=2), ps[:, 0:2, 0:3 * T],
                                  raw(ptH[:, :].rearrange("p (i m) -> p i m", i=2)),
                                  ALU.subtract).then_inc(c_probT_low, 1)

            def cross_recip(b):
                dve.wait_ge(c_exp, b + 1)
                dve.reciprocal(srec[:, b:b + 1], ssum[:, b:b + 1]).then_inc(c_rec, 1)

            def cross_attendedT(b):
                dve.wait_ge(c_attT_high, b + 1)
                dve.tensor_tensor(AL[:, :, b * T:(b + 1) * T], ps[:, 3, 0:KC * T].rearrange("p (k t) -> p k t", k=KC),
                                  raw(AH[:, :, b * T:(b + 1) * T]), ALU.subtract).then_inc(c_attT_low, 1)

            def norm_between(i, n, dst):
                unit(n, 1, [0])
                statistics(0, 8 * (i - 1))
                unit(n, 1, [1])
                normalise(i, 0, dst)
                unit(n, 1, [2])
                norm_features(i, 0)
                unit(n, 1, [3])
                unit(n + 1, 0, [0])
                statistics(1, 8 * (i - 1) + HB)
                unit(n + 1, 0, [1])
                normalise(i, 1, dst)
                unit(n + 1, 0, [2])
                norm_features(i, 1)
                unit(n + 1, 0, [3])

            def last_norms(h):
                statistics(h, 16 + HB * h)
                dve.wait_ge(stats_ready, 7 + 2 * h)
                dve.wait_ge(gb_loaded, 32)
                for j in range(HB):
                    b = HB * h + j
                    z = dve.scalar_tensor_tensor(out=tok2[:, b, :], in0=ps[0:T, 4 + j, :], scalar=mv[:, b, 0:1],
                                                 in1=g3b[0:T, :], op0=ALU.subtract, op1=ALU.mult)
                settle(z)
                dve.wait_ge(rstd_ready, 6 + 2 * h + 1)
                dve.wait_ge(xres_ready, HB * (h + 1))
                for j in range(HB):
                    b = HB * h + j
                    z = dve.scalar_tensor_tensor(out=tok[:, b, :], in0=tok2[:, b, :], scalar=rstd[:, b:b + 1],
                                                 in1=tok[:, b, :], op0=ALU.mult, op1=ALU.add)
                settle(z)
                statistics(h, None)
                dve.wait_ge(rstd_ready, 6 + 2 * h + 2)
                for j in range(HB):
                    b = HB * h + j
                    dve.tensor_scalar(tok2[:, b, :], tok[:, b, :], mv[:, b, 0:1], rstd[:, b:b + 1], ALU.subtract,
                                      ALU.mult).then_inc(tok_ready, 1)

            def gate_top():
                dve.wait_ge(g_cols, 1)
                settle(dve.tensor_copy(gl[:, :, :], ps[0:T, 6, 0:B * NE].rearrange("p (b e) -> p b e", b=B)))
                for b in range(B):
                    tp = dve.max(gtop[:, b, :], gl[:, b, :])
                settle(tp)
                dve.tensor_tensor(gexp[:, :, :], gl[:, :, :], gtop[:, :, 0:1].to_broadcast([T, B, NE]),
                                  ALU.subtract).then_inc(g_shift, 1)
                dve.tensor_tensor(gsm[:, 0, :], gtop[:, :, 1], gtop[:, :, 0], ALU.subtract).then_inc(g_shift, 1)

            def gate_weights():
                dve.wait_ge(g_exp, 1)
                settle(dve.tensor_reduce(gsm[:, 1, :], gexp[:, :, :], AX.X, ALU.add))
                settle(dve.reciprocal(gsm[:, 2, :], gsm[:, 1, :]))
                settle(dve.tensor_tensor(gsm[:, 3, :], gsm[:, 0, :], gsm[:, 2, :], ALU.mult))
                settle(dve.tensor_tensor(gsm[:, 4, :], gsm[:, 2, :], gsm[:, 3, :], ALU.add))
                settle(dve.tensor_scalar(gsm[:, 4, :], gsm[:, 4, :], F32_EPS, None, ALU.max))
                settle(dve.reciprocal(gsm[:, 5, :], gsm[:, 4, :]))
                settle(dve.tensor_tensor(gsm[:, 2, :], gsm[:, 2, :], gsm[:, 5, :], ALU.mult))
                settle(dve.tensor_tensor(gsm[:, 3, :], gsm[:, 3, :], gsm[:, 5, :], ALU.mult))
                dve.tensor_tensor(gsm[:, 6, :], gsm[:, 2, :], gsm[:, 3, :], ALU.add).then_inc(g_weight, 1)

            def finish(h):
                dve.wait_ge(g_weight, 1)
                for j in range(HB):
                    b = HB * h + j
                    dve.wait_ge(to_tok, 24 + b + 1)
                    if b >= 4:
                        dve.wait_ge(stored, 16 * B // 2)
                    dve.scalar_tensor_tensor(out=outb[:, b % 4, :], in0=ps[0:T, 4 + j, :], scalar=gsm[:, 6, b:b + 1],
                                             in1=tok[:, b, :], op0=ALU.mult, op1=ALU.add).then_inc(out_ready, 1)

            dve.wait_ge(x_loaded[0], 16)
            statistics(0, None)
            dve.wait_ge(x_loaded[1], 16)
            statistics(1, None)
            normalise(0, 0, tok)
            normalise(0, 1, tok)
            dve.wait_ge(small_high, 1)
            dve.tensor_tensor(bkS[:, :, 1], cst[:, C_CBK:C_CBK + KC], raw(bkS[:, :, 0]), ALU.subtract)
            dve.tensor_tensor(wgS[:, :, NE:2 * NE], cst[:, C_WG:C_ALL].rearrange("p (k e) -> p k e", k=KC),
                              raw(wgS[:, :, 0:NE]), ALU.subtract).then_inc(small_low, 1)
            for k in range(KC):
                split_weights(0, k)
            norm_features(0, 0)
            unit(U_Q, 0)
            norm_features(0, 1)
            unit(U_Q, 1)
            unit(U_K, 0)
            unit(U_K, 1, [0])
            self_max(0)
            unit(U_K, 1, [1, 2, 3])
            self_normalise(0)
            self_max(1)
            self_attended(0)
            unit(U_V, 0, [0])
            self_normalise(1)
            unit(U_V, 0, [1, 2, 3])
            self_attended(1)
            unit(U_V, 1)
            unit(U_O, 0)
            norm_between(1, U_O, tok)
            split_ct(0, 0)
            split_ct(0, 1)
            unit(U_CQ, 1)
            unit(U_CK, 0)
            for i in range(3):
                split_cn(0, i)
            unit(U_CK, 1)
            split_ct(1, 0)
            dve.wait_ge(c_col, 1)
            dve.tensor_copy(cshift[:, :], ps[0:T, 6, 0:B]).then_inc(c_col_sb, 1)
            dve.wait_ge(c_col_sb, 1)
            cross_max(0)
            split_ct(1, 1)
            cross_recip(0)
            for b in range(B):
                if b + 1 < B:
                    cross_max(b + 1)
                cross_probT(b)
                if b + 1 < B:
                    cross_recip(b + 1)
                if b + 2 < B:
                    split_ct(b + 2, 0)
                    split_ct(b + 2, 1)
                if b + 1 < B:
                    for i in range(3):
                        split_cn(b + 1, i)
                cross_attendedT(b)
            unit(U_CV, 0)
            norm_between(2, U_CV, tok2)
            unit(U_F, 1)
            for n in range(U_F + 1, U_M - 1):
                unit(n, 0)
                unit(n, 1)
            unit(U_M - 1, 0)
            n = U_M - 1
            unit(n, 1, [0])
            last_norms(0)
            unit(n, 1, [1, 2])
            norm_features(3, 0)
            unit(n, 1, [3])
            unit(n + 1, 0, [0])
            last_norms(1)
            unit(n + 1, 0, [1, 2])
            norm_features(3, 1)
            unit(n + 1, 0, [3])
            unit(U_M, 1)
            unit(U_M + 1, 0)
            gate_top()
            unit(U_M + 1, 1)
            gate_weights()
            for n in range(U_M + 2, NU - 1):
                unit(n, 0)
                unit(n, 1)
            unit(NU - 1, 0)
            unit(NU - 1, 1, [0])
            finish(0)
            unit(NU - 1, 1, [1, 2, 3])
            finish(1)


def _chunks(np, v):
    return np.asarray(v).reshape(-1, P).T


def kernel(**inputs):
    import numpy as np
    import concourse.bacc as bacc
    from concourse import mybir as mb
    from concourse.bass_utils import run_bass_kernel_spmd as run

    a = {k: np.asarray(v) for k, v in inputs.items()}
    x, mem = a["x"], a["ctx_1024"]
    ipw, ipb = a["L0_xattn_in_proj_w"], a["L0_xattn_in_proj_b"]

    def block(w):
        return w.reshape(KC, P, D).transpose(1, 0, 2)

    units = [ipw[0:D].T, ipw[D:2 * D].T, ipw[2 * D:3 * D].T, a["L0_xattn_out_proj_w"].T,
             a["L0_xattn_wq"].T, a["L0_xattn_wk"], a["L0_xattn_wv"].T]
    for up, down in ((a["L0_xattn_w1"].T, a["L0_xattn_w2"].T), (a["L0_ffn_w1"], a["L0_ffn_w2"])):
        for j in range(NF):
            units += [up[:, j * D:(j + 1) * D], down[j * D:(j + 1) * D, :]]
    wts = np.ascontiguousarray(np.stack([block(u) for u in units]))
    vectors = [ipb[0:D], ipb[D:2 * D], ipb[2 * D:3 * D], a["L0_xattn_out_proj_b"], a["L0_xattn_bq"],
               a["L0_xattn_bk"], a["L0_xattn_bv"], a["L0_xattn_b1"], a["L0_xattn_b2"], a["L0_xattn_g1"],
               a["L0_xattn_be1"], a["L0_xattn_g2"], a["L0_xattn_be2"]]
    gate = a["L0_ffn_Wg"].reshape(KC, P, NE).transpose(1, 0, 2).reshape(P, KC * NE)
    consts = np.ascontiguousarray(np.concatenate([_chunks(np, v) for v in vectors] + [gate], axis=1))
    arrays = {
        "x_in": np.ascontiguousarray(x),
        "ctxt_in": np.ascontiguousarray(mem.transpose(0, 2, 1)),
        "ctxn_in": np.ascontiguousarray(mem),
        "wts_in": wts,
        "consts_in": consts,
        "g3_in": np.ascontiguousarray(a["L0_xattn_g3"]),
        "be3_in": np.ascontiguousarray(a["L0_xattn_be3"]),
    }
    nc = bacc.Bacc("TRN2", target_bir_lowering=False, num_devices=1)
    args = [nc.dram_tensor(n, v.shape, mb.dt.from_np(v.dtype), kind="ExternalInput").ap() for n, v in arrays.items()]
    args.append(nc.dram_tensor("out", (B, T, D), F32, kind="ExternalOutput").ap())
    build(nc, *args)
    r = run(nc, [arrays], core_ids=[0])
    return r.results[0]["out"]
```

```python
from contextlib import ExitStack

import concourse.bass as bass
from concourse import mybir

F32 = mybir.dt.float32
F32R = mybir.dt.float32r
ALU = mybir.AluOpType
ACT = mybir.ActivationFunctionType
AX = mybir.AxisListType

P = 128
B, T, D = 8, 100, 512
M = 722
FF = 2048
NE = 8
N = B * T
HALF = N // 2
HB = B // 2
KC = D // P
MC = (M + P - 1) // P
MH = M // 2
MW = MH + 1
ML = M - (MC - 1) * P
NF = FF // D
EPS = 1e-5
F32_EPS = 1.1920928955078125e-07
SCALE = 1.0 / float(D) ** 0.5

U_Q, U_K, U_V, U_O, U_CQ, U_CK, U_CV = range(7)
U_F = 7
U_M = U_F + 2 * NF
NU = U_M + 2 * NF
KINDS = (["fp32", "fp32", "split", "residual", "split", "split_nobias", "residual"]
         + ["relu_bias", "down_residual"] + ["relu_bias", "down_add"] * (NF - 1)
         + ["relu", "down_first"] + ["relu", "down_add"] * (NF - 1))

ORDER = ([(U_Q, 0), (U_K, 0), (U_Q, 1), (U_K, 1), (U_V, 0), (U_O, 0), (U_V, 1), (U_O, 1)]
         + [(U_CQ, 0), (U_CK, 0), (U_CQ, 1), (U_CK, 1), (U_CV, 0), (U_CV, 1)])
for _first in (U_F, U_M):
    _up, _down = [[_first + 2 * j + i for j in range(NF)] for i in range(2)]
    if _first == U_F:
        ORDER += [(_up[0], 0), (_down[0], 0), (_up[0], 1), (_down[0], 1),
                  (_up[1], 0), (_up[1], 1), (_down[1], 0), (_down[1], 1),
                  (_up[2], 0), (_up[2], 1), (_down[2], 0), (_up[3], 0), (_down[3], 0),
                  (_down[2], 1), (_up[3], 1), (_down[3], 1)]
    else:
        ORDER += [(_up[0], 0), (_down[0], 0), (_up[1], 0), (_up[0], 1), (_down[0], 1), (_up[1], 1),
                  (_down[1], 0), (_down[1], 1)]
        for _j in range(2, NF):
            ORDER += [(_up[_j], 0), (_up[_j], 1), (_down[_j], 0), (_down[_j], 1)]
POS = {nh: i for i, nh in enumerate(ORDER)}
LAST = {n: max(POS[n, 0], POS[n, 1]) for n in range(NU)}
SLOT = [n % 2 if n < U_F + 2 else [2, 1, 0][(n - U_F - 2) % 3] for n in range(NU)]
BEFORE = {n: max((m for m in range(n) if SLOT[m] == SLOT[n]), default=None) for n in range(NU)}
SPLIT_AT = {LAST[BEFORE[n]] + 1 + (n == U_F): n for n in range(2, NU) if BEFORE[n] is not None}
SPLIT_AT.update({0: 1, POS[U_F + 1, 0]: U_F + 2})
assert len(SPLIT_AT) == NU - 1
assert all(POS[n, 0] > at for at, n in SPLIT_AT.items())

C_BQ, C_BK, C_BV, C_BO, C_CBQ, C_CBK, C_CBV, C_B1 = 0, 4, 8, 12, 16, 20, 24, 28
C_B2, C_G1, C_E1, C_G2, C_E2, C_WG = 44, 48, 52, 56, 60, 64
C_ALL = C_WG + KC * NE


def act_writes(n):
    return KINDS[n] in ("fp32", "split", "split_nobias", "relu_bias", "relu")


def dve_writes(n):
    return KINDS[n] != "fp32"


def gemm_count(n, h, e):
    return KC * POS[n, h] + e + 1


def act_count(n, h, e):
    return KC * sum(act_writes(m) for m, _ in ORDER[:POS[n, h]]) + e + 1


def dve_count(n, h, e):
    return KC * sum(dve_writes(m) for m, _ in ORDER[:POS[n, h]]) + e + 1


def frees_on_act(n):
    return KINDS[n] in ("fp32", "relu_bias")


def build(nc, x, ctxt, ctxn, wts, consts, g3, be3, out):
    with ExitStack() as ctx:
        def sem(name):
            return ctx.enter_context(nc.semaphore(name))

        base = 16512
        at = {}
        for name, size in (("X", 2 * KC * N * 4), ("R1", 2 * KC * N * 4), ("R2", 29312), ("R3", B * D * 4),
                           ("R4", 2 * KC * 724 * 4), ("R5", 2 * MC * D * 4), ("R6", KC * M * 4 + MC * D * 4),
                           ("W", 5 * KC * D * 4), ("C", 3360)):
            at[name] = base
            base += (size + 31) // 32 * 32

        def sb(name, region, offset, shape, dt=F32):
            return nc.alloc_sbuf_tensor_at(name, shape, dt, offset=at[region] + offset)

        HS = KC * HALF * 4

        def halves(name, region, dt=F32R, start=0, step=2 * HS):
            return [sb(name + str(h), region, start + step * h, [P, KC, HALF], dt) for h in range(2)]

        XH = halves("XH", "X")
        XL = halves("XL", "X", start=HS)
        XS = halves("XS", "X", F32)
        XT = halves("XT", "X", F32, HS)
        xn = [sb("xn%d" % h, "X", 2 * HS * h, [T, HB, D]) for h in range(2)]
        qT = halves("qT", "R1", F32)
        kT = halves("kT", "R1", F32, HS)
        AH = halves("AH", "R1")
        AL = halves("AL", "R1", start=HS)
        AT = halves("AT", "R1", F32, HS)
        QH = halves("QH", "R2")
        QL = halves("QL", "R2", start=HS)
        acc = halves("acc", "R2", F32, step=HS)
        tok = sb("tok", "R3", 0, [T, B, D])
        CTS = KC * 724 * 4
        ctH = [sb("ctH0", "R4", 0, [P, KC, 724], F32R), sb("ctH1", "R2", 0, [P, KC, 724], F32R)]
        ctL = [sb("ctL0", "R4", CTS, [P, KC, 724], F32R), sb("ctL1", "R3", 0, [P, KC, 724], F32R)]
        cnH = sb("cnH", "R5", 0, [P, MC, D], F32R)
        cnL = sb("cnL", "R5", MC * D * 4, [P, MC, D], F32R)
        prob = [sb("prob0", "R2", 4 * HS, [T, MC * P]), sb("prob1", "R2", 2 * HS, [T, MC * P])]
        ptH = [sb("ptH0", "R3", CTS, [P, MC * T], F32R), sb("ptH1", "R2", 2 * HS + 3072, [P, MC * T], F32R)]
        ptL = [sb("ptL0", "R3", CTS + 2400, [P, MC * T], F32R), sb("ptL1", "R2", 2 * HS + 5472, [P, MC * T], F32R)]
        utok = sb("utok", "R2", 2 * HS + 7872, [T, 2, D])
        crow = sb("crow", "R3", CTS, [2, N])
        sprob = [sb("sprob%d" % h, "R5", 1600 * h, [T, HB, T]) for h in range(2)]
        sprobT = [sb("sprobT%d" % h, "R5", 3200 + 1600 * h, [T, HB, T]) for h in range(2)]
        tok2 = sb("tok2", "R4", 0, [T, B, D])
        g3b = sb("g3b", "R5", 0, [P, D])
        be3b = sb("be3b", "R5", 2048, [P, D])
        glog = sb("glog", "R5", 4096, [2 * NE, N])
        outb = sb("outb", "R5", 8192, [T, B, D])
        ctR = sb("ctR", "R6", 0, [P, KC, M])
        cnR = sb("cnR", "R6", KC * M * 4, [P, MC, D])
        wat = [("W", 0), ("W", 16384), ("R6", 0)]
        WH = [sb("WH%d" % i, r, o, [P, KC, D], F32R) for i, (r, o) in enumerate(wat)]
        WL = [sb("WL%d" % i, r, o + 8192, [P, KC, D], F32R) for i, (r, o) in enumerate(wat)]
        WR = sb("WR", "W", 32768, [P, KC, D])
        off = [0]

        def small(name, shape, dt=F32):
            size = 4
            for s in shape[1:]:
                size *= s
            t = sb(name, "C", off[0], shape, dt)
            off[0] += (size + 31) // 32 * 32
            return t

        ident = small("ident", [P, P])
        cst = small("cst", [P, C_ALL])
        bkS = small("bkS", [P, KC, 2], F32R)
        wgS = small("wgS", [P, KC, 2 * NE], F32R)
        ones2 = small("ones2", [2, 1])
        fold = small("fold", [2 * NE, NE])
        bnst = small("bnst", [T, B, 6])
        mv = small("mv", [T, B, 2])
        veps = small("veps", [T, HB])
        rstd = small("rstd", [T, B])
        nmr = small("nmr", [T, B])
        nhalf = small("nhalf", [T, HB])
        smx = small("smx", [T, B])
        snb = small("snb", [T, B])
        ssum = small("ssum", [T, B])
        srec = small("srec", [T, B])
        cshift = small("cshift", [T, B])
        gl = small("gl", [T, B, NE])
        gtop = small("gtop", [T, B, NE])
        gexp = small("gexp", [T, B, NE])
        gsm = small("gsm", [T, 8, B])
        assert off[0] <= 3360, off[0]

        ps = ctx.enter_context(nc.psum_tensor("ps", [P, 8, 512], F32))

        x_loaded = [sem("x_loaded%d" % i) for i in range(4)]
        w0_loaded = sem("w0_loaded")
        consts_loaded = sem("consts_loaded")
        weights_loaded = sem("weights_loaded")
        ct_loaded = [sem("ct_loaded0"), sem("ct_loaded1")]
        cn_loaded = [sem("cn_loaded0"), sem("cn_loaded1"), sem("cn_loaded2")]
        xres_loaded = sem("xres_loaded")
        gb_loaded = sem("gb_loaded")
        stored = sem("stored")
        pool_init = sem("pool_init")
        pads_set = sem("pads_set")
        pool_step = sem("pool_step")
        rstd_ready = sem("rstd_ready")
        xres_ready = sem("xres_ready")
        w_high = sem("w_high")
        w_low = sem("w_low")
        ct_high, ct_low = sem("ct_high"), sem("ct_low")
        cn_high, cn_low = sem("cn_high"), sem("cn_low")
        small_high, small_low = sem("small_high"), sem("small_low")
        gemm_done = sem("gemm_done")
        act_evac, dve_evac = sem("act_evac"), sem("dve_evac")
        dve_step = sem("dve_step")
        stats_ready = sem("stats_ready")
        nmr_ready = sem("nmr_ready")
        tok_ready = sem("tok_ready")
        to_tok = sem("to_tok")
        to_feat = sem("to_feat")
        x_high, x_ready = sem("x_high"), sem("x_ready")
        s_scores, s_max, s_exp, s_norm = sem("s_scores"), sem("s_max"), sem("s_exp"), sem("s_norm")
        s_probT, s_probT_sb = sem("s_probT"), sem("s_probT_sb")
        s_att, s_att_high, s_att_low = sem("s_att"), sem("s_att_high"), sem("s_att_low")
        c_row, c_row_sb, c_col, c_col_sb = sem("c_row"), sem("c_row_sb"), sem("c_col"), sem("c_col_sb")
        c_scores, c_max, c_exp, c_rec = sem("c_scores"), sem("c_max"), sem("c_exp"), sem("c_rec")
        c_probT, c_probT_high, c_probT_low = sem("c_probT"), sem("c_probT_high"), sem("c_probT_low")
        c_chunk = sem("c_chunk")
        c_att_sb = sem("c_att_sb")
        c_attT, c_attT_high, c_attT_low = sem("c_attT"), sem("c_attT_high"), sem("c_attT_low")
        g_rows, g_rows_sb, g_cols, g_shift = sem("g_rows"), sem("g_rows_sb"), sem("g_cols"), sem("g_shift")
        g_exp, g_weight = sem("g_exp"), sem("g_weight")
        out_ready = sem("out_ready")

        def half(t, h, k):
            return t[h][:, k, :]

        def tokens(t, b):
            return t[b // HB][:, :, b % HB * T:(b % HB + 1) * T]

        def bank(n, h, e):
            return e % 2 if (n, h) == (U_CV, 0) else e

        def raw(ap):
            return ap.bitcast(F32)

        operand = {}
        for n in range(NU):
            operand[n] = (XH, XL)
        operand[U_V] = operand[U_CK] = (QH, QL)
        operand[U_O] = operand[U_CV] = (AH, AL)
        for j in range(NF):
            operand[U_F + 2 * j + 1] = operand[U_M + 2 * j + 1] = (AH, AL)

        def wait_operand(eng, n, h, k):
            if n in (U_Q, U_K):
                eng.wait_ge(x_ready, KC * h + k + 1)
            elif n == U_V:
                eng.wait_ge(s_att_low, KC * h + k + 1)
            elif n in (U_O, U_CK):
                eng.wait_ge(dve_evac, dve_count(n - 1, h, k))
            elif n == U_CQ:
                eng.wait_ge(x_ready, 8 + KC * h + k + 1)
            elif n == U_CV:
                eng.wait_ge(c_attT_low, HB * (h + 1))
            elif n >= U_F and (n - U_F) % 2:
                eng.wait_ge(dve_evac, dve_count(n - 1, h, k))
            elif n < U_M:
                eng.wait_ge(x_ready, 16 + KC * h + k + 1)
            else:
                eng.wait_ge(x_ready, 24 + KC * h + k + 1)

        block = ctx.enter_context(nc.Block())

        @block.sync
        def _(sp):
            def load_x(i):
                sp.dma_start(tok[:, 2 * i:2 * i + 2, :], x[2 * i:2 * i + 2].rearrange("b t d -> t b d")
                             ).then_inc(x_loaded[i], 16)

            load_x(0)
            load_x(1)
            sp.dma_start(cst[:, :], consts).then_inc(consts_loaded, 16)
            sp.dma_start(WR[:, 0:2, :], wts[0, :, 0:2, :]).then_inc(w0_loaded, 16)
            sp.dma_start(WR[:, 2:KC, :], wts[0, :, 2:KC, :]).then_inc(weights_loaded, 16)
            load_x(2)
            load_x(3)

            def load_weights(n):
                sp.wait_ge(w_low, KC * n)
                sp.dma_start(WR[:, :, :], wts[n]).then_inc(weights_loaded, 16)

            def load_ct(b):
                for i in range(2):
                    if b >= 1:
                        sp.wait_ge(ct_low, 2 * (b - 1) + i + 1)
                    sp.dma_start(ctR[:, 2 * i:2 * i + 2, :],
                                 ctxt[b, 2 * P * i:2 * P * (i + 1), :].rearrange("(k p) m -> p k m", p=P)
                                 ).then_inc(ct_loaded[i], 16)

            def load_cn(b):
                for i in range(3):
                    if b >= 1:
                        sp.wait_ge(cn_low, 3 * (b - 1) + i + 1)
                    if b == 0 and i == 2:
                        sp.wait_ge(pads_set, 1)
                    full = 2 if i < 2 else 1
                    sp.dma_start(cnR[:, 2 * i:2 * i + full, :],
                                 ctxn[b, 2 * P * i:2 * P * i + full * P, :].rearrange("(c p) d -> p c d", p=P)
                                 ).then_inc(cn_loaded[i], 16)
                    if i == 2:
                        sp.dma_start(cnR[0:ML, MC - 1, :], ctxn[b, (MC - 1) * P:M, :]).then_inc(cn_loaded[i], 16)

            load_ct(0)
            load_weights(1)
            load_weights(2)
            load_cn(0)
            for n in range(3, U_CQ + 1):
                load_weights(n)
            load_ct(1)
            load_weights(U_CK)
            load_weights(U_CV)
            load_cn(1)
            load_ct(2)
            load_weights(U_F)
            load_ct(3)
            for b in range(B):
                if b + 2 < B:
                    load_cn(b + 2)
                if b + 4 < B:
                    load_ct(b + 4)
            sp.wait_ge(c_attT, B)
            sp.dma_start(tok[:, :, :], x.rearrange("b t d -> t b d")).then_inc(xres_loaded, 16)
            sp.dma_start(g3b[:, :], g3.partition_broadcast(P)).then_inc(gb_loaded, 16)
            sp.dma_start(be3b[:, :], be3.partition_broadcast(P)).then_inc(gb_loaded, 16)
            for n in range(U_F + 1, NU):
                load_weights(n)
            for b in range(B):
                sp.wait_ge(out_ready, b + 1)
                sp.dma_start(out[b], outb[:, b, :]).then_inc(stored, 16)
            sp.wait_ge(stored, 16 * B)

        @block.gpsimd
        def _(pool):
            pool.memset(ident[:, :], 0.0).then_inc(pool_step, 1)
            pool.wait_ge(pool_step, 1)
            pool.affine_select(out=ident[:, :], in_=ident[:, :], compare_op=ALU.not_equal, fill=1.0, base=0,
                               pattern=[[-1, P]], channel_multiplier=1).then_inc(pool_step, 1)
            pool.memset(nhalf[:, :], -0.5)
            pool.memset(ones2[:, :], 1.0)
            pool.wait_ge(pool_step, 2)
            pool.tensor_tensor(fold[:, :], ident[0:2 * NE, 0:NE], ident[0:2 * NE, NE:2 * NE],
                               ALU.add).then_inc(pool_init, 1)
            pool.memset(cnR[:, MC - 1, :], 0.0).then_inc(pads_set, 1)
            for t in (ctH[0], ctL[0]):
                pool.memset(t[:, :, M:724].bitcast(F32), 0.0).then_inc(pads_set, 1)

            def inverse_deviation(i, h):
                pool.wait_ge(stats_ready, i + 1)
                if i >= 1:
                    pool.wait_ge(rstd_ready, i)
                pool.tensor_scalar(veps[:, :], mv[:, HB * h:HB * (h + 1), 1], EPS, None,
                                   ALU.add).then_inc(pool_step, 1)
                pool.wait_ge(pool_step, i + 3)
                pool.tensor_tensor(rstd[:, HB * h:HB * (h + 1)], veps[:, :], nhalf[:, :],
                                   ALU.pow).then_inc(rstd_ready, 1)

            for i in range(4):
                inverse_deviation(i, i % 2)
            pool.wait_ge(gemm_done, gemm_count(U_CK, 0, KC - 1))
            pool.wait_ge(c_row, 1)
            for t in (ctH[1], ctL[1]):
                pool.memset(t[:, :, M:724].bitcast(F32), 0.0).then_inc(pads_set, 1)
            pool.memset(prob[0][:, M:MC * P], 0.0).then_inc(pads_set, 1)
            pool.wait_ge(gemm_done, gemm_count(U_CK, 1, KC - 1))
            pool.memset(prob[1][:, M:MC * P], 0.0).then_inc(pads_set, 1)
            for i in range(4, 6):
                inverse_deviation(i, i % 2)
            pool.wait_ge(xres_loaded, 16)
            pool.wait_ge(gb_loaded, 32)
            for b in range(B):
                pool.tensor_tensor(tok[:, b, :], tok[:, b, :], be3b[0:T, :], ALU.add).then_inc(xres_ready, 1)
            for i in range(6, 10):
                inverse_deviation(i, (i - 6) // 2)

        @block.tensor
        def _(pe):
            def unit(n, h, groups=range(KC)):
                at = POS[n, h]
                mh, ml = operand[n]
                for e in groups:
                    pn, ph = ORDER[at - 1]
                    if n == U_V and h == 0:
                        pe.wait_ge(s_att_low, e + 1)
                    elif n == U_O and h == 0:
                        pe.wait_ge(s_att_low, KC + e + 1)
                    elif (n, h) == (U_CV, 0) and e >= 2:
                        pe.wait_ge(dve_evac, dve_count(n, h, e - 2))
                    elif (n, h) == (U_CV, 1):
                        if e < 2:
                            pe.wait_ge(dve_evac, dve_count(U_CV, 0, e + 2))
                        elif e == 2:
                            pe.wait_ge(c_att_sb, B)
                        else:
                            pe.wait_ge(c_attT_low, B)
                    elif at >= 1:
                        if frees_on_act(pn):
                            pe.wait_ge(act_evac, act_count(pn, ph, e))
                        else:
                            pe.wait_ge(dve_evac, dve_count(pn, ph, e))
                    dst = ps[:, bank(n, h, e), 0:HALF]
                    for k in range(KC):
                        if e == 0:
                            wait_operand(pe, n, h, k)
                        if e == 0 and h == 0:
                            pe.wait_ge(w_low, KC * n + k + 1)
                        wh = WH[SLOT[n]][:, k, e * P:(e + 1) * P]
                        wl = WL[SLOT[n]][:, k, e * P:(e + 1) * P]
                        pe.matmul(dst, wh, half(mh, h, k), start=(k == 0), stop=False)
                        pe.matmul(dst, wh, half(ml, h, k), start=False, stop=False)
                        mm = pe.matmul(dst, wl, half(mh, h, k), start=False, stop=(k == KC - 1))
                    mm.then_inc(gemm_done, 1)

            def to_features(i, h, tiles):
                pe.wait_ge(tok_ready, 8 * i + HB * (h + 1))
                if i == 0 and h == 1:
                    pe.wait_ge(x_ready, KC)
                for k in range(KC):
                    for j in range(HB):
                        mm = pe.transpose(ps[:, 4 + k, j * T:(j + 1) * T], tiles[:, j, k * P:(k + 1) * P],
                                          ident[0:T, 0:T])
                    mm.then_inc(to_feat, 1)

            def to_tokens(i, h, n, src):
                pe.wait_ge(dve_evac, dve_count(n, h, KC - 1))
                for j in range(HB):
                    if i == 2 and h == 0:
                        pe.wait_ge(*((c_exp, B) if j < 2 else (c_probT_low, B)))
                    elif i == 4 and h == 1:
                        pe.wait_ge(out_ready, j + 1)
                    elif h == 1:
                        pe.wait_ge(x_ready, 8 * i + j + 1)
                    else:
                        pe.wait_ge(x_ready, 8 * min(i, 4))
                    for k in range(KC):
                        mm = pe.transpose(ps[0:T, 4 + j, k * P:(k + 1) * P], src[h][:, k, j * T:(j + 1) * T],
                                          ident[:, :])
                    mm.then_inc(to_tok, 1)

            def self_scores(h):
                pe.wait_ge(act_evac, act_count(U_K, h, KC - 1))
                pe.wait_ge(x_ready, 2 * KC)
                for j in range(HB):
                    cols = slice(j * T, (j + 1) * T)
                    for k in range(KC):
                        mm = pe.matmul(ps[0:T, 4 + h, cols], qT[h][:, k, cols], kT[h][:, k, cols],
                                       start=(k == 0), stop=(k == KC - 1))
                mm.then_inc(s_scores, 1)

            def self_prob_transpose(h):
                pe.wait_ge(s_norm, h + 1)
                for j in range(HB):
                    mm = pe.transpose(ps[0:T, 6 + h, j * T:(j + 1) * T], sprob[h][:, j, :], ident[0:T, 0:T])
                mm.then_inc(s_probT, 1)

            def self_attend(h):
                pe.wait_ge(s_probT_sb, h + 1)
                for k in range(KC):
                    if h == 0:
                        pe.wait_ge(act_evac, act_count(U_K, 1, k))
                    else:
                        pe.wait_ge(dve_evac, dve_count(U_V, 0, k))
                    for j in range(HB):
                        mm = pe.matmul(ps[:, k, j * T:(j + 1) * T], tok[:, HB * h + j, k * P:(k + 1) * P],
                                       sprobT[h][:, j, :], start=True, stop=True)
                    mm.then_inc(s_att, 1)

            def key_bias_rows(h):
                pe.wait_ge(dve_evac, dve_count(U_CQ, h, KC - 1))
                pe.wait_ge(small_low, 1)
                pe.wait_ge(x_ready, 16)
                for k in range(KC):
                    pe.matmul(ps[0:2, 6 + h, 0:HALF], bkS[:, k, :], half(QH, h, k), start=(k == 0), stop=False)
                    mm = pe.matmul(ps[0:2, 6 + h, 0:HALF], bkS[:, k, :], half(QL, h, k), start=False,
                                   stop=(k == KC - 1))
                mm.then_inc(c_row, 1)

            def key_bias_columns():
                pe.wait_ge(c_row_sb, 2)
                for b in range(B):
                    mm = pe.matmul(ps[0:T, 6, b:b + 1], crow[:, b * T:(b + 1) * T], ones2[:, :],
                                   start=True, stop=True)
                mm.then_inc(c_col, 1)

            def cross_scores(b):
                if b % HB == 0:
                    pe.wait_ge(dve_evac, dve_count(U_CK, b // HB, KC - 1))
                if b == 0:
                    pe.wait_ge(x_ready, 16)
                if b >= 1:
                    pe.wait_ge(c_exp, b)
                pe.wait_ge(pads_set, 3 if b == 0 else 5)
                qh, ql = tokens(AH, b), tokens(AL, b)
                for k in range(KC):
                    pe.wait_ge(ct_low, 2 * b + k // 2 + 1)
                    for i in range(2):
                        ch = ctH[b % 2][:, k, i * MH:i * MH + MW]
                        cl = ctL[b % 2][:, k, i * MH:i * MH + MW]
                        dst = ps[0:T, 4 + i, 0:MW]
                        pe.matmul(dst, qh[:, k, :], ch, start=(k == 0), stop=False)
                        pe.matmul(dst, qh[:, k, :], cl, start=False, stop=False)
                        mm = pe.matmul(dst, ql[:, k, :], ch, start=False, stop=(k == KC - 1))
                mm.then_inc(c_scores, 1)

            def cross_prob_transpose(b):
                pe.wait_ge(c_exp, b + 1)
                pe.wait_ge(pads_set, 6 if b == 0 else 7)
                if b == 0:
                    pe.wait_ge(c_col_sb, 1)
                if b >= 1:
                    pe.wait_ge(c_probT_low, b)
                for c in range(MC):
                    mm = pe.transpose(ps[:, 6 + c // 3, (c % 3) * T:(c % 3 + 1) * T],
                                      prob[b % 2][:, c * P:(c + 1) * P], ident[0:T, 0:T])
                mm.then_inc(c_probT, 1)

            def cross_attend(b):
                pe.wait_ge(c_probT_low, b + 1)
                if b == 0:
                    pe.wait_ge(dve_evac, dve_count(U_CK, 1, 2))
                else:
                    pe.wait_ge(c_att_sb, b)
                for c in range(MC):
                    pe.wait_ge(cn_low, 3 * b + c // 2 + 1)
                    ph, pl = ptH[b % 2][:, c * T:(c + 1) * T], ptL[b % 2][:, c * T:(c + 1) * T]
                    pe.matmul(ps[0:T, 2, :], ph, cnH[:, c, :], start=(c == 0), stop=False)
                    pe.matmul(ps[0:T, 2, :], ph, cnL[:, c, :], start=False, stop=False)
                    pe.matmul(ps[0:T, 2, :], pl, cnH[:, c, :], start=False,
                              stop=(c == MC - 1)).then_inc(c_chunk, 1)

            def cross_attend_transpose(b):
                pe.wait_ge(c_att_sb, b + 1)
                if b == 0:
                    pe.wait_ge(dve_evac, dve_count(U_CK, 1, 3))
                else:
                    pe.wait_ge(c_attT_low, b)
                for k in range(KC):
                    mm = pe.transpose(ps[:, 3, k * T:(k + 1) * T], utok[:, b % 2, k * P:(k + 1) * P],
                                      ident[0:T, 0:T])
                mm.then_inc(c_attT, 1)

            def gate_rows(h):
                pe.wait_ge(x_ready, 32)
                for k in range(KC):
                    pe.matmul(ps[0:2 * NE, 4 + h, 0:HALF], wgS[:, k, :], half(XH, h, k), start=(k == 0), stop=False)
                    mm = pe.matmul(ps[0:2 * NE, 4 + h, 0:HALF], wgS[:, k, :], half(XL, h, k), start=False,
                                   stop=(k == KC - 1))
                mm.then_inc(g_rows, 1)

            def gate_columns():
                pe.wait_ge(g_rows_sb, 2)
                for b in range(B):
                    mm = pe.matmul(ps[0:T, 6, b * NE:(b + 1) * NE], glog[:, b * T:(b + 1) * T], fold[:, :],
                                   start=True, stop=True)
                mm.then_inc(g_cols, 1)

            tiles = [tok[:, 0:HB, :], tok[:, HB:B, :]]
            tiles2 = [tok2[:, 0:HB, :], tok2[:, HB:B, :]]

            pe.wait_ge(pool_init, 1)
            to_features(0, 0, tiles[0])
            unit(U_Q, 0)
            to_features(0, 1, tiles[1])
            unit(U_K, 0)
            unit(U_Q, 1)
            self_scores(0)
            unit(U_K, 1)
            self_prob_transpose(0)
            self_scores(1)
            self_attend(0)
            unit(U_V, 0, [0, 1, 2])
            self_prob_transpose(1)
            unit(U_V, 0, [3])
            self_attend(1)
            unit(U_O, 0)
            unit(U_V, 1)
            to_tokens(1, 0, U_O, XS)
            unit(U_O, 1, [0, 1, 2])
            to_features(1, 0, tiles[0])
            unit(U_O, 1, [3])
            unit(U_CQ, 0, [0])
            to_tokens(1, 1, U_O, XS)
            unit(U_CQ, 0, [1, 2, 3])
            to_features(1, 1, tiles[1])
            unit(U_CK, 0)
            unit(U_CQ, 1)
            key_bias_rows(0)
            unit(U_CK, 1, [0])
            key_bias_rows(1)
            cross_scores(0)
            unit(U_CK, 1, [1])
            key_bias_columns()
            unit(U_CK, 1, [2, 3])
            cross_prob_transpose(0)
            cross_scores(1)
            for b in range(B):
                cross_attend(b)
                if b + 1 < B:
                    cross_prob_transpose(b + 1)
                if b + 2 < B:
                    cross_scores(b + 2)
                else:
                    unit(U_CV, 0, [[0, 1], [2, 3]][b + 2 - B])
                cross_attend_transpose(b)
            to_tokens(2, 0, U_CV, XS)
            unit(U_CV, 1)
            to_features(2, 0, xn[0])
            unit(U_F, 0, [0])
            to_tokens(2, 1, U_CV, XS)
            unit(U_F, 0, [1, 2, 3])
            unit(U_F + 1, 0, [0, 1, 2])
            to_features(2, 1, xn[1])
            unit(U_F + 1, 0, [3])
            for n, h in ORDER[POS[U_F, 1]:POS[U_M - 3, 1]]:
                unit(n, h)
            unit(U_M - 3, 1, [0])
            to_tokens(3, 0, U_M - 1, acc)
            unit(U_M - 3, 1, [1, 2, 3])
            unit(U_M - 2, 1)
            unit(U_M - 1, 1, [0, 1])
            to_features(3, 0, tiles2[0])
            unit(U_M - 1, 1, [2, 3])
            unit(U_M, 0, [0])
            to_tokens(3, 1, U_M - 1, acc)
            unit(U_M, 0, [1, 2, 3])
            unit(U_M + 1, 0)
            unit(U_M + 2, 0, [0, 1, 2])
            to_features(3, 1, tiles2[1])
            unit(U_M + 2, 0, [3])
            unit(U_M, 1)
            gate_rows(0)
            gate_rows(1)
            unit(U_M + 1, 1)
            gate_columns()
            unit(U_M + 2, 1)
            for n, h in ORDER[POS[U_M + 3, 0]:POS[NU - 1, 1]]:
                unit(n, h)
            unit(NU - 1, 1, [0])
            to_tokens(4, 0, NU - 1, acc)
            unit(NU - 1, 1, [1, 2, 3])
            to_tokens(4, 1, NU - 1, acc)

        @block.scalar
        def _(act):
            def split_weights(n, k):
                if n == 0 and k == 0:
                    act.wait_ge(w0_loaded, 16)
                elif k == 0 or (n == 0 and k == 2):
                    act.wait_ge(weights_loaded, 16 * (n + 1))
                if k == 0 and BEFORE[n] is not None:
                    m, h = ORDER[LAST[BEFORE[n]]]
                    act.wait_ge(gemm_done, gemm_count(m, h, KC - 1))
                elif k == 0 and SLOT[n] == 2:
                    act.wait_ge(ct_low, 2 * B)
                    act.wait_ge(cn_low, 3 * B)
                act.activation(WH[SLOT[n]][:, k, :], WR[:, k, :], ACT.Copy).then_inc(w_high, 1)

            def split_ct(b, i):
                act.wait_ge(ct_loaded[i], 16 * (b + 1))
                if b == 1:
                    act.wait_ge(gemm_done, gemm_count(U_CK, 0, KC - 1))
                    act.wait_ge(c_row, 1)
                if b >= 2:
                    act.wait_ge(c_scores, b - 1)
                act.activation(ctH[b % 2][:, 2 * i:2 * i + 2, 0:M], ctR[:, 2 * i:2 * i + 2, :],
                               ACT.Copy).then_inc(ct_high, 1)

            def split_cn(b, i):
                act.wait_ge(cn_loaded[i], (16 if i < 2 else 32) * (b + 1))
                if b >= 1:
                    act.wait_ge(c_chunk, MC * (b - 1) + 2 * i + 2)
                act.activation(cnH[:, 2 * i:2 * i + 2, :], cnR[:, 2 * i:2 * i + 2, :],
                               ACT.Copy).then_inc(cn_high, 1)

            def unit(n, h, groups=range(KC)):
                for e in groups:
                    src = ps[:, bank(n, h, e), 0:HALF]
                    kind = KINDS[n]
                    if act_writes(n):
                        act.wait_ge(gemm_done, gemm_count(n, h, e))
                    if kind == "fp32":
                        dst, col = (qT, C_BQ) if n == U_Q else (kT, C_BK)
                        act.activation(half(dst, h, e), src, ACT.Identity,
                                       bias=cst[:, col + e:col + e + 1]).then_inc(act_evac, 1)
                    elif kind == "split":
                        dst, col = (AH, C_BV) if n == U_V else (QH, C_CBQ)
                        act.activation(half(dst, h, e), src, ACT.Identity,
                                       bias=cst[:, col + e:col + e + 1]).then_inc(act_evac, 1)
                    elif kind == "split_nobias":
                        act.activation(half(AH, h, e), src, ACT.Copy).then_inc(act_evac, 1)
                    elif kind == "relu_bias":
                        col = C_B1 + KC * ((n - U_F) // 2) + e
                        act.activation(half(AT, h, e), src, ACT.Relu, bias=cst[:, col:col + 1])
                        act.activation(half(AH, h, e), src, ACT.Relu,
                                       bias=cst[:, col:col + 1]).then_inc(act_evac, 1)
                    elif kind == "relu":
                        act.activation(half(AH, h, e), src, ACT.Relu).then_inc(act_evac, 1)
                    if POS[n, h] in SPLIT_AT:
                        for k in [[0, 1], [2], [3], []][e]:
                            split_weights(SPLIT_AT[POS[n, h]], k)

            def normalise(i, h, dst):
                act.wait_ge(nmr_ready, 2 * (i - 1) + h + 1)
                for j in range(HB // 2, HB):
                    b = HB * h + j
                    src = tok[:, b, :] if i == 3 else ps[0:T, 4 + j, :]
                    act.activation(dst[:, j, :], src, ACT.Identity, bias=nmr[:, b:b + 1],
                                   scale=rstd[:, b:b + 1]).then_inc(tok_ready, 1)

            def norm_features(i, h):
                for k in range(KC):
                    act.wait_ge(to_feat, 8 * i + KC * h + (KC if i == 2 else k + 1))
                    src = ps[:, 4 + k, 0:HALF]
                    if i in (0, 3):
                        act.activation(half(XH, h, k), src, ACT.Copy).then_inc(x_high, 1)
                        continue
                    gc, bc = (C_G1, C_E1) if i == 1 else (C_G2, C_E2)
                    gain, shift = cst[:, gc + k:gc + k + 1], cst[:, bc + k:bc + k + 1]
                    act.activation(half(XT, h, k), src, ACT.Identity, bias=shift, scale=gain)
                    act.activation(half(XH, h, k), src, ACT.Identity, bias=shift,
                                   scale=gain).then_inc(x_high, 1)

            def self_exp(h):
                act.wait_ge(s_max, h + 1)
                for j in range(HB):
                    b = HB * h + j
                    ex = act.activation(sprob[h][:, j, :], ps[0:T, 4 + h, j * T:(j + 1) * T], ACT.Exp,
                                        bias=snb[:, b:b + 1], scale=SCALE, accum_out=ssum[:, b:b + 1])
                ex.then_inc(s_exp, 1)

            def self_probT(h):
                act.wait_ge(s_probT, h + 1)
                act.activation(sprobT[h][:, :, :].rearrange("p a b -> p (a b)"), ps[0:T, 6 + h, 0:HALF],
                               ACT.Copy).then_inc(s_probT_sb, 1)

            def self_attended(h):
                for k in range(KC):
                    act.wait_ge(s_att, KC * h + k + 1)
                    act.activation(half(QH, h, k), ps[:, k, 0:HALF], ACT.Copy).then_inc(s_att_high, 1)

            def key_bias_rows(h):
                act.wait_ge(c_row, h + 1)
                act.activation(crow[:, h * HALF:(h + 1) * HALF], ps[0:2, 6 + h, 0:HALF],
                               ACT.Copy).then_inc(c_row_sb, 1)

            def cross_exp(b):
                act.wait_ge(c_max, b + 1)
                if b == 1:
                    act.wait_ge(gemm_done, gemm_count(U_CK, 1, KC - 1))
                if b >= 2:
                    act.wait_ge(c_probT, b - 1)
                act.activation(prob[b % 2][:, 0:M].rearrange("p (i m) -> p i m", i=2), ps[0:T, 4:6, 0:MH],
                               ACT.Exp, bias=snb[:, b:b + 1], scale=SCALE,
                               accum_out=ssum[:, b:b + 1]).then_inc(c_exp, 1)

            def cross_probT(b):
                act.wait_ge(c_probT, b + 1)
                if b >= 2:
                    act.wait_ge(c_chunk, MC * (b - 1))
                act.activation(ptH[b % 2][:, :].rearrange("p (i m) -> p i m", i=2), ps[:, 6:8, 0:3 * T],
                               ACT.Copy).then_inc(c_probT_high, 1)

            def cross_attended(b):
                act.wait_ge(c_chunk, MC * (b + 1))
                act.wait_ge(c_rec, b + 1)
                if b >= 2:
                    act.wait_ge(c_attT, b - 1)
                act.activation(utok[:, b % 2, :], ps[0:T, 2, :], ACT.Copy,
                               scale=srec[:, b:b + 1]).then_inc(c_att_sb, 1)

            def cross_attendedT(b):
                act.wait_ge(c_attT, b + 1)
                act.activation(tokens(AH, b), ps[:, 3, 0:KC * T].rearrange("p (k t) -> p k t", k=KC),
                               ACT.Copy).then_inc(c_attT_high, 1)

            tiles = [tok[:, 0:HB, :], tok[:, HB:B, :]]
            tiles2 = [tok2[:, 0:HB, :], tok2[:, HB:B, :]]

            act.wait_ge(consts_loaded, 16)
            act.activation(bkS[:, :, 0], cst[:, C_CBK:C_CBK + KC], ACT.Copy)
            act.activation(wgS[:, :, 0:NE], cst[:, C_WG:C_ALL].rearrange("p (k e) -> p k e", k=KC),
                           ACT.Copy).then_inc(small_high, 1)
            for k in range(KC):
                split_weights(0, k)
            norm_features(0, 0)
            unit(U_Q, 0)
            norm_features(0, 1)
            unit(U_K, 0)
            split_ct(0, 0)
            unit(U_Q, 1)
            self_exp(0)
            split_ct(0, 1)
            unit(U_K, 1)
            self_probT(0)
            self_exp(1)
            self_attended(0)
            unit(U_V, 0, [0, 1, 2])
            self_probT(1)
            unit(U_V, 0, [3])
            self_attended(1)
            unit(U_O, 0)
            unit(U_V, 1, [0])
            split_cn(0, 0)
            unit(U_V, 1, [1])
            split_cn(0, 1)
            unit(U_V, 1, [2])
            split_cn(0, 2)
            unit(U_V, 1, [3])
            unit(U_O, 1, [0, 1])
            normalise(1, 0, tiles[0])
            unit(U_O, 1, [2])
            norm_features(1, 0)
            unit(U_O, 1, [3])
            unit(U_CQ, 0, [0, 1, 2])
            normalise(1, 1, tiles[1])
            unit(U_CQ, 0, [3])
            norm_features(1, 1)
            unit(U_CK, 0)
            unit(U_CQ, 1)
            unit(U_CK, 1, [0])
            key_bias_rows(0)
            key_bias_rows(1)
            split_ct(1, 0)
            unit(U_CK, 1, [1])
            split_ct(1, 1)
            cross_exp(0)
            unit(U_CK, 1, [2, 3])
            cross_probT(0)
            split_ct(2, 0)
            cross_exp(1)
            split_ct(2, 1)
            for b in range(B):
                if b + 1 < B:
                    split_cn(b + 1, 0)
                cross_attended(b)
                if b + 1 < B:
                    cross_probT(b + 1)
                    split_cn(b + 1, 1)
                    split_cn(b + 1, 2)
                if b + 3 < B:
                    split_ct(b + 3, 0)
                if b + 2 >= B:
                    unit(U_CV, 0, [[0, 1], [2, 3]][b + 2 - B])
                if b + 2 < B:
                    cross_exp(b + 2)
                cross_attendedT(b)
                if b + 3 < B:
                    split_ct(b + 3, 1)
            unit(U_CV, 1, [0, 1])
            normalise(2, 0, xn[0])
            unit(U_CV, 1, [2, 3])
            norm_features(2, 0)
            unit(U_F, 0, [0, 1, 2])
            normalise(2, 1, xn[1])
            unit(U_F, 0, [3])
            unit(U_F + 1, 0, [0, 1, 2])
            norm_features(2, 1)
            unit(U_F + 1, 0, [3])
            for n, h in ORDER[POS[U_F, 1]:POS[U_M - 1, 1]]:
                unit(n, h)
            normalise(3, 0, tiles2[0])
            unit(U_M - 1, 1, [0, 1])
            norm_features(3, 0)
            unit(U_M - 1, 1, [2, 3])
            unit(U_M, 0)
            unit(U_M + 1, 0)
            normalise(3, 1, tiles2[1])
            unit(U_M + 2, 0, [0, 1, 2])
            norm_features(3, 1)
            unit(U_M + 2, 0, [3])
            unit(U_M, 1)
            for h in range(2):
                act.wait_ge(g_rows, h + 1)
                act.activation(glog[:, h * HALF:(h + 1) * HALF], ps[0:2 * NE, 4 + h, 0:HALF],
                               ACT.Copy).then_inc(g_rows_sb, 1)
            unit(U_M + 1, 1)
            unit(U_M + 2, 1)
            act.wait_ge(g_shift, 2)
            act.activation(gexp[:, :, :], gexp[:, :, :], ACT.Exp)
            act.activation(gsm[:, 0, :], gsm[:, 0, :], ACT.Exp).then_inc(g_exp, 1)
            for n, h in ORDER[POS[U_M + 3, 0]:]:
                unit(n, h)

        @block.vector
        def _(dve):
            steps = [0]

            def settle(ins):
                steps[0] += 1
                ins.then_inc(dve_step, 1)
                dve.wait_ge(dve_step, steps[0])

            def split_weights(n, k):
                dve.wait_ge(w_high, KC * n + k + 1)
                dve.tensor_tensor(WL[SLOT[n]][:, k, :], WR[:, k, :], raw(WH[SLOT[n]][:, k, :]),
                                  ALU.subtract).then_inc(w_low, 1)

            def split_ct(b, i):
                dve.wait_ge(ct_high, 2 * b + i + 1)
                dve.tensor_tensor(ctL[b % 2][:, 2 * i:2 * i + 2, 0:M], ctR[:, 2 * i:2 * i + 2, :],
                                  raw(ctH[b % 2][:, 2 * i:2 * i + 2, 0:M]), ALU.subtract).then_inc(ct_low, 1)

            def split_cn(b, i):
                dve.wait_ge(cn_high, 3 * b + i + 1)
                dve.tensor_tensor(cnL[:, 2 * i:2 * i + 2, :], cnR[:, 2 * i:2 * i + 2, :],
                                  raw(cnH[:, 2 * i:2 * i + 2, :]), ALU.subtract).then_inc(cn_low, 1)

            def unit(n, h, groups=range(KC)):
                for e in groups:
                    src = ps[:, bank(n, h, e), 0:HALF]
                    kind = KINDS[n]
                    if act_writes(n) and dve_writes(n):
                        dve.wait_ge(act_evac, act_count(n, h, e))
                    elif dve_writes(n):
                        dve.wait_ge(gemm_done, gemm_count(n, h, e))
                    if kind == "split":
                        dh, dl, col = (AH, AL, C_BV) if n == U_V else (QH, QL, C_CBQ)
                        dve.scalar_tensor_tensor(out=half(dl, h, e), in0=src, scalar=cst[:, col + e:col + e + 1],
                                                 in1=raw(half(dh, h, e)), op0=ALU.add,
                                                 op1=ALU.subtract).then_inc(dve_evac, 1)
                    elif kind == "split_nobias":
                        dve.tensor_tensor(half(AL, h, e), src, raw(half(AH, h, e)),
                                          ALU.subtract).then_inc(dve_evac, 1)
                    elif kind == "relu_bias":
                        dve.tensor_tensor(half(AL, h, e), half(AT, h, e), raw(half(AH, h, e)),
                                          ALU.subtract).then_inc(dve_evac, 1)
                    elif kind == "relu":
                        dve.scalar_tensor_tensor(out=half(AL, h, e), in0=src, scalar=0.0, in1=raw(half(AH, h, e)),
                                                 op0=ALU.max, op1=ALU.subtract).then_inc(dve_evac, 1)
                    elif kind in ("residual", "down_residual"):
                        col = {U_O: C_BO, U_CV: C_CBV}.get(n, C_B2)
                        dst = XS if kind == "residual" else acc
                        settle(dve.scalar_tensor_tensor(out=half(dst, h, e), in0=src,
                                                        scalar=cst[:, col + e:col + e + 1],
                                                        in1=raw(half(XH, h, e)), op0=ALU.add, op1=ALU.add))
                        dve.tensor_tensor(half(dst, h, e), half(dst, h, e), raw(half(XL, h, e)),
                                          ALU.add).then_inc(dve_evac, 1)
                    elif kind == "down_first":
                        dve.tensor_copy(half(acc, h, e), src).then_inc(dve_evac, 1)
                    elif kind == "down_add":
                        dve.wait_ge(dve_evac, dve_count(n - 2, h, e))
                        dve.tensor_tensor(half(acc, h, e), src, half(acc, h, e), ALU.add).then_inc(dve_evac, 1)
                    if POS[n, h] in SPLIT_AT:
                        for k in [[0, 1], [2], [3], []][e]:
                            split_weights(SPLIT_AT[POS[n, h]], k)

            def statistics(h, before):
                for j in range(HB):
                    b = HB * h + j
                    if before is None:
                        if j % 2 == 0:
                            dve.wait_ge(x_loaded[b // 2], 16)
                        st = dve.bn_stats(bnst[:, b, :], tok[:, b, :])
                    else:
                        dve.wait_ge(to_tok, before + j + 1)
                        st = dve.bn_stats(bnst[:, b, :], ps[0:T, 4 + j, :])
                settle(st)
                for j in range(HB):
                    ag = dve.bn_aggr(mv[:, HB * h + j, :], bnst[:, HB * h + j, :])
                ag.then_inc(stats_ready, 1)

            def normalise(i, h, dst):
                dve.wait_ge(rstd_ready, {0: h, 1: 2 + h, 2: 4 + h, 3: 7 + 2 * h}[i] + 1)
                if i:
                    cols = slice(HB * h, HB * (h + 1))
                    dve.scalar_tensor_tensor(out=nmr[:, cols], in0=mv[:, cols, 0], scalar=-1.0, in1=rstd[:, cols],
                                             op0=ALU.mult, op1=ALU.mult).then_inc(nmr_ready, 1)
                for j in range(HB // 2 if i else HB):
                    b = HB * h + j
                    src = tok[:, b, :] if i in (0, 3) else ps[0:T, 4 + j, :]
                    dve.tensor_scalar(dst[:, j, :], src, mv[:, b, 0:1], rstd[:, b:b + 1], ALU.subtract,
                                      ALU.mult).then_inc(tok_ready, 1)

            def norm_features(i, h, chunks=range(KC)):
                for k in chunks:
                    dve.wait_ge(x_high, 8 * i + KC * h + k + 1)
                    src = ps[:, 4 + k, 0:HALF] if i in (0, 3) else half(XT, h, k)
                    dve.tensor_tensor(half(XL, h, k), src, raw(half(XH, h, k)), ALU.subtract).then_inc(x_ready, 1)

            def self_max(h):
                dve.wait_ge(s_scores, h + 1)
                settle(dve.tensor_reduce(smx[:, HB * h:HB * (h + 1)],
                                         ps[0:T, 4 + h, 0:HALF].rearrange("p (j s) -> p j s", j=HB), AX.X, ALU.max))
                dve.tensor_scalar(snb[:, HB * h:HB * (h + 1)], smx[:, HB * h:HB * (h + 1)], -SCALE, None,
                                  ALU.mult).then_inc(s_max, 1)

            def self_normalise(h):
                dve.wait_ge(s_exp, h + 1)
                settle(dve.reciprocal(srec[:, HB * h:HB * (h + 1)], ssum[:, HB * h:HB * (h + 1)]))
                for j in range(HB):
                    b = HB * h + j
                    nm = dve.tensor_scalar(sprob[h][:, j, :], sprob[h][:, j, :], srec[:, b:b + 1], None, ALU.mult)
                nm.then_inc(s_norm, 1)

            def self_attended(h):
                for k in range(KC):
                    dve.wait_ge(s_att_high, KC * h + k + 1)
                    dve.tensor_tensor(half(QL, h, k), ps[:, k, 0:HALF], raw(half(QH, h, k)),
                                      ALU.subtract).then_inc(s_att_low, 1)

            def cross_max(b):
                dve.wait_ge(c_scores, b + 1)
                settle(dve.tensor_reduce(smx[:, b:b + 1], ps[0:T, 4:6, 0:MH], AX.XY, ALU.max))
                settle(dve.tensor_scalar(smx[:, b:b + 1], smx[:, b:b + 1], cshift[:, b:b + 1], -SCALE, ALU.add,
                                         ALU.mult))
                dve.scalar_tensor_tensor(out=snb[:, b:b + 1], in0=cshift[:, b:b + 1], scalar=SCALE,
                                         in1=smx[:, b:b + 1], op0=ALU.mult, op1=ALU.add).then_inc(c_max, 1)

            def cross_probT(b):
                dve.wait_ge(c_probT_high, b + 1)
                dve.tensor_tensor(ptL[b % 2][:, :].rearrange("p (i m) -> p i m", i=2), ps[:, 6:8, 0:3 * T],
                                  raw(ptH[b % 2][:, :].rearrange("p (i m) -> p i m", i=2)),
                                  ALU.subtract).then_inc(c_probT_low, 1)

            def cross_recip(b):
                dve.wait_ge(c_exp, b + 1)
                dve.reciprocal(srec[:, b:b + 1], ssum[:, b:b + 1]).then_inc(c_rec, 1)

            def cross_attendedT(b):
                dve.wait_ge(c_attT_high, b + 1)
                dve.tensor_tensor(tokens(AL, b), ps[:, 3, 0:KC * T].rearrange("p (k t) -> p k t", k=KC),
                                  raw(tokens(AH, b)), ALU.subtract).then_inc(c_attT_low, 1)

            def last_scale(h):
                dve.wait_ge(stats_ready, 7 + 2 * h)
                dve.wait_ge(gb_loaded, 32)
                for j in range(HB):
                    b = HB * h + j
                    z = dve.scalar_tensor_tensor(out=tok2[:, b, :], in0=ps[0:T, 4 + j, :], scalar=mv[:, b, 0:1],
                                                 in1=g3b[0:T, :], op0=ALU.subtract, op1=ALU.mult)
                settle(z)

            def last_residual(h):
                dve.wait_ge(rstd_ready, 6 + 2 * h + 1)
                dve.wait_ge(xres_ready, HB * (h + 1))
                for j in range(HB):
                    b = HB * h + j
                    z = dve.scalar_tensor_tensor(out=tok[:, b, :], in0=tok2[:, b, :], scalar=rstd[:, b:b + 1],
                                                 in1=tok[:, b, :], op0=ALU.mult, op1=ALU.add)
                settle(z)

            def gate_top():
                dve.wait_ge(g_cols, 1)
                settle(dve.tensor_copy(gl[:, :, :], ps[0:T, 6, 0:B * NE].rearrange("p (b e) -> p b e", b=B)))
                for b in range(B):
                    tp = dve.max(gtop[:, b, :], gl[:, b, :])
                settle(tp)
                dve.tensor_tensor(gexp[:, :, :], gl[:, :, :], gtop[:, :, 0:1].to_broadcast([T, B, NE]),
                                  ALU.subtract).then_inc(g_shift, 1)
                dve.tensor_tensor(gsm[:, 0, :], gtop[:, :, 1], gtop[:, :, 0], ALU.subtract).then_inc(g_shift, 1)

            def gate_weights():
                dve.wait_ge(g_exp, 1)
                settle(dve.tensor_reduce(gsm[:, 1, :], gexp[:, :, :], AX.X, ALU.add))
                settle(dve.reciprocal(gsm[:, 2, :], gsm[:, 1, :]))
                settle(dve.tensor_tensor(gsm[:, 3, :], gsm[:, 0, :], gsm[:, 2, :], ALU.mult))
                settle(dve.tensor_tensor(gsm[:, 4, :], gsm[:, 2, :], gsm[:, 3, :], ALU.add))
                settle(dve.tensor_scalar(gsm[:, 4, :], gsm[:, 4, :], F32_EPS, None, ALU.max))
                settle(dve.reciprocal(gsm[:, 5, :], gsm[:, 4, :]))
                settle(dve.tensor_tensor(gsm[:, 2, :], gsm[:, 2, :], gsm[:, 5, :], ALU.mult))
                settle(dve.tensor_tensor(gsm[:, 3, :], gsm[:, 3, :], gsm[:, 5, :], ALU.mult))
                dve.tensor_tensor(gsm[:, 6, :], gsm[:, 2, :], gsm[:, 3, :], ALU.add).then_inc(g_weight, 1)

            def finish(h):
                dve.wait_ge(g_weight, 1)
                for j in range(HB):
                    b = HB * h + j
                    dve.wait_ge(to_tok, 24 + b + 1)
                    dve.scalar_tensor_tensor(out=outb[:, b, :], in0=ps[0:T, 4 + j, :], scalar=gsm[:, 6, b:b + 1],
                                             in1=tok[:, b, :], op0=ALU.mult, op1=ALU.add).then_inc(out_ready, 1)

            tiles = [tok[:, 0:HB, :], tok[:, HB:B, :]]
            tiles2 = [tok2[:, 0:HB, :], tok2[:, HB:B, :]]

            statistics(0, None)
            split_weights(0, 0)
            normalise(0, 0, tiles[0])
            for k in range(KC):
                if k:
                    split_weights(0, k)
                norm_features(0, 0, [k])
            statistics(1, None)
            normalise(0, 1, tiles[1])
            unit(U_Q, 0)
            norm_features(0, 1)
            dve.wait_ge(small_high, 1)
            dve.tensor_tensor(bkS[:, :, 1], cst[:, C_CBK:C_CBK + KC], raw(bkS[:, :, 0]), ALU.subtract)
            dve.tensor_tensor(wgS[:, :, NE:2 * NE], cst[:, C_WG:C_ALL].rearrange("p (k e) -> p k e", k=KC),
                              raw(wgS[:, :, 0:NE]), ALU.subtract).then_inc(small_low, 1)
            unit(U_K, 0)
            split_ct(0, 0)
            unit(U_Q, 1)
            self_max(0)
            self_normalise(0)
            split_ct(0, 1)
            unit(U_K, 1)
            self_max(1)
            self_attended(0)
            self_normalise(1)
            unit(U_V, 0)
            self_attended(1)
            unit(U_O, 0)
            unit(U_V, 1, [0])
            split_cn(0, 0)
            unit(U_V, 1, [1])
            split_cn(0, 1)
            unit(U_V, 1, [2])
            split_cn(0, 2)
            unit(U_V, 1, [3])
            statistics(0, 0)
            unit(U_O, 1, [0])
            normalise(1, 0, tiles[0])
            unit(U_O, 1, [1, 2])
            norm_features(1, 0)
            unit(U_O, 1, [3])
            unit(U_CQ, 0, [0])
            statistics(1, HB)
            unit(U_CQ, 0, [1])
            normalise(1, 1, tiles[1])
            unit(U_CQ, 0, [2, 3])
            norm_features(1, 1)
            unit(U_CK, 0)
            unit(U_CQ, 1)
            unit(U_CK, 1, [0])
            split_ct(1, 0)
            unit(U_CK, 1, [1])
            dve.wait_ge(c_col, 1)
            dve.tensor_copy(cshift[:, :], ps[0:T, 6, 0:B]).then_inc(c_col_sb, 1)
            dve.wait_ge(c_col_sb, 1)
            cross_max(0)
            split_ct(1, 1)
            unit(U_CK, 1, [2, 3])
            cross_recip(0)
            cross_probT(0)
            split_ct(2, 0)
            cross_max(1)
            split_ct(2, 1)
            for b in range(B):
                if b + 1 < B:
                    split_cn(b + 1, 0)
                    cross_recip(b + 1)
                    cross_probT(b + 1)
                    split_cn(b + 1, 1)
                    split_cn(b + 1, 2)
                if b + 3 < B:
                    split_ct(b + 3, 0)
                if b + 2 < B:
                    cross_max(b + 2)
                else:
                    unit(U_CV, 0, [[0, 1], [2, 3]][b + 2 - B])
                cross_attendedT(b)
                if b + 3 < B:
                    split_ct(b + 3, 1)
            statistics(0, 8)
            unit(U_CV, 1, [0])
            normalise(2, 0, xn[0])
            unit(U_CV, 1, [1, 2, 3])
            norm_features(2, 0)
            unit(U_F, 0, [0])
            statistics(1, 8 + HB)
            unit(U_F, 0, [1])
            normalise(2, 1, xn[1])
            unit(U_F, 0, [2, 3])
            unit(U_F + 1, 0, [0, 1, 2])
            norm_features(2, 1)
            unit(U_F + 1, 0, [3])
            for n, h in ORDER[POS[U_F, 1]:POS[U_M - 3, 1]]:
                unit(n, h)
            unit(U_M - 3, 1, [0])
            statistics(0, 16)
            unit(U_M - 3, 1, [1])
            last_scale(0)
            unit(U_M - 3, 1, [2])
            last_residual(0)
            unit(U_M - 3, 1, [3])
            unit(U_M - 2, 1, [0])
            statistics(0, None)
            unit(U_M - 2, 1, [1, 2])
            normalise(3, 0, tiles2[0])
            unit(U_M - 2, 1, [3])
            unit(U_M - 1, 1, [0, 1])
            norm_features(3, 0)
            unit(U_M - 1, 1, [2, 3])
            unit(U_M, 0, [0])
            statistics(1, 16 + HB)
            unit(U_M, 0, [1])
            last_scale(1)
            unit(U_M, 0, [2])
            last_residual(1)
            unit(U_M, 0, [3])
            unit(U_M + 1, 0, [0])
            statistics(1, None)
            unit(U_M + 1, 0, [1, 2])
            normalise(3, 1, tiles2[1])
            unit(U_M + 1, 0, [3])
            unit(U_M + 2, 0, [0, 1, 2])
            norm_features(3, 1)
            unit(U_M + 2, 0, [3])
            unit(U_M, 1)
            unit(U_M + 1, 1)
            gate_top()
            unit(U_M + 2, 1)
            gate_weights()
            for n, h in ORDER[POS[U_M + 3, 0]:POS[NU - 1, 1]]:
                unit(n, h)
            unit(NU - 1, 1, [0])
            finish(0)
            unit(NU - 1, 1, [1, 2, 3])
            finish(1)


def _chunks(np, v):
    return np.asarray(v).reshape(-1, P).T


def kernel(**inputs):
    import numpy as np
    import concourse.bacc as bacc
    from concourse import mybir as mb
    from concourse.bass_utils import run_bass_kernel_spmd as run

    a = {k: np.asarray(v) for k, v in inputs.items()}
    x, mem = a["x"], a["ctx_1024"]
    ipw, ipb = a["L0_xattn_in_proj_w"], a["L0_xattn_in_proj_b"]

    def block(w):
        return w.reshape(KC, P, D).transpose(1, 0, 2)

    units = [ipw[0:D].T, ipw[D:2 * D].T, ipw[2 * D:3 * D].T, a["L0_xattn_out_proj_w"].T,
             a["L0_xattn_wq"].T, a["L0_xattn_wk"], a["L0_xattn_wv"].T]
    for up, down in ((a["L0_xattn_w1"].T, a["L0_xattn_w2"].T), (a["L0_ffn_w1"], a["L0_ffn_w2"])):
        for j in range(NF):
            units += [up[:, j * D:(j + 1) * D], down[j * D:(j + 1) * D, :]]
    wts = np.ascontiguousarray(np.stack([block(u) for u in units]))
    vectors = [ipb[0:D], ipb[D:2 * D], ipb[2 * D:3 * D], a["L0_xattn_out_proj_b"], a["L0_xattn_bq"],
               a["L0_xattn_bk"], a["L0_xattn_bv"], a["L0_xattn_b1"], a["L0_xattn_b2"], a["L0_xattn_g1"],
               a["L0_xattn_be1"], a["L0_xattn_g2"], a["L0_xattn_be2"]]
    gate = a["L0_ffn_Wg"].reshape(KC, P, NE).transpose(1, 0, 2).reshape(P, KC * NE)
    consts = np.ascontiguousarray(np.concatenate([_chunks(np, v) for v in vectors] + [gate], axis=1))
    arrays = {
        "x_in": np.ascontiguousarray(x),
        "ctxt_in": np.ascontiguousarray(mem.transpose(0, 2, 1)),
        "ctxn_in": np.ascontiguousarray(mem),
        "wts_in": wts,
        "consts_in": consts,
        "g3_in": np.ascontiguousarray(a["L0_xattn_g3"]),
        "be3_in": np.ascontiguousarray(a["L0_xattn_be3"]),
    }
    nc = bacc.Bacc("TRN2", target_bir_lowering=False, num_devices=1)
    args = [nc.dram_tensor(n, v.shape, mb.dt.from_np(v.dtype), kind="ExternalInput").ap() for n, v in arrays.items()]
    args.append(nc.dram_tensor("out", (B, T, D), F32, kind="ExternalOutput").ap())
    build(nc, *args)
    r = run(nc, [arrays], core_ids=[0])
    return r.results[0]["out"]
```

```python
from contextlib import ExitStack

import concourse.bass as bass
from concourse import mybir

F32 = mybir.dt.float32
F32R = mybir.dt.float32r
ALU = mybir.AluOpType
ACT = mybir.ActivationFunctionType
AX = mybir.AxisListType

P = 128
B, T, D = 8, 100, 512
M = 722
FF = 2048
NE = 8
N = B * T
HALF = N // 2
HB = B // 2
KC = D // P
MC = (M + P - 1) // P
MH = M // 2
MW = MH + 1
ML = M - (MC - 1) * P
NF = FF // D
EPS = 1e-5
F32_EPS = 1.1920928955078125e-07
SCALE = 1.0 / float(D) ** 0.5
WARM_UP = 11


U_Q, U_K, U_VO, S_CQ, S_CK, U_A, U_CV = range(7)
U_F = 7
U_M = U_F + 2 * NF
NU = U_M + 2 * NF
LOADED = [n for n in range(NU) if n not in (U_VO, U_A)]
KINDS = (["fp32", "fp32", "residual", None, None, "split", "residual"]
         + ["relu_bias", "down_residual"] + ["relu_bias", "down_add"] * (NF - 1)
         + ["relu", "down_first"] + ["relu", "down_add"] * (NF - 1))


ORDER = ([(U_Q, 0), (U_K, 0), (U_Q, 1), (U_K, 1), (U_VO, 0), (U_VO, 1)]
         + [(U_A, 0), (U_A, 1), (U_CV, 0), (U_CV, 1)])
for _first in (U_F, U_M):
    _up, _down = [[_first + 2 * j + i for j in range(NF)] for i in range(2)]
    if _first == U_F:
        ORDER += [(_up[0], 0), (_down[0], 0), (_up[0], 1), (_down[0], 1),
                  (_up[1], 0), (_up[1], 1), (_down[1], 0), (_down[1], 1),
                  (_up[2], 0), (_up[2], 1), (_down[2], 0), (_up[3], 0), (_down[3], 0),
                  (_down[2], 1), (_up[3], 1), (_down[3], 1)]
    else:
        ORDER += [(_up[0], 0), (_down[0], 0), (_up[1], 0), (_up[0], 1), (_down[0], 1), (_up[1], 1),
                  (_down[1], 0), (_down[1], 1)]
        for _j in range(2, NF):
            ORDER += [(_up[_j], 0), (_up[_j], 1), (_down[_j], 0), (_down[_j], 1)]
POS = {nh: i for i, nh in enumerate(ORDER)}
LAST = {n: max(POS[n, 0], POS[n, 1]) for n in range(NU) if (n, 0) in POS}
SLOT = [{U_Q: 0, U_K: 1, U_VO: 3, S_CQ: 0, S_CK: 1, U_A: 0, U_CV: 1, U_F: 0, U_F + 1: 1}.get(
        n, [2, 0, 1][(n - U_F - 2) % 3]) for n in range(NU)]
BEFORE = {n: max((m for m in LAST if m < n and SLOT[m] == SLOT[n]), default=None) for n in range(NU)}
SPLIT_AT = {LAST[BEFORE[n]] + 1: n for n in LOADED[2:] if BEFORE[n] is not None and n not in (U_CV, U_F)}
SPLIT_AT.update({0: U_K, POS[U_A, 0]: U_CV, POS[U_F + 1, 0]: U_F + 2})
assert len(SPLIT_AT) == len(LOADED) - 2
assert all(POS[n, 0] > at for at, n in SPLIT_AT.items() if n in LAST)
POOL_UNITS = (U_Q, S_CQ, S_CK, U_CV, U_F, U_F + 1, U_F + 2, U_M, U_M + 1, U_M + 2)

C_BQ, C_BK, C_BV, C_BO, C_CBQ, C_CBK, C_CBV, C_B1 = 0, 4, 8, 12, 16, 20, 24, 28
C_B2, C_G1, C_E1, C_G2, C_E2, C_WG = 44, 48, 52, 56, 60, 64
C_ALL = C_WG + KC * NE


def act_writes(n):
    return KINDS[n] in ("fp32", "split", "relu_bias", "relu")


def dve_writes(n):
    return KINDS[n] != "fp32"


def gemm_count(n, h, e):
    return KC * POS[n, h] + e + 1


def act_count(n, h, e):
    return KC * sum(act_writes(m) for m, _ in ORDER[:POS[n, h]]) + e + 1


def dve_count(n, h, e):
    return KC * sum(dve_writes(m) for m, _ in ORDER[:POS[n, h]]) + e + 1


def frees_on_act(n):
    return KINDS[n] in ("fp32", "relu_bias")


def build(nc, x, ctxt, ctxn, wvo, wts, consts, g3, be3, out):
    with ExitStack() as ctx:
        def sem(name):
            return ctx.enter_context(nc.semaphore(name))

        base = 16512
        at = {}
        for name, size in (("X", 2 * KC * N * 4), ("R1", 2 * KC * N * 4), ("R2", 29696), ("R3", B * D * 4),
                           ("R4", 2 * KC * 724 * 4), ("R5", 2 * MC * D * 4), ("R6", KC * M * 4 + MC * D * 4),
                           ("W", 5 * KC * D * 4), ("C", 2976)):
            at[name] = base
            base += (size + 31) // 32 * 32

        def sb(name, region, offset, shape, dt=F32):
            return nc.alloc_sbuf_tensor_at(name, shape, dt, offset=at[region] + offset)

        HS = KC * HALF * 4

        def halves(name, region, dt=F32R, start=0, step=2 * HS):
            return [sb(name + str(h), region, start + step * h, [P, KC, HALF], dt) for h in range(2)]

        XH = halves("XH", "X")
        XL = halves("XL", "X", start=HS)
        XS = halves("XS", "X", F32)
        XT = halves("XT", "X", F32, HS)
        xn = [sb("xn%d" % h, "X", 2 * HS * h, [T, HB, D]) for h in range(2)]
        qT = halves("qT", "R1", F32)
        kT = halves("kT", "R1", F32, HS)
        AH = halves("AH", "R1")
        AL = halves("AL", "R1", start=HS)
        AT = halves("AT", "R1", F32, HS)
        QH = halves("QH", "R2")
        QL = halves("QL", "R2", start=HS)
        acc = halves("acc", "R2", F32, step=HS)
        tok = sb("tok", "R3", 0, [T, B, D])
        CTS = KC * 724 * 4
        ctH = [sb("ctH0", "R4", 0, [P, KC, 724], F32R), sb("ctH1", "R2", 0, [P, KC, 724], F32R)]
        ctL = [sb("ctL0", "R4", CTS, [P, KC, 724], F32R), sb("ctL1", "R3", 0, [P, KC, 724], F32R)]
        cnH = sb("cnH", "R5", 0, [P, MC, D], F32R)
        cnL = sb("cnL", "R5", MC * D * 4, [P, MC, D], F32R)
        prob = [sb("prob0", "R2", 4 * HS, [T, MC * P]), sb("prob1", "R2", 2 * HS, [T, MC * P])]
        ptH = [sb("ptH0", "R3", CTS, [P, MC * T], F32R), sb("ptH1", "R2", 2 * HS + 3072, [P, MC * T], F32R)]
        ptL = [sb("ptL0", "R3", CTS + 2400, [P, MC * T], F32R), sb("ptL1", "R2", 2 * HS + 5472, [P, MC * T], F32R)]
        utok = sb("utok", "R2", 2 * HS + 7872, [T, 2, D])
        crow = sb("crow", "R3", CTS, [2, N])
        sprob = [sb("sprob%d" % h, "R5", 1600 * h, [T, HB, T]) for h in range(2)]
        sprobT = [sb("sprobT%d" % h, "R5", 3200 + 1600 * h, [T, HB, T]) for h in range(2)]
        tok2 = sb("tok2", "R4", 0, [T, B, D])
        g3b = sb("g3b", "R5", 0, [P, D])
        be3b = sb("be3b", "R5", 2048, [P, D])
        glog = sb("glog", "R5", 4096, [2 * NE, N])
        outb = sb("outb", "R5", 8192, [T, B, D])
        ctR = sb("ctR", "R6", 0, [P, KC, M])
        cnR = sb("cnR", "R6", KC * M * 4, [P, MC, D])
        wat = [("W", 0), ("W", 16384), ("R6", 0), ("R5", 8192)]
        WH = [sb("WH%d" % i, r, o, [P, KC, D], F32R) for i, (r, o) in enumerate(wat)]
        WL = [sb("WL%d" % i, r, o + 8192, [P, KC, D], F32R) for i, (r, o) in enumerate(wat)]
        WR = sb("WR", "W", 32768, [P, KC, D])
        VH, VL = [sb(name, "R4", o, [P, KC, D], F32R) for name, o in (("VH", 0), ("VL", 8192))]
        OH, OL = [sb(name, "R1", o, [P, KC, D], F32R) for name, o in (("OH", 0), ("OL", 8192))]
        VR, OR = [sb(name, "R2", o, [P, KC, D]) for name, o in (("VR", 0), ("OR", 8192))]
        off = [0]

        def small(name, shape, dt=F32):
            size = 4
            for s in shape[1:]:
                size *= s
            t = sb(name, "C", off[0], shape, dt)
            off[0] += (size + 31) // 32 * 32
            return t

        ident = small("ident", [P, P])
        cst = small("cst", [P, C_ALL])
        u_o = sb("u_o", "R2", 16384, [P, D])
        u_q = sb("u_q", "R2", 25600, [P, D])
        u_k = sb("u_k", "R2", 27648, [P, D])
        keyS = small("keyS", [P, KC, 2], F32R)
        gv = small("gv", [P, 2 * KC])
        qk = small("qk", [P, KC])
        qks = small("qks", [P, 2])
        qk2 = small("qk2", [2, 1])
        ones1 = small("ones1", [P, 1])
        wgS = small("wgS", [P, KC, 2 * NE], F32R)
        vob = small("vob", [P, KC])
        ones2 = small("ones2", [2, 1])
        fold = small("fold", [2 * NE, NE])
        bnst = small("bnst", [T, B, 6])
        mv = small("mv", [T, B, 2])
        veps = small("veps", [T, HB])
        rstd = small("rstd", [T, B])
        nmr = small("nmr", [T, B])
        nhalf = small("nhalf", [T, HB])
        smx = small("smx", [T, B])
        snb = small("snb", [T, B])
        ssum = small("ssum", [T, B])
        srec = small("srec", [T, B])
        cshift = small("cshift", [T, B])
        gl, gtop, gexp = [sb(name, "R5", o, [T, B, NE]) for name, o in (("gl", 7296), ("gtop", 7552), ("gexp", 7808))]
        gsm = small("gsm", [T, 8, B])
        assert off[0] <= 2976, off[0]

        ps = ctx.enter_context(nc.psum_tensor("ps", [P, 8, 512], F32))

        x_loaded = [sem("x_loaded%d" % i) for i in range(4)]
        vo_loaded = [sem("vo_loaded%d" % k) for k in range(KC)]
        w0_loaded = sem("w0_loaded")
        consts_loaded = sem("consts_loaded")
        weights_loaded = sem("weights_loaded")
        ct_loaded = [sem("ct_loaded0"), sem("ct_loaded1")]
        cn_loaded = [sem("cn_loaded0"), sem("cn_loaded1"), sem("cn_loaded2")]
        xres_loaded = sem("xres_loaded")
        gb_loaded = sem("gb_loaded")
        stored = sem("stored")
        pool_init = sem("pool_init")
        pads_set = sem("pads_set")
        pool_step = sem("pool_step")
        rstd_ready = sem("rstd_ready")
        xres_ready = sem("xres_ready")
        w_high = sem("w_high")
        w_low = sem("w_low")
        w_low_pool = sem("w_low_pool")
        v_high, v_low = sem("v_high"), sem("v_low")
        o_high, o_low = sem("o_high"), sem("o_low")
        o_low_pool = sem("o_low_pool")
        vo_made = sem("vo_made")
        vo_high, vo_low = sem("vo_high"), sem("vo_low")
        vo_bias, vob_ready = sem("vo_bias"), sem("vob_ready")
        ct_high, ct_low = sem("ct_high"), sem("ct_low")
        cn_high, cn_low = sem("cn_high"), sem("cn_low")
        cn_low_pool = sem("cn_low_pool")
        small_high, small_low = sem("small_high"), sem("small_low")
        gemm_done = sem("gemm_done")
        act_evac, dve_evac = sem("act_evac"), sem("dve_evac")
        dve_step = sem("dve_step")
        stats_ready = sem("stats_ready")
        nmr_ready = sem("nmr_ready")
        tok_ready = sem("tok_ready")
        to_tok = sem("to_tok")
        to_feat = sem("to_feat")
        x_affine = sem("x_affine")
        x_high, x_ready = sem("x_high"), sem("x_ready")
        s_scores, s_max, s_exp, s_norm = sem("s_scores"), sem("s_max"), sem("s_exp"), sem("s_norm")
        s_probT, s_probT_sb = sem("s_probT"), sem("s_probT_sb")
        s_att, s_att_high, s_att_low = sem("s_att"), sem("s_att_high"), sem("s_att_low")
        qk_made = sem("qk_made")
        qk_high, qk_low = sem("qk_high"), sem("qk_low")
        u_o_ready, u_q_ready, u_k_ready = sem("u_o_ready"), sem("u_q_ready"), sem("u_k_ready")
        qks_ready = sem("qks_ready")
        gv_made, gv_ready = sem("gv_made"), sem("gv_ready")
        key_high, key_low = sem("key_high"), sem("key_low")
        c_row, c_row_sb, c_col, c_col_sb = sem("c_row"), sem("c_row_sb"), sem("c_col"), sem("c_col_sb")
        c_scores, c_max, c_exp, c_rec = sem("c_scores"), sem("c_max"), sem("c_exp"), sem("c_rec")
        c_probT, c_probT_high, c_probT_low = sem("c_probT"), sem("c_probT_high"), sem("c_probT_low")
        c_chunk = sem("c_chunk")
        c_att_sb = sem("c_att_sb")
        c_attT, c_attT_high, c_attT_low = sem("c_attT"), sem("c_attT_high"), sem("c_attT_low")
        g_rows, g_rows_sb, g_cols, g_shift = sem("g_rows"), sem("g_rows_sb"), sem("g_cols"), sem("g_shift")
        g_exp, g_weight = sem("g_exp"), sem("g_weight")
        out_ready = sem("out_ready")

        def half(t, h, k):
            return t[h][:, k, :]

        def tokens(t, b):
            return t[b // HB][:, :, b % HB * T:(b % HB + 1) * T]

        def wait_w_low(eng, n, k):
            if n == U_VO:
                eng.wait_ge(vo_low, k + 1)
                return
            if n == U_A:
                eng.wait_ge(qk_low, k + 1)
                return
            here = n in POOL_UNITS
            before = sum((m in POOL_UNITS) == here for m in LOADED[:LOADED.index(n)])
            eng.wait_ge(w_low_pool if here else w_low, KC * before + k + 1)

        def wait_cn_low(eng, b, i):
            if b >= 1 and i == 2:
                eng.wait_ge(cn_low_pool, b)
            else:
                eng.wait_ge(cn_low, i + 1 if b == 0 else 3 + 2 * (b - 1) + i + 1)

        def bank(n, h, e):
            return e % 2 if (n, h) == (U_CV, 0) else e

        def raw(ap):
            return ap.bitcast(F32)

        operand = {}
        for n in range(NU):
            operand[n] = (XH, XL)
        operand[U_VO] = (QH, QL)
        operand[U_CV] = (AH, AL)
        for j in range(NF):
            operand[U_F + 2 * j + 1] = operand[U_M + 2 * j + 1] = (AH, AL)

        def wait_operand(eng, n, h, k):
            if n in (U_Q, U_K):
                eng.wait_ge(x_ready, KC * h + k + 1)
            elif n == U_VO:
                eng.wait_ge(s_att_low, KC * h + k + 1)
            elif n == U_A:
                eng.wait_ge(x_ready, 8 + KC * h + k + 1)
            elif n == U_CV:
                eng.wait_ge(c_attT_low, HB * (h + 1))
            elif n >= U_F and (n - U_F) % 2:
                eng.wait_ge(dve_evac, dve_count(n - 1, h, k))
            elif n < U_M:
                eng.wait_ge(x_ready, 16 + KC * h + k + 1)
            else:
                eng.wait_ge(x_ready, 24 + KC * h + k + 1)

        block = ctx.enter_context(nc.Block())

        @block.sync
        def _(sp):
            def load_x(i):
                sp.dma_start(tok[:, 2 * i:2 * i + 2, :], x[2 * i:2 * i + 2].rearrange("b t d -> t b d")
                             ).then_inc(x_loaded[i], 16)

            def load_vo(k):
                sp.dma_start(VR[:, k, :], wvo[0, :, k, :]).then_inc(vo_loaded[k], 16)
                sp.dma_start(OR[:, k, :], wvo[1, :, k, :]).then_inc(vo_loaded[k], 16)

            load_vo(0)
            load_vo(1)
            load_x(0)
            load_x(1)
            sp.dma_start(cst[:, :], consts).then_inc(consts_loaded, 16)
            load_vo(2)
            load_vo(3)
            sp.dma_start(WR[:, 0:2, :], wts[0, :, 0:2, :]).then_inc(w0_loaded, 16)
            sp.dma_start(WR[:, 2:KC, :], wts[0, :, 2:KC, :]).then_inc(weights_loaded, 16)
            load_x(2)
            load_x(3)

            def load_weights(n):
                i = LOADED.index(n)
                wait_w_low(sp, LOADED[i - 1], KC - 1)
                if n == S_CK:
                    sp.wait_ge(u_q_ready, 1)
                elif n == U_CV:
                    sp.wait_ge(u_k_ready, 1)
                sp.dma_start(WR[:, :, :], wts[i]).then_inc(weights_loaded, 16)

            def load_ct(b):
                for i in range(2):
                    if b >= 1:
                        sp.wait_ge(ct_low, 2 * (b - 1) + i + 1)
                    sp.dma_start(ctR[:, 2 * i:2 * i + 2, :],
                                 ctxt[b, 2 * P * i:2 * P * (i + 1), :].rearrange("(k p) m -> p k m", p=P)
                                 ).then_inc(ct_loaded[i], 16)

            def load_cn(b):
                for i in range(3):
                    if b >= 1:
                        wait_cn_low(sp, b - 1, i)
                    if b == 0 and i == 2:
                        sp.wait_ge(pads_set, 1)
                    full = 2 if i < 2 else 1
                    sp.dma_start(cnR[:, 2 * i:2 * i + full, :],
                                 ctxn[b, 2 * P * i:2 * P * i + full * P, :].rearrange("(c p) d -> p c d", p=P)
                                 ).then_inc(cn_loaded[i], 16)
                    if i == 2:
                        sp.dma_start(cnR[0:ML, MC - 1, :], ctxn[b, (MC - 1) * P:M, :]).then_inc(cn_loaded[i], 16)

            load_ct(0)
            load_weights(U_K)
            load_cn(0)
            load_weights(S_CQ)
            load_ct(1)
            load_weights(S_CK)
            load_weights(U_CV)
            load_cn(1)
            load_ct(2)
            load_weights(U_F)
            load_ct(3)
            for b in range(B):
                if b + 2 < B:
                    load_cn(b + 2)
                if b + 4 < B:
                    load_ct(b + 4)
            sp.wait_ge(c_attT, B)
            sp.dma_start(tok[:, :, :], x.rearrange("b t d -> t b d")).then_inc(xres_loaded, 16)
            sp.dma_start(g3b[:, :], g3.partition_broadcast(P)).then_inc(gb_loaded, 16)
            sp.dma_start(be3b[:, :], be3.partition_broadcast(P)).then_inc(gb_loaded, 16)
            for n in range(U_F + 1, NU):
                load_weights(n)
            for b in range(HB):
                sp.wait_ge(out_ready, b + 1)
                sp.dma_start(out[b], outb[:, b, :]).then_inc(stored, 16)
            last = (KC - 1) * P
            for i, (a, c) in enumerate(((0, last), (last, D))):
                for b in range(HB, B, 2):
                    sp.wait_ge(out_ready, HB * i + b + 2)
                    sp.dma_start(out[b:b + 2, :, a:c].rearrange("b t d -> t b d"),
                                 outb[:, b:b + 2, a:c]).then_inc(stored, 16)
            sp.wait_ge(stored, 16 * B)

        @block.gpsimd
        def _(pool):
            pool.memset(ident[:, :], 0.0).then_inc(pool_step, 1)
            pool.wait_ge(pool_step, 1)
            pool.affine_select(out=ident[:, :], in_=ident[:, :], compare_op=ALU.not_equal, fill=1.0, base=0,
                               pattern=[[-1, P]], channel_multiplier=1).then_inc(pool_step, 1)
            pool.memset(nhalf[:, :], -0.5)
            pool.memset(ones2[:, :], 1.0)
            pool.memset(ones1[:, :], 1.0)
            pool.memset(qks[:, 1:2], 0.0)
            pool.wait_ge(pool_step, 2)
            pool.tensor_tensor(fold[:, :], ident[0:2 * NE, 0:NE], ident[0:2 * NE, NE:2 * NE],
                               ALU.add).then_inc(pool_init, 1)
            pool.memset(cnR[:, MC - 1, :], 0.0).then_inc(pads_set, 1)
            def inverse_deviation(i, h):
                pool.wait_ge(stats_ready, i + 1)
                if i >= 1:
                    pool.wait_ge(rstd_ready, i)
                pool.tensor_scalar(veps[:, :], mv[:, HB * h:HB * (h + 1), 1], EPS, None,
                                   ALU.add).then_inc(pool_step, 1)
                pool.wait_ge(pool_step, i + 3)
                pool.tensor_tensor(rstd[:, HB * h:HB * (h + 1)], veps[:, :], nhalf[:, :],
                                   ALU.pow).then_inc(rstd_ready, 1)

            def split_weights(n, chunks=range(KC)):
                for k in chunks:
                    pool.wait_ge(w_high, KC * LOADED.index(n) + k + 1)
                    pool.tensor_tensor(WL[SLOT[n]][:, k, :], WR[:, k, :], raw(WH[SLOT[n]][:, k, :]),
                                       ALU.subtract).then_inc(w_low_pool, 1)

            def split_cn(b, i):
                pool.wait_ge(cn_high, 3 * b + i + 1)
                pool.tensor_tensor(cnL[:, 2 * i:2 * i + 2, :], cnR[:, 2 * i:2 * i + 2, :],
                                   raw(cnH[:, 2 * i:2 * i + 2, :]), ALU.subtract).then_inc(cn_low_pool, 1)

            def split_o(k):
                pool.wait_ge(o_high, k + 1)
                pool.tensor_tensor(OL[:, k, :], OR[:, k, :], raw(OH[:, k, :]), ALU.subtract).then_inc(o_low_pool, 1)

            split_o(2)
            inverse_deviation(0, 0)
            split_o(3)
            split_weights(U_Q)
            inverse_deviation(1, 1)
            pool.wait_ge(vo_made, KC)
            for t in (ctH[0], ctL[0]):
                pool.memset(t[:, :, M:724].bitcast(F32), 0.0).then_inc(pads_set, 1)
            split_weights(S_CQ)
            split_weights(S_CK)
            inverse_deviation(2, 0)
            inverse_deviation(3, 1)
            pool.wait_ge(to_feat, 16)
            for t in (ctH[1], ctL[1]):
                pool.memset(t[:, :, M:724].bitcast(F32), 0.0).then_inc(pads_set, 1)
            for t in prob:
                pool.memset(t[:, M:MC * P], 0.0).then_inc(pads_set, 1)
            split_weights(U_CV)
            for b in range(1, B):
                split_cn(b, 2)
            split_weights(U_F)
            inverse_deviation(4, 0)
            split_weights(U_F + 1, [0, 1])
            inverse_deviation(5, 1)
            split_weights(U_F + 1, [2, 3])
            split_weights(U_F + 2)
            pool.wait_ge(xres_loaded, 16)
            pool.wait_ge(gb_loaded, 32)
            for b in range(B):
                pool.tensor_tensor(tok[:, b, :], tok[:, b, :], be3b[0:T, :], ALU.add).then_inc(xres_ready, 1)
            inverse_deviation(6, 0)
            split_weights(U_M)
            inverse_deviation(7, 0)
            split_weights(U_M + 1)
            split_weights(U_M + 2)
            inverse_deviation(8, 1)
            inverse_deviation(9, 1)

        @block.tensor
        def _(pe):
            def unit(n, h, groups=range(KC)):
                at = POS[n, h]
                mh, ml = operand[n]
                for e in groups:
                    pn, ph = ORDER[at - 1]
                    if n == U_VO:
                        pe.wait_ge(s_att_low, KC * h + e + 1)
                    elif (n, h) == (U_CV, 0) and e >= 2:
                        pe.wait_ge(dve_evac, dve_count(n, h, e - 2))
                    elif (n, h) == (U_CV, 1):
                        if e < 2:
                            pe.wait_ge(dve_evac, dve_count(U_CV, 0, e + 2))
                        elif e == 2:
                            pe.wait_ge(c_att_sb, B)
                        else:
                            pe.wait_ge(c_attT_low, B)
                    elif at >= 1:
                        if frees_on_act(pn):
                            pe.wait_ge(act_evac, act_count(pn, ph, e))
                        else:
                            pe.wait_ge(dve_evac, dve_count(pn, ph, e))
                    dst = ps[:, bank(n, h, e), 0:HALF]
                    for k in range(KC):
                        if e == 0:
                            wait_operand(pe, n, h, k)
                        if e == 0 and h == 0:
                            wait_w_low(pe, n, k)
                        wh = WH[SLOT[n]][:, k, e * P:(e + 1) * P]
                        wl = WL[SLOT[n]][:, k, e * P:(e + 1) * P]
                        pe.matmul(dst, wh, half(mh, h, k), start=(k == 0), stop=False)
                        pe.matmul(dst, wh, half(ml, h, k), start=False, stop=False)
                        mm = pe.matmul(dst, wl, half(mh, h, k), start=False, stop=(k == KC - 1))
                    mm.then_inc(gemm_done, 1)

            def to_features(i, h, tiles):
                if i == 0 and h == 0:
                    for j in range(HB):
                        pe.wait_ge(tok_ready, j + 1)
                        for k in range(KC):
                            mm = pe.transpose(ps[:, k, j * T:(j + 1) * T], tiles[:, j, k * P:(k + 1) * P],
                                              ident[0:T, 0:T])
                            if j == HB - 1:
                                mm.then_inc(to_feat, 1)
                    return
                pe.wait_ge(tok_ready, 8 * i + HB * (h + 1))
                if i == 0 and h == 1:
                    pe.wait_ge(vo_low, KC)
                for k in range(KC):
                    for j in range(HB):
                        mm = pe.transpose(ps[:, 4 + k, j * T:(j + 1) * T], tiles[:, j, k * P:(k + 1) * P],
                                          ident[0:T, 0:T])
                    mm.then_inc(to_feat, 1)

            def to_tokens(i, h, n, src, chunks=range(KC)):
                for k in chunks:
                    pe.wait_ge(dve_evac, dve_count(n, h, k))
                    if (i, h, k) == (4, 1, KC - 1):
                        pe.wait_ge(out_ready, 2 * HB)
                    for j in range(HB):
                        if k:
                            pass
                        elif i == 2 and h == 0:
                            pe.wait_ge(*((c_exp, B) if j < 2 else (c_probT_low, B)))
                        elif i == 4 and h == 1:
                            pe.wait_ge(out_ready, j + 1)
                        elif h == 1:
                            pe.wait_ge(x_ready, 8 * i + j + 1)
                        else:
                            pe.wait_ge(x_ready, 8 * min(i, 4))
                        mm = pe.transpose(ps[0:T, 4 + j, k * P:(k + 1) * P], src[h][:, k, j * T:(j + 1) * T],
                                          ident[:, :])
                        if k == KC - 1 or (i, h, k) == (4, 1, KC - 2):
                            mm.then_inc(to_tok, 1)

            def self_scores(h):
                pe.wait_ge(act_evac, act_count(U_K, h, KC - 1))
                pe.wait_ge(x_ready, 2 * KC)
                for j in range(HB):
                    cols = slice(j * T, (j + 1) * T)
                    for k in range(KC):
                        mm = pe.matmul(ps[0:T, 4 + h, cols], qT[h][:, k, cols], kT[h][:, k, cols],
                                       start=(k == 0), stop=(k == KC - 1))
                mm.then_inc(s_scores, 1)

            def combine_weights(k):
                pe.wait_ge(v_low, k + 1)
                if k < 2:
                    pe.wait_ge(o_low, k + 1)
                else:
                    pe.wait_ge(o_low_pool, k - 1)
                for e in range(KC):
                    dst, cols = ps[:, 4 + e, :], slice(e * P, (e + 1) * P)
                    pe.matmul(dst, VH[:, k, cols], OH[:, k, :], start=(k == 0), stop=False)
                    pe.matmul(dst, VH[:, k, cols], OL[:, k, :], start=False, stop=False)
                    mm = pe.matmul(dst, VL[:, k, cols], OH[:, k, :], start=False, stop=(k == KC - 1))
                    if k == KC - 1:
                        mm.then_inc(vo_made, 1)

            def combine_bias():
                pe.wait_ge(x_ready, 2 * KC)
                pe.wait_ge(u_o_ready, 1)
                for e in range(KC):
                    mm = pe.matmul(ps[:, 7, e:e + 1], u_o[:, e * P:(e + 1) * P], ones1[:, :], start=True, stop=True)
                mm.then_inc(vo_bias, 1)

            def combine_cross(k):
                wait_w_low(pe, S_CQ, k)
                wait_w_low(pe, S_CK, k)
                qh, ql = WH[SLOT[S_CQ]], WL[SLOT[S_CQ]]
                kh, kl = WH[SLOT[S_CK]], WL[SLOT[S_CK]]
                for e in range(KC):
                    if k == 0:
                        pe.wait_ge(dve_evac, dve_count(U_VO, 1, e))
                    dst, cols = ps[:, e, :], slice(e * P, (e + 1) * P)
                    pe.matmul(dst, qh[:, k, cols], kh[:, k, :], start=(k == 0), stop=False)
                    pe.matmul(dst, qh[:, k, cols], kl[:, k, :], start=False, stop=False)
                    mm = pe.matmul(dst, ql[:, k, cols], kh[:, k, :], start=False, stop=(k == KC - 1))
                    if k == KC - 1:
                        mm.then_inc(qk_made, 1)

            def combine_cross_bias():
                pe.wait_ge(u_q_ready, 1)
                pe.wait_ge(qks_ready, 1)
                pe.wait_ge(u_k_ready, 1)
                for i, u in enumerate((u_k, u_q)):
                    for e in range(KC):
                        at = HALF + KC * i + e
                        pe.matmul(ps[:, 7, at:at + 1], u[:, e * P:(e + 1) * P], ones1[:, :], start=True, stop=True)
                at = HALF + 2 * KC
                pe.matmul(ps[0:2, 7, at:at + 1], qks[:, :], ones1[:, :], start=True, stop=True).then_inc(gv_made, 1)

            def self_prob_transpose(h):
                pe.wait_ge(s_norm, h + 1)
                if h == 1:
                    pe.wait_ge(vob_ready, 1)
                for j in range(HB):
                    mm = pe.transpose(ps[0:T, 6 + h, j * T:(j + 1) * T], sprob[h][:, j, :], ident[0:T, 0:T])
                mm.then_inc(s_probT, 1)

            def self_attend(h):
                pe.wait_ge(s_probT_sb, h + 1)
                for k in range(KC):
                    if h == 0:
                        pe.wait_ge(act_evac, act_count(U_K, 1, k))
                    else:
                        pe.wait_ge(dve_evac, dve_count(U_VO, 0, k))
                    for j in range(HB):
                        mm = pe.matmul(ps[:, k, j * T:(j + 1) * T], tok[:, HB * h + j, k * P:(k + 1) * P],
                                       sprobT[h][:, j, :], start=True, stop=True)
                    mm.then_inc(s_att, 1)

            def key_bias_rows(h):
                pe.wait_ge(key_low, 1)
                pe.wait_ge(x_ready, 16)
                for k in range(KC):
                    pe.matmul(ps[0:2, 6 + h, 0:HALF], keyS[:, k, :], half(XH, h, k), start=(k == 0), stop=False)
                    mm = pe.matmul(ps[0:2, 6 + h, 0:HALF], keyS[:, k, :], half(XL, h, k), start=False,
                                   stop=(k == KC - 1))
                mm.then_inc(c_row, 1)

            def key_bias_columns():
                pe.wait_ge(c_row_sb, 2)
                for b in range(B):
                    mm = pe.matmul(ps[0:T, 6, b:b + 1], crow[:, b * T:(b + 1) * T], ones2[:, :],
                                   start=True, stop=True)
                mm.then_inc(c_col, 1)

            def cross_scores(b):
                if b % HB == 0:
                    pe.wait_ge(dve_evac, dve_count(U_A, b // HB, KC - 1))
                if b == 0:
                    pe.wait_ge(x_ready, 16)
                if b >= 1:
                    pe.wait_ge(c_exp, b)
                pe.wait_ge(pads_set, 3 if b == 0 else 5)
                qh, ql = tokens(AH, b), tokens(AL, b)
                for k in range(KC):
                    pe.wait_ge(ct_low, 2 * b + k // 2 + 1)
                    for i in range(2):
                        ch = ctH[b % 2][:, k, i * MH:i * MH + MW]
                        cl = ctL[b % 2][:, k, i * MH:i * MH + MW]
                        dst = ps[0:T, 4 + i, 0:MW]
                        pe.matmul(dst, qh[:, k, :], ch, start=(k == 0), stop=False)
                        pe.matmul(dst, qh[:, k, :], cl, start=False, stop=False)
                        mm = pe.matmul(dst, ql[:, k, :], ch, start=False, stop=(k == KC - 1))
                mm.then_inc(c_scores, 1)

            def cross_prob_transpose(b):
                pe.wait_ge(c_exp, b + 1)
                pe.wait_ge(pads_set, 6 if b == 0 else 7)
                if b == 0:
                    pe.wait_ge(c_col_sb, 1)
                if b >= 1:
                    pe.wait_ge(c_probT_low, b)
                for c in range(MC):
                    mm = pe.transpose(ps[:, 6 + c // 3, (c % 3) * T:(c % 3 + 1) * T],
                                      prob[b % 2][:, c * P:(c + 1) * P], ident[0:T, 0:T])
                mm.then_inc(c_probT, 1)

            def cross_attend(b):
                pe.wait_ge(c_probT_low, b + 1)
                if b == 0:
                    pe.wait_ge(dve_evac, dve_count(U_A, 1, 2))
                else:
                    pe.wait_ge(c_att_sb, b)
                for c in range(MC):
                    wait_cn_low(pe, b, c // 2)
                    ph, pl = ptH[b % 2][:, c * T:(c + 1) * T], ptL[b % 2][:, c * T:(c + 1) * T]
                    pe.matmul(ps[0:T, 2, :], ph, cnH[:, c, :], start=(c == 0), stop=False)
                    pe.matmul(ps[0:T, 2, :], ph, cnL[:, c, :], start=False, stop=False)
                    pe.matmul(ps[0:T, 2, :], pl, cnH[:, c, :], start=False,
                              stop=(c == MC - 1)).then_inc(c_chunk, 1)

            def cross_attend_transpose(b):
                pe.wait_ge(c_att_sb, b + 1)
                if b == 0:
                    pe.wait_ge(dve_evac, dve_count(U_A, 1, 3))
                else:
                    pe.wait_ge(c_attT_low, b)
                for k in range(KC):
                    mm = pe.transpose(ps[:, 3, k * T:(k + 1) * T], utok[:, b % 2, k * P:(k + 1) * P],
                                      ident[0:T, 0:T])
                mm.then_inc(c_attT, 1)

            def gate_rows(h):
                pe.wait_ge(x_ready, 32)
                for k in range(KC):
                    pe.matmul(ps[0:2 * NE, 4 + h, 0:HALF], wgS[:, k, :], half(XH, h, k), start=(k == 0), stop=False)
                    mm = pe.matmul(ps[0:2 * NE, 4 + h, 0:HALF], wgS[:, k, :], half(XL, h, k), start=False,
                                   stop=(k == KC - 1))
                mm.then_inc(g_rows, 1)

            def gate_columns():
                pe.wait_ge(g_rows_sb, 2)
                for b in range(B):
                    mm = pe.matmul(ps[0:T, 6, b * NE:(b + 1) * NE], glog[:, b * T:(b + 1) * T], fold[:, :],
                                   start=True, stop=True)
                mm.then_inc(g_cols, 1)

            tiles = [tok[:, 0:HB, :], tok[:, HB:B, :]]
            tiles2 = [tok2[:, 0:HB, :], tok2[:, HB:B, :]]

            pe.wait_ge(pool_init, 1)
            for _ in range(WARM_UP):
                pe.matmul(ps[:, 3, 0:P], ident[:, :], ident[:, :], start=True, stop=True)
            combine_weights(0)
            combine_weights(1)
            combine_weights(2)
            to_features(0, 0, tiles[0])
            combine_weights(3)
            unit(U_Q, 0)
            to_features(0, 1, tiles[1])
            unit(U_K, 0)
            unit(U_Q, 1)
            self_scores(0)
            unit(U_K, 1)
            self_prob_transpose(0)
            combine_bias()
            self_scores(1)
            self_attend(0)
            unit(U_VO, 0, [0, 1, 2])
            self_prob_transpose(1)
            unit(U_VO, 0, [3])
            self_attend(1)
            to_tokens(1, 0, U_VO, XS)
            unit(U_VO, 1, [0, 1, 2])
            to_features(1, 0, tiles[0])
            combine_cross_bias()
            unit(U_VO, 1, [3])
            combine_cross(0)
            to_tokens(1, 1, U_VO, XS)
            combine_cross(1)
            combine_cross(2)
            combine_cross(3)
            to_features(1, 1, tiles[1])
            unit(U_A, 0)
            key_bias_rows(0)
            unit(U_A, 1, [0])
            key_bias_rows(1)
            cross_scores(0)
            unit(U_A, 1, [1])
            key_bias_columns()
            unit(U_A, 1, [2, 3])
            cross_prob_transpose(0)
            cross_scores(1)
            for b in range(B):
                cross_attend(b)
                if b + 1 < B:
                    cross_prob_transpose(b + 1)
                if b + 2 < B:
                    cross_scores(b + 2)
                else:
                    unit(U_CV, 0, [[0, 1], [2, 3]][b + 2 - B])
                cross_attend_transpose(b)
            to_tokens(2, 0, U_CV, XS)
            unit(U_CV, 1, [0, 1, 2])
            to_features(2, 0, xn[0])
            unit(U_CV, 1, [3])
            unit(U_F, 0, [0])
            to_tokens(2, 1, U_CV, XS)
            unit(U_F, 0, [1, 2, 3])
            unit(U_F + 1, 0, [0])
            to_features(2, 1, xn[1])
            unit(U_F + 1, 0, [1, 2, 3])
            for n, h in ORDER[POS[U_F, 1]:POS[U_M - 3, 1]]:
                unit(n, h)
            unit(U_M - 3, 1, [0])
            to_tokens(3, 0, U_M - 1, acc)
            unit(U_M - 3, 1, [1, 2, 3])
            unit(U_M - 2, 1)
            unit(U_M - 1, 1, [0, 1])
            to_features(3, 0, tiles2[0])
            unit(U_M - 1, 1, [2, 3])
            unit(U_M, 0, [0])
            to_tokens(3, 1, U_M - 1, acc)
            unit(U_M, 0, [1, 2, 3])
            unit(U_M + 1, 0)
            unit(U_M + 2, 0, [0, 1])
            to_features(3, 1, tiles2[1])
            unit(U_M + 2, 0, [2, 3])
            unit(U_M, 1)
            gate_rows(0)
            gate_rows(1)
            unit(U_M + 1, 1)
            gate_columns()
            unit(U_M + 2, 1)
            for n, h in ORDER[POS[U_M + 3, 0]:POS[NU - 1, 1]]:
                unit(n, h)
            unit(NU - 1, 1, [0])
            to_tokens(4, 0, NU - 1, acc)
            unit(NU - 1, 1, [1, 2])
            to_tokens(4, 1, NU - 1, acc, [0, 1, 2])
            unit(NU - 1, 1, [3])
            to_tokens(4, 1, NU - 1, acc, [3])

        @block.scalar
        def _(act):
            def split_weights(n, k):
                if n == 0 and k == 0:
                    act.wait_ge(w0_loaded, 16)
                elif k == 0 or (n == 0 and k == 2):
                    act.wait_ge(weights_loaded, 16 * (LOADED.index(n) + 1))
                if k == 0 and BEFORE[n] is not None:
                    m, h = ORDER[LAST[BEFORE[n]]]
                    act.wait_ge(gemm_done, gemm_count(m, h, KC - 1))
                elif k == 0 and SLOT[n] == 2:
                    act.wait_ge(ct_low, 2 * B)
                    for i in (1, 2):
                        wait_cn_low(act, B - 1, i)
                act.activation(WH[SLOT[n]][:, k, :], WR[:, k, :], ACT.Copy).then_inc(w_high, 1)

            def split_ct(b, i):
                act.wait_ge(ct_loaded[i], 16 * (b + 1))
                if b == 1:
                    act.wait_ge(to_feat, 16)
                if b >= 2:
                    act.wait_ge(c_scores, b - 1)
                act.activation(ctH[b % 2][:, 2 * i:2 * i + 2, 0:M], ctR[:, 2 * i:2 * i + 2, :],
                               ACT.Copy).then_inc(ct_high, 1)

            def split_cn(b, i):
                act.wait_ge(cn_loaded[i], (16 if i < 2 else 32) * (b + 1))
                if b >= 1:
                    act.wait_ge(c_chunk, MC * (b - 1) + 2 * i + 2)
                act.activation(cnH[:, 2 * i:2 * i + 2, :], cnR[:, 2 * i:2 * i + 2, :],
                               ACT.Copy).then_inc(cn_high, 1)

            def unit(n, h, groups=range(KC)):
                for e in groups:
                    src = ps[:, bank(n, h, e), 0:HALF]
                    kind = KINDS[n]
                    if act_writes(n):
                        act.wait_ge(gemm_done, gemm_count(n, h, e))
                    if kind == "fp32":
                        dst, col = (qT, C_BQ) if n == U_Q else (kT, C_BK)
                        act.activation(half(dst, h, e), src, ACT.Identity,
                                       bias=cst[:, col + e:col + e + 1]).then_inc(act_evac, 1)
                    elif kind == "split":
                        act.activation(half(AH, h, e), src, ACT.Identity, bias=gv[:, e:e + 1]).then_inc(act_evac, 1)
                    elif kind == "relu_bias":
                        col = C_B1 + KC * ((n - U_F) // 2) + e
                        act.activation(half(AT, h, e), src, ACT.Relu, bias=cst[:, col:col + 1])
                        act.activation(half(AH, h, e), src, ACT.Relu,
                                       bias=cst[:, col:col + 1]).then_inc(act_evac, 1)
                    elif kind == "relu":
                        act.activation(half(AH, h, e), src, ACT.Relu).then_inc(act_evac, 1)
                    if POS[n, h] in SPLIT_AT:
                        for k in [[0, 1], [2], [3], []][e]:
                            split_weights(SPLIT_AT[POS[n, h]], k)

            def normalise(i, h, dst):
                act.wait_ge(nmr_ready, 2 * (i - 1) + h + 1)
                for j in range(HB // 2, HB):
                    b = HB * h + j
                    src = tok[:, b, :] if i == 3 else ps[0:T, 4 + j, :]
                    act.activation(dst[:, j, :], src, ACT.Identity, bias=nmr[:, b:b + 1],
                                   scale=rstd[:, b:b + 1]).then_inc(tok_ready, 1)

            def norm_features(i, h):
                for k in range(KC):
                    act.wait_ge(to_feat, 8 * i + KC * h + (KC if i == 2 else k + 1))
                    src = ps[:, k if (i, h) == (0, 0) else 4 + k, 0:HALF]
                    if i in (0, 3):
                        act.activation(half(XH, h, k), src, ACT.Copy).then_inc(x_high, 1)
                        continue
                    gc, bc = (C_G1, C_E1) if i == 1 else (C_G2, C_E2)
                    gain, shift = cst[:, gc + k:gc + k + 1], cst[:, bc + k:bc + k + 1]
                    if k % 2:
                        act.wait_ge(x_affine, 4 * (i - 1) + 2 * h + k // 2 + 1)
                        act.activation(half(XH, h, k), half(XT, h, k), ACT.Copy).then_inc(x_high, 1)
                        continue
                    act.activation(half(XT, h, k), src, ACT.Identity, bias=shift, scale=gain)
                    act.activation(half(XH, h, k), src, ACT.Identity, bias=shift,
                                   scale=gain).then_inc(x_high, 1)

            def self_exp(h):
                act.wait_ge(s_max, h + 1)
                for j in range(HB):
                    b = HB * h + j
                    ex = act.activation(sprob[h][:, j, :], ps[0:T, 4 + h, j * T:(j + 1) * T], ACT.Exp,
                                        bias=snb[:, b:b + 1], scale=SCALE, accum_out=ssum[:, b:b + 1])
                ex.then_inc(s_exp, 1)

            def self_probT(h):
                act.wait_ge(s_probT, h + 1)
                act.activation(sprobT[h][:, :, :].rearrange("p a b -> p (a b)"), ps[0:T, 6 + h, 0:HALF],
                               ACT.Copy).then_inc(s_probT_sb, 1)

            def self_attended(h):
                for k in range(KC):
                    act.wait_ge(s_att, KC * h + k + 1)
                    act.activation(half(QH, h, k), ps[:, k, 0:HALF], ACT.Copy).then_inc(s_att_high, 1)

            def key_bias_rows(h):
                act.wait_ge(c_row, h + 1)
                act.activation(crow[:, h * HALF:(h + 1) * HALF], ps[0:2, 6 + h, 0:HALF], ACT.Identity,
                               bias=qk2[:, :]).then_inc(c_row_sb, 1)

            def cross_exp(b):
                act.wait_ge(c_max, b + 1)
                if b >= 2:
                    act.wait_ge(c_probT, b - 1)
                act.activation(prob[b % 2][:, 0:M].rearrange("p (i m) -> p i m", i=2), ps[0:T, 4:6, 0:MH],
                               ACT.Exp, bias=snb[:, b:b + 1], scale=SCALE,
                               accum_out=ssum[:, b:b + 1]).then_inc(c_exp, 1)

            def cross_probT(b):
                act.wait_ge(c_probT, b + 1)
                if b >= 2:
                    act.wait_ge(c_chunk, MC * (b - 1))
                act.activation(ptH[b % 2][:, :].rearrange("p (i m) -> p i m", i=2), ps[:, 6:8, 0:3 * T],
                               ACT.Copy).then_inc(c_probT_high, 1)

            def cross_attended(b):
                act.wait_ge(c_chunk, MC * (b + 1))
                act.wait_ge(c_rec, b + 1)
                if b >= 2:
                    act.wait_ge(c_attT, b - 1)
                act.activation(utok[:, b % 2, :], ps[0:T, 2, :], ACT.Copy,
                               scale=srec[:, b:b + 1]).then_inc(c_att_sb, 1)

            def cross_attendedT(b):
                act.wait_ge(c_attT, b + 1)
                act.activation(tokens(AH, b), ps[:, 3, 0:KC * T].rearrange("p (k t) -> p k t", k=KC),
                               ACT.Copy).then_inc(c_attT_high, 1)

            tiles = [tok[:, 0:HB, :], tok[:, HB:B, :]]
            tiles2 = [tok2[:, 0:HB, :], tok2[:, HB:B, :]]

            def split_vo(k):
                act.wait_ge(vo_loaded[k], 32)
                act.activation(VH[:, k, :], VR[:, k, :], ACT.Copy).then_inc(v_high, 1)
                act.activation(OH[:, k, :], OR[:, k, :], ACT.Copy).then_inc(o_high, 1)

            split_vo(0)
            split_vo(1)
            act.wait_ge(consts_loaded, 16)
            act.activation(wgS[:, :, 0:NE], cst[:, C_WG:C_ALL].rearrange("p (k e) -> p k e", k=KC),
                           ACT.Copy).then_inc(small_high, 1)
            split_vo(2)
            split_vo(3)
            for k in range(KC):
                split_weights(U_Q, k)
            norm_features(0, 0)
            for e in range(KC):
                act.wait_ge(vo_made, e + 1)
                act.activation(WH[SLOT[U_VO]][:, e, :], ps[:, 4 + e, :], ACT.Copy).then_inc(vo_high, 1)
            unit(U_Q, 0)
            norm_features(0, 1)
            unit(U_K, 0)
            split_ct(0, 0)
            unit(U_Q, 1)
            self_exp(0)
            split_ct(0, 1)
            unit(U_K, 1)
            self_probT(0)
            self_exp(1)
            self_attended(0)
            unit(U_VO, 0, [0, 1, 2])
            self_probT(1)
            unit(U_VO, 0, [3])
            self_attended(1)
            normalise(1, 0, tiles[0])
            norm_features(1, 0)
            act.wait_ge(gv_ready, 1)
            act.activation(keyS[:, :, 0], gv[:, KC:2 * KC], ACT.Copy).then_inc(key_high, 1)
            split_cn(0, 0)
            split_cn(0, 1)
            normalise(1, 1, tiles[1])
            split_cn(0, 2)
            act.wait_ge(qk_made, KC)
            for e in range(KC):
                act.activation(WH[SLOT[U_A]][:, e, :], ps[:, e, :], ACT.Copy).then_inc(qk_high, 1)
            norm_features(1, 1)
            unit(U_A, 0)
            act.wait_ge(gv_ready, 2)
            unit(U_A, 1, [0])
            key_bias_rows(0)
            key_bias_rows(1)
            split_ct(1, 0)
            unit(U_A, 1, [1])
            split_ct(1, 1)
            cross_exp(0)
            unit(U_A, 1, [2, 3])
            cross_probT(0)
            split_ct(2, 0)
            cross_exp(1)
            split_ct(2, 1)
            for b in range(B):
                if b + 1 < B:
                    split_cn(b + 1, 0)
                    split_cn(b + 1, 1)
                cross_attended(b)
                if b + 1 < B:
                    cross_probT(b + 1)
                    split_cn(b + 1, 2)
                if b + 3 < B:
                    split_ct(b + 3, 0)
                    split_ct(b + 3, 1)
                if b + 2 >= B:
                    unit(U_CV, 0, [[0, 1], [2, 3]][b + 2 - B])
                if b + 2 < B:
                    cross_exp(b + 2)
                cross_attendedT(b)
                if b == B - 2:
                    for k in range(KC):
                        split_weights(U_F, k)
            normalise(2, 0, xn[0])
            norm_features(2, 0)
            unit(U_F, 0)
            normalise(2, 1, xn[1])
            norm_features(2, 1)
            unit(U_F + 1, 0)
            for n, h in ORDER[POS[U_F, 1]:POS[U_M - 1, 1]]:
                unit(n, h)
            normalise(3, 0, tiles2[0])
            unit(U_M - 1, 1, [0, 1])
            norm_features(3, 0)
            unit(U_M - 1, 1, [2, 3])
            unit(U_M, 0)
            unit(U_M + 1, 0)
            normalise(3, 1, tiles2[1])
            unit(U_M + 2, 0, [0, 1])
            norm_features(3, 1)
            unit(U_M + 2, 0, [2, 3])
            unit(U_M, 1)
            for h in range(2):
                act.wait_ge(g_rows, h + 1)
                act.activation(glog[:, h * HALF:(h + 1) * HALF], ps[0:2 * NE, 4 + h, 0:HALF],
                               ACT.Copy).then_inc(g_rows_sb, 1)
            unit(U_M + 1, 1)
            unit(U_M + 2, 1)
            act.wait_ge(g_shift, 2)
            act.activation(gexp[:, :, :], gexp[:, :, :], ACT.Exp)
            act.activation(gsm[:, 0, :], gsm[:, 0, :], ACT.Exp).then_inc(g_exp, 1)
            for n, h in ORDER[POS[U_M + 3, 0]:]:
                unit(n, h)

        @block.vector
        def _(dve):
            steps = [0]

            def settle(ins):
                steps[0] += 1
                ins.then_inc(dve_step, 1)
                dve.wait_ge(dve_step, steps[0])

            def split_weights(n, k):
                dve.wait_ge(w_high, KC * LOADED.index(n) + k + 1)
                dve.tensor_tensor(WL[SLOT[n]][:, k, :], WR[:, k, :], raw(WH[SLOT[n]][:, k, :]),
                                  ALU.subtract).then_inc(w_low, 1)

            def split_ct(b, i):
                dve.wait_ge(ct_high, 2 * b + i + 1)
                dve.tensor_tensor(ctL[b % 2][:, 2 * i:2 * i + 2, 0:M], ctR[:, 2 * i:2 * i + 2, :],
                                  raw(ctH[b % 2][:, 2 * i:2 * i + 2, 0:M]), ALU.subtract).then_inc(ct_low, 1)

            def split_cn(b, i):
                dve.wait_ge(cn_high, 3 * b + i + 1)
                dve.tensor_tensor(cnL[:, 2 * i:2 * i + 2, :], cnR[:, 2 * i:2 * i + 2, :],
                                  raw(cnH[:, 2 * i:2 * i + 2, :]), ALU.subtract).then_inc(cn_low, 1)

            def unit(n, h, groups=range(KC)):
                for e in groups:
                    src = ps[:, bank(n, h, e), 0:HALF]
                    kind = KINDS[n]
                    if act_writes(n) and dve_writes(n):
                        dve.wait_ge(act_evac, act_count(n, h, e))
                    elif dve_writes(n):
                        dve.wait_ge(gemm_done, gemm_count(n, h, e))
                    if kind == "split":
                        dve.scalar_tensor_tensor(out=half(AL, h, e), in0=src, scalar=gv[:, e:e + 1],
                                                 in1=raw(half(AH, h, e)), op0=ALU.add,
                                                 op1=ALU.subtract).then_inc(dve_evac, 1)
                    elif kind == "relu_bias":
                        dve.tensor_tensor(half(AL, h, e), half(AT, h, e), raw(half(AH, h, e)),
                                          ALU.subtract).then_inc(dve_evac, 1)
                    elif kind == "relu":
                        dve.scalar_tensor_tensor(out=half(AL, h, e), in0=src, scalar=0.0, in1=raw(half(AH, h, e)),
                                                 op0=ALU.max, op1=ALU.subtract).then_inc(dve_evac, 1)
                    elif kind in ("residual", "down_residual"):
                        col = C_CBV if n == U_CV else C_B2
                        bias = vob[:, e:e + 1] if n == U_VO else cst[:, col + e:col + e + 1]
                        dst = XS if kind == "residual" else acc
                        settle(dve.scalar_tensor_tensor(out=half(dst, h, e), in0=src,
                                                        scalar=bias,
                                                        in1=raw(half(XH, h, e)), op0=ALU.add, op1=ALU.add))
                        dve.tensor_tensor(half(dst, h, e), half(dst, h, e), raw(half(XL, h, e)),
                                          ALU.add).then_inc(dve_evac, 1)
                    elif kind == "down_first":
                        dve.tensor_copy(half(acc, h, e), src).then_inc(dve_evac, 1)
                    elif kind == "down_add":
                        dve.wait_ge(dve_evac, dve_count(n - 2, h, e))
                        dve.tensor_tensor(half(acc, h, e), src, half(acc, h, e), ALU.add).then_inc(dve_evac, 1)
                    if POS[n, h] in SPLIT_AT and SPLIT_AT[POS[n, h]] not in POOL_UNITS:
                        for k in [[0, 1], [2], [3], []][e]:
                            split_weights(SPLIT_AT[POS[n, h]], k)

            def bias_product(u, w, col, n, ready, chunks=range(KC)):
                for k in chunks:
                    if n is not None:
                        dve.wait_ge(w_high, KC * LOADED.index(n) + k + 1)
                    b = cst[:, col + k:col + k + 1]
                    if k == 0:
                        ins = dve.tensor_scalar(u[:, :], w[:, 0, :], b, None, ALU.mult)
                    else:
                        ins = dve.scalar_tensor_tensor(out=u[:, :], in0=w[:, k, :], scalar=b, in1=u[:, :],
                                                       op0=ALU.mult, op1=ALU.add)
                    if k < KC - 1:
                        settle(ins)
                    else:
                        ins.then_inc(ready, 1)

            def statistics(h, before, js=range(HB)):
                for j in js:
                    b = HB * h + j
                    if before is None:
                        if j % 2 == 0:
                            dve.wait_ge(x_loaded[b // 2], 16)
                        st = dve.bn_stats(bnst[:, b, :], tok[:, b, :])
                    else:
                        dve.wait_ge(to_tok, before + j + 1)
                        st = dve.bn_stats(bnst[:, b, :], ps[0:T, 4 + j, :])
                if js[-1] < HB - 1:
                    return
                settle(st)
                for j in range(HB):
                    ag = dve.bn_aggr(mv[:, HB * h + j, :], bnst[:, HB * h + j, :])
                ag.then_inc(stats_ready, 1)

            def normalise(i, h, dst):
                dve.wait_ge(rstd_ready, {0: h, 1: 2 + h, 2: 4 + h, 3: 7 + 2 * h}[i] + 1)
                if i:
                    cols = slice(HB * h, HB * (h + 1))
                    dve.scalar_tensor_tensor(out=nmr[:, cols], in0=mv[:, cols, 0], scalar=-1.0, in1=rstd[:, cols],
                                             op0=ALU.mult, op1=ALU.mult).then_inc(nmr_ready, 1)
                for j in range(HB // 2 if i else HB):
                    b = HB * h + j
                    src = tok[:, b, :] if i in (0, 3) else ps[0:T, 4 + j, :]
                    dve.tensor_scalar(dst[:, j, :], src, mv[:, b, 0:1], rstd[:, b:b + 1], ALU.subtract,
                                      ALU.mult).then_inc(tok_ready, 1)

            def affine_features(i, h, chunks=(1, 3)):
                gc, bc = (C_G1, C_E1) if i == 1 else (C_G2, C_E2)
                for k in chunks:
                    dve.wait_ge(to_feat, 8 * i + KC * h + (KC if i == 2 else k + 1))
                    dve.tensor_scalar(half(XT, h, k), ps[:, 4 + k, 0:HALF], cst[:, gc + k:gc + k + 1],
                                      cst[:, bc + k:bc + k + 1], ALU.mult, ALU.add).then_inc(x_affine, 1)

            def norm_features(i, h, chunks=range(KC)):
                for k in chunks:
                    dve.wait_ge(x_high, 8 * i + KC * h + k + 1)
                    src = (half(XT, h, k) if i in (1, 2) else
                           ps[:, k if (i, h) == (0, 0) else 4 + k, 0:HALF])
                    dve.tensor_tensor(half(XL, h, k), src, raw(half(XH, h, k)), ALU.subtract).then_inc(x_ready, 1)

            def self_max(h):
                dve.wait_ge(s_scores, h + 1)
                settle(dve.tensor_reduce(smx[:, HB * h:HB * (h + 1)],
                                         ps[0:T, 4 + h, 0:HALF].rearrange("p (j s) -> p j s", j=HB), AX.X, ALU.max))
                dve.tensor_scalar(snb[:, HB * h:HB * (h + 1)], smx[:, HB * h:HB * (h + 1)], -SCALE, None,
                                  ALU.mult).then_inc(s_max, 1)

            def self_normalise(h):
                dve.wait_ge(s_exp, h + 1)
                settle(dve.reciprocal(srec[:, HB * h:HB * (h + 1)], ssum[:, HB * h:HB * (h + 1)]))
                for j in range(HB):
                    b = HB * h + j
                    nm = dve.tensor_scalar(sprob[h][:, j, :], sprob[h][:, j, :], srec[:, b:b + 1], None, ALU.mult)
                nm.then_inc(s_norm, 1)

            def self_attended(h):
                for k in range(KC):
                    dve.wait_ge(s_att_high, KC * h + k + 1)
                    dve.tensor_tensor(half(QL, h, k), ps[:, k, 0:HALF], raw(half(QH, h, k)),
                                      ALU.subtract).then_inc(s_att_low, 1)

            def cross_max(b):
                dve.wait_ge(c_scores, b + 1)
                settle(dve.tensor_reduce(smx[:, b:b + 1], ps[0:T, 4:6, 0:MH], AX.XY, ALU.max))
                settle(dve.tensor_scalar(smx[:, b:b + 1], smx[:, b:b + 1], cshift[:, b:b + 1], -SCALE, ALU.add,
                                         ALU.mult))
                dve.scalar_tensor_tensor(out=snb[:, b:b + 1], in0=cshift[:, b:b + 1], scalar=SCALE,
                                         in1=smx[:, b:b + 1], op0=ALU.mult, op1=ALU.add).then_inc(c_max, 1)

            def cross_probT(b):
                dve.wait_ge(c_probT_high, b + 1)
                dve.tensor_tensor(ptL[b % 2][:, :].rearrange("p (i m) -> p i m", i=2), ps[:, 6:8, 0:3 * T],
                                  raw(ptH[b % 2][:, :].rearrange("p (i m) -> p i m", i=2)),
                                  ALU.subtract).then_inc(c_probT_low, 1)

            def cross_recip(b):
                dve.wait_ge(c_exp, b + 1)
                dve.reciprocal(srec[:, b:b + 1], ssum[:, b:b + 1]).then_inc(c_rec, 1)

            def cross_attendedT(b):
                dve.wait_ge(c_attT_high, b + 1)
                dve.tensor_tensor(tokens(AL, b), ps[:, 3, 0:KC * T].rearrange("p (k t) -> p k t", k=KC),
                                  raw(tokens(AH, b)), ALU.subtract).then_inc(c_attT_low, 1)

            def last_scale(h, js):
                dve.wait_ge(stats_ready, 7 + 2 * h)
                dve.wait_ge(gb_loaded, 32)
                for j in js:
                    b = HB * h + j
                    z = dve.scalar_tensor_tensor(out=tok2[:, b, :], in0=ps[0:T, 4 + j, :], scalar=mv[:, b, 0:1],
                                                 in1=g3b[0:T, :], op0=ALU.subtract, op1=ALU.mult)
                settle(z)

            def last_residual(h, js):
                dve.wait_ge(rstd_ready, 6 + 2 * h + 1)
                dve.wait_ge(xres_ready, HB * (h + 1))
                for j in js:
                    b = HB * h + j
                    z = dve.scalar_tensor_tensor(out=tok[:, b, :], in0=tok2[:, b, :], scalar=rstd[:, b:b + 1],
                                                 in1=tok[:, b, :], op0=ALU.mult, op1=ALU.add)
                settle(z)

            def last_norm(h, first, second, third):
                unit(*first, [0])
                statistics(h, 16 + HB * h)
                unit(*first, [1])
                last_scale(h, [0, 1])
                unit(*first, [2])
                last_scale(h, [2, 3])
                unit(*first, [3])
                last_residual(h, [0, 1])
                unit(*second, [0])
                last_residual(h, [2, 3])
                unit(*second, [1])
                statistics(h, None, [0, 1])
                unit(*second, [2])
                statistics(h, None, [2, 3])
                unit(*second, [3])
                normalise(3, h, tiles2[h])
                unit(*third, [0, 1])
                norm_features(3, h)
                unit(*third, [2, 3])

            def gate_top():
                dve.wait_ge(g_cols, 1)
                settle(dve.tensor_copy(gl[:, :, :], ps[0:T, 6, 0:B * NE].rearrange("p (b e) -> p b e", b=B)))
                for b in range(B):
                    tp = dve.max(gtop[:, b, :], gl[:, b, :])
                settle(tp)
                dve.tensor_tensor(gexp[:, :, :], gl[:, :, :], gtop[:, :, 0:1].to_broadcast([T, B, NE]),
                                  ALU.subtract).then_inc(g_shift, 1)
                dve.tensor_tensor(gsm[:, 0, :], gtop[:, :, 1], gtop[:, :, 0], ALU.subtract).then_inc(g_shift, 1)

            def gate_weights():
                dve.wait_ge(g_exp, 1)
                settle(dve.tensor_reduce(gsm[:, 1, :], gexp[:, :, :], AX.X, ALU.add))
                settle(dve.reciprocal(gsm[:, 2, :], gsm[:, 1, :]))
                settle(dve.tensor_tensor(gsm[:, 3, :], gsm[:, 0, :], gsm[:, 2, :], ALU.mult))
                settle(dve.tensor_tensor(gsm[:, 4, :], gsm[:, 2, :], gsm[:, 3, :], ALU.add))
                settle(dve.tensor_scalar(gsm[:, 4, :], gsm[:, 4, :], F32_EPS, None, ALU.max))
                settle(dve.reciprocal(gsm[:, 5, :], gsm[:, 4, :]))
                settle(dve.tensor_tensor(gsm[:, 2, :], gsm[:, 2, :], gsm[:, 5, :], ALU.mult))
                settle(dve.tensor_tensor(gsm[:, 3, :], gsm[:, 3, :], gsm[:, 5, :], ALU.mult))
                dve.tensor_tensor(gsm[:, 6, :], gsm[:, 2, :], gsm[:, 3, :], ALU.add).then_inc(g_weight, 1)

            def finish(h, chunks, before):
                dve.wait_ge(g_weight, 1)
                cols = slice(chunks[0] * P, (chunks[-1] + 1) * P)
                for j in range(HB):
                    b = HB * h + j
                    dve.wait_ge(to_tok, before + j + 1)
                    dve.scalar_tensor_tensor(out=outb[:, b, cols], in0=ps[0:T, 4 + j, cols],
                                             scalar=gsm[:, 6, b:b + 1], in1=tok[:, b, cols], op0=ALU.mult,
                                             op1=ALU.add).then_inc(out_ready, 1)

            tiles = [tok[:, 0:HB, :], tok[:, HB:B, :]]
            tiles2 = [tok2[:, 0:HB, :], tok2[:, HB:B, :]]

            def split_v(k):
                dve.wait_ge(v_high, k + 1)
                dve.tensor_tensor(VL[:, k, :], VR[:, k, :], raw(VH[:, k, :]), ALU.subtract).then_inc(v_low, 1)

            for k in range(2):
                split_v(k)
                dve.wait_ge(o_high, k + 1)
                dve.tensor_tensor(OL[:, k, :], OR[:, k, :], raw(OH[:, k, :]), ALU.subtract).then_inc(o_low, 1)
            statistics(0, None)
            split_v(2)
            split_v(3)
            normalise(0, 0, tiles[0])
            norm_features(0, 0)
            for e in range(KC):
                dve.wait_ge(vo_high, e + 1)
                dve.tensor_tensor(WL[SLOT[U_VO]][:, e, :], ps[:, 4 + e, :], raw(WH[SLOT[U_VO]][:, e, :]),
                                  ALU.subtract).then_inc(vo_low, 1)
            statistics(1, None)
            normalise(0, 1, tiles[1])
            unit(U_Q, 0)
            norm_features(0, 1)
            dve.wait_ge(small_high, 1)
            dve.tensor_tensor(wgS[:, :, NE:2 * NE], cst[:, C_WG:C_ALL].rearrange("p (k e) -> p k e", k=KC),
                              raw(wgS[:, :, 0:NE]), ALU.subtract).then_inc(small_low, 1)
            unit(U_K, 0)
            split_ct(0, 0)
            unit(U_Q, 1)
            bias_product(u_o, OR, C_BV, None, u_o_ready)
            settle(dve.tensor_tensor(qk[:, :], cst[:, C_CBQ:C_CBQ + KC], cst[:, C_CBK:C_CBK + KC], ALU.mult))
            dve.tensor_reduce(qks[:, 0:1], qk[:, :], AX.X, ALU.add).then_inc(qks_ready, 1)
            self_max(0)
            self_normalise(0)
            split_ct(0, 1)
            bias_product(u_q, WR, C_CBK, S_CQ, u_q_ready)
            dve.wait_ge(vo_bias, 1)
            dve.tensor_tensor(vob[:, :], ps[:, 7, 0:KC], cst[:, C_BO:C_BO + KC], ALU.add).then_inc(vob_ready, 1)
            self_max(1)
            self_attended(0)
            self_normalise(1)
            dve.wait_ge(vob_ready, 1)
            unit(U_VO, 0, [0, 1])
            bias_product(u_k, WR, C_CBQ, S_CK, u_k_ready, [0])
            unit(U_VO, 0, [2])
            bias_product(u_k, WR, C_CBQ, S_CK, u_k_ready, [1])
            unit(U_VO, 0, [3])
            bias_product(u_k, WR, C_CBQ, S_CK, u_k_ready, [2, 3])
            self_attended(1)
            statistics(0, 0)
            unit(U_VO, 1, [0])
            normalise(1, 0, tiles[0])
            unit(U_VO, 1, [1, 2])
            affine_features(1, 0, [1])
            norm_features(1, 0, [0, 1])
            unit(U_VO, 1, [3])
            dve.wait_ge(gv_made, 1)
            dve.tensor_copy(gv[:, :], ps[:, 7, HALF:HALF + 2 * KC]).then_inc(gv_ready, 1)
            dve.tensor_copy(qk2[:, :], ps[0:2, 7, HALF + 2 * KC:HALF + 2 * KC + 1]).then_inc(gv_ready, 1)
            affine_features(1, 0, [3])
            norm_features(1, 0, [2, 3])
            dve.wait_ge(key_high, 1)
            dve.tensor_tensor(keyS[:, :, 1], gv[:, KC:2 * KC], raw(keyS[:, :, 0]), ALU.subtract).then_inc(key_low, 1)
            statistics(1, HB)
            split_cn(0, 0)
            normalise(1, 1, tiles[1])
            split_cn(0, 1)
            split_cn(0, 2)
            for e in range(KC):
                dve.wait_ge(qk_high, e + 1)
                dve.tensor_tensor(WL[SLOT[U_A]][:, e, :], ps[:, e, :], raw(WH[SLOT[U_A]][:, e, :]),
                                  ALU.subtract).then_inc(qk_low, 1)
            affine_features(1, 1)
            norm_features(1, 1)
            unit(U_A, 0)
            unit(U_A, 1, [0])
            split_ct(1, 0)
            unit(U_A, 1, [1])
            dve.wait_ge(c_col, 1)
            dve.tensor_copy(cshift[:, :], ps[0:T, 6, 0:B]).then_inc(c_col_sb, 1)
            dve.wait_ge(c_col_sb, 1)
            cross_max(0)
            split_ct(1, 1)
            unit(U_A, 1, [2, 3])
            cross_recip(0)
            cross_probT(0)
            split_ct(2, 0)
            cross_max(1)
            split_ct(2, 1)
            for b in range(B):
                if b + 1 < B:
                    split_cn(b + 1, 0)
                    split_cn(b + 1, 1)
                    cross_recip(b + 1)
                    cross_probT(b + 1)
                if b + 2 < B:
                    cross_max(b + 2)
                if b + 3 < B:
                    split_ct(b + 3, 0)
                if b + 2 >= B:
                    unit(U_CV, 0, [[0, 1], [2, 3]][b + 2 - B])
                if b + 3 < B:
                    split_ct(b + 3, 1)
                cross_attendedT(b)
            statistics(0, 8)
            unit(U_CV, 1, [0])
            normalise(2, 0, xn[0])
            unit(U_CV, 1, [1, 2])
            affine_features(2, 0)
            norm_features(2, 0, [0, 1])
            unit(U_CV, 1, [3])
            norm_features(2, 0, [2, 3])
            unit(U_F, 0, [0])
            statistics(1, 8 + HB)
            unit(U_F, 0, [1])
            normalise(2, 1, xn[1])
            unit(U_F, 0, [2, 3])
            unit(U_F + 1, 0, [0])
            affine_features(2, 1)
            unit(U_F + 1, 0, [1])
            norm_features(2, 1, [0, 1, 2])
            unit(U_F + 1, 0, [2])
            norm_features(2, 1, [3])
            unit(U_F + 1, 0, [3])
            for n, h in ORDER[POS[U_F, 1]:POS[U_M - 3, 1]]:
                unit(n, h)
            last_norm(0, (U_M - 3, 1), (U_M - 2, 1), (U_M - 1, 1))
            last_norm(1, (U_M, 0), (U_M + 1, 0), (U_M + 2, 0))
            unit(U_M, 1)
            unit(U_M + 1, 1)
            gate_top()
            unit(U_M + 2, 1)
            gate_weights()
            for n, h in ORDER[POS[U_M + 3, 0]:POS[NU - 1, 1]]:
                unit(n, h)
            unit(NU - 1, 1, [0])
            finish(0, range(KC), 24)
            unit(NU - 1, 1, [1, 2])
            finish(1, range(KC - 1), 24 + HB)
            unit(NU - 1, 1, [3])
            finish(1, [KC - 1], 24 + 2 * HB)


def _chunks(np, v):
    return np.asarray(v).reshape(-1, P).T


def kernel(**inputs):
    import numpy as np
    import concourse.bacc as bacc
    from concourse import mybir as mb
    from concourse.bass_utils import run_bass_kernel_spmd as run

    a = {k: np.asarray(v) for k, v in inputs.items()}
    x, mem = a["x"], a["ctx_1024"]
    ipw, ipb = a["L0_xattn_in_proj_w"], a["L0_xattn_in_proj_b"]

    def block(w):
        return w.reshape(KC, P, D).transpose(1, 0, 2)

    wvo = np.ascontiguousarray(np.stack([block(ipw[2 * D:3 * D]), block(a["L0_xattn_out_proj_w"].T)]))
    units = [ipw[0:D].T, ipw[D:2 * D].T, a["L0_xattn_wq"], a["L0_xattn_wk"], a["L0_xattn_wv"].T]
    for up, down in ((a["L0_xattn_w1"].T, a["L0_xattn_w2"].T), (a["L0_ffn_w1"], a["L0_ffn_w2"])):
        for j in range(NF):
            units += [up[:, j * D:(j + 1) * D], down[j * D:(j + 1) * D, :]]
    wts = np.ascontiguousarray(np.stack([block(u) for u in units]))
    vectors = [ipb[0:D], ipb[D:2 * D], ipb[2 * D:3 * D], a["L0_xattn_out_proj_b"], a["L0_xattn_bq"],
               a["L0_xattn_bk"], a["L0_xattn_bv"], a["L0_xattn_b1"], a["L0_xattn_b2"], a["L0_xattn_g1"],
               a["L0_xattn_be1"], a["L0_xattn_g2"], a["L0_xattn_be2"]]
    gate = a["L0_ffn_Wg"].reshape(KC, P, NE).transpose(1, 0, 2).reshape(P, KC * NE)
    consts = np.ascontiguousarray(np.concatenate([_chunks(np, v) for v in vectors] + [gate], axis=1))
    arrays = {
        "x_in": np.ascontiguousarray(x),
        "ctxt_in": np.ascontiguousarray(mem.transpose(0, 2, 1)),
        "ctxn_in": np.ascontiguousarray(mem),
        "wvo_in": wvo,
        "wts_in": wts,
        "consts_in": consts,
        "g3_in": np.ascontiguousarray(a["L0_xattn_g3"]),
        "be3_in": np.ascontiguousarray(a["L0_xattn_be3"]),
    }
    nc = bacc.Bacc("TRN2", target_bir_lowering=False, num_devices=1)
    args = [nc.dram_tensor(n, v.shape, mb.dt.from_np(v.dtype), kind="ExternalInput").ap() for n, v in arrays.items()]
    args.append(nc.dram_tensor("out", (B, T, D), F32, kind="ExternalOutput").ap())
    build(nc, *args)
    r = run(nc, [arrays], core_ids=[0])
    return r.results[0]["out"]
```
